# Optimizing a Trainium2 kernel written in Bass

```python
import numpy as np
import jax
import jax.numpy as jnp

def _softmax(x, axis=-1):
    return jax.nn.softmax(x, axis=axis)

def _gelu(x):
    return jax.nn.gelu(x, approximate=True)

def _silu(x):
    return jax.nn.silu(x)

def _sigmoid(x):
    return jax.nn.sigmoid(x)

def _layernorm(x, axis=-1, eps=1e-05):
    m = jnp.mean(x, axis=axis, keepdims=True)
    v = jnp.var(x, axis=axis, keepdims=True)
    return (x - m) / jnp.sqrt(v + eps)

def _scatter_add(tgt, idx, src, axis=0):
    return tgt.at[idx].add(src)

def _segment_sum(src, seg, n):
    return jax.ops.segment_sum(src, seg, n)
kernel_name = 'mk_seq_postln_d2_jaxref_r8_a6da7d'

def setup_inputs(seed: int=0):
    np.random.seed(seed)
    _w = jnp.asarray

    def _L0_attn_setup():
        import jax, jax.numpy as jnp
        import numpy as np
        DIM = 128
        B, S = (8, 256)
        LN_EPS = 1e-05
        key = jax.random.key(seed)
        k1, k2, k3 = jax.random.split(key, 3)
        x = jax.random.normal(k1, (B, S, DIM), dtype=jnp.float32)
        w_qkv = jax.random.normal(k2, (3 * DIM, DIM), dtype=jnp.float32) * np.sqrt(2.0 / (DIM + 3 * DIM))
        w_fc = jax.random.normal(k3, (DIM, DIM), dtype=jnp.float32) * np.sqrt(2.0 / (DIM + DIM))
        b_fc = jnp.zeros((DIM,), dtype=jnp.float32)
        gamma = jnp.ones((DIM,), dtype=jnp.float32)
        beta = jnp.zeros((DIM,), dtype=jnp.float32)
        return {'x': x, 'w_qkv': w_qkv, 'w_fc': w_fc, 'b_fc': b_fc, 'gamma': gamma, 'beta': beta}
    _L0_attn_in = _L0_attn_setup()

    def _L0_ffn_setup():
        import jax, jax.numpy as jnp
        import numpy as np
        EMB = 128
        HID = 256
        HEADS = 16
        HEAD_DIM = EMB // HEADS
        EXPERTS = 8
        TOPK = 2
        EPS = 1e-05

        def layernorm(x, scale, shift):
            mean = jnp.mean(x, axis=-1, keepdims=True)
            var = jnp.mean((x - mean) ** 2, axis=-1, keepdims=True)
            return scale * (x - mean) / jnp.sqrt(var + EPS) + shift

        def attention(x, wq, wk, wv, wo, bo):
            b, t, _ = x.shape
            q = (x @ wq).reshape(b, t, HEADS, HEAD_DIM)
            k = (x @ wk).reshape(b, t, HEADS, HEAD_DIM)
            v = (x @ wv).reshape(b, t, HEADS, HEAD_DIM)
            scores = jnp.einsum('bqhd,bkhd->bhqk', q, k)
            mask = jnp.arange(t)[:, None] < jnp.arange(t)[None, :]
            scores = jnp.where(mask, -jnp.inf, scores)
            attn = jax.nn.softmax(scores / np.sqrt(HEAD_DIM), axis=-1)
            ctx = jnp.einsum('bhqk,bkhd->bqhd', attn, v).reshape(b, t, EMB)
            return ctx @ wo + bo

        def moe_ff(x, gate_w, w1, w2, w3):
            b, t, d = x.shape
            xf = x.reshape(b * t, d)
            scores = xf @ gate_w
            topk_scores, topk_idx = jax.lax.top_k(scores, TOPK)
            topk_probs = jax.nn.softmax(topk_scores, axis=-1)
            weight = jnp.sum(jax.nn.one_hot(topk_idx, EXPERTS, dtype=xf.dtype) * topk_probs[..., None], axis=1)
            h = jax.nn.silu(jnp.einsum('td,edh->eth', xf, w1)) * jnp.einsum('td,edh->eth', xf, w2)
            out_e = jnp.einsum('eth,ehd->etd', h, w3)
            out = jnp.einsum('etd,te->td', out_e, weight)
            return out.reshape(b, t, d)
        key = jax.random.key(seed)
        ks = jax.random.split(key, 12)
        s = lambda k, shape, fan: jax.random.normal(k, shape, jnp.float32) / np.sqrt(fan)
        return {'x': jax.random.normal(ks[0], (2, 256, EMB), jnp.float32), 'ln1_scale': jnp.ones((EMB,), jnp.float32), 'ln1_shift': jnp.zeros((EMB,), jnp.float32), 'wq': s(ks[1], (EMB, EMB), EMB), 'wk': s(ks[2], (EMB, EMB), EMB), 'wv': s(ks[3], (EMB, EMB), EMB), 'wo': s(ks[4], (EMB, EMB), EMB), 'bo': jnp.zeros((EMB,), jnp.float32), 'ln2_scale': jnp.ones((EMB,), jnp.float32), 'ln2_shift': jnp.zeros((EMB,), jnp.float32), 'gate_w': s(ks[5], (EMB, EXPERTS), EMB), 'w1': s(ks[6], (EXPERTS, EMB, HID), EMB), 'w2': s(ks[7], (EXPERTS, EMB, HID), EMB), 'w3': s(ks[8], (EXPERTS, HID, EMB), HID)}
    _L0_ffn_in = _L0_ffn_setup()

    def _L1_attn_setup():
        import jax, jax.numpy as jnp
        import numpy as np

        def _sin_rpe(Lq, d_model, dtype):
            inv_freq = 1.0 / 10000.0 ** (jnp.arange(0, d_model, 2, dtype=jnp.float32) / d_model)
            pos = jnp.arange(-(Lq - 1), Lq, dtype=jnp.float32)
            ang = pos[:, None] * inv_freq[None, :]
            emb = jnp.zeros((2 * Lq - 1, d_model), dtype=jnp.float32)
            emb = emb.at[:, 0::2].set(jnp.sin(ang)).at[:, 1::2].set(jnp.cos(ang))
            return emb.astype(dtype)

        def _rel_shift(x):
            B, H, Lq, Lr = x.shape
            xp = jnp.concatenate([jnp.zeros((B, H, Lq, 1), x.dtype), x], axis=-1)
            xp = xp.reshape(B, H, Lr + 1, Lq)
            return xp[:, :, 1:].reshape(B, H, Lq, Lr)[..., Lr - Lq:]
        key = jax.random.key(seed)
        ks = jax.random.split(key, 7)
        B, Lq, D, H = (1, 256, 128, 16)
        d_head = D // H
        s = 0.02
        return {'w': jax.random.normal(ks[0], (B, Lq, D), jnp.float32), 'Wq': jax.random.normal(ks[1], (D, D), jnp.float32) * s, 'Wk': jax.random.normal(ks[2], (D, D), jnp.float32) * s, 'Wv': jax.random.normal(ks[3], (D, D), jnp.float32) * s, 'Wr': jax.random.normal(ks[4], (D, D), jnp.float32) * s, 'u_bias': jax.random.normal(ks[5], (H, d_head), jnp.float32) * 0.02, 'v_bias': jax.random.normal(ks[6], (H, d_head), jnp.float32) * 0.02}
    _L1_attn_in = _L1_attn_setup()

    def _L1_ffn_setup():
        import jax, jax.numpy as jnp
        import numpy as np
        D_MODEL, D_FF, RANK = (128, 512, 32)
        B, S = (4, 512)
        key = jax.random.key(seed)
        ks = jax.random.split(key, 7)
        return {'x': jax.random.normal(ks[0], (B, S, D_MODEL), dtype=jnp.float32), 'U1': jax.random.normal(ks[1], (D_MODEL, RANK), dtype=jnp.float32) * 0.02, 'V1': jax.random.normal(ks[2], (RANK, D_FF), dtype=jnp.float32) * 0.02, 'b1': jnp.zeros((D_FF,), dtype=jnp.float32), 'U2': jax.random.normal(ks[3], (D_FF, RANK), dtype=jnp.float32) * 0.02, 'V2': jax.random.normal(ks[4], (RANK, D_MODEL), dtype=jnp.float32) * 0.02, 'b2': jnp.zeros((D_MODEL,), dtype=jnp.float32)}
    _L1_ffn_in = _L1_ffn_setup()
    _d = {'L0_attn_x': _L0_attn_in['x'], 'L0_attn_w_qkv': _L0_attn_in['w_qkv'], 'L0_attn_w_fc': _L0_attn_in['w_fc'], 'L0_attn_b_fc': _L0_attn_in['b_fc'], 'L0_attn_gamma': _L0_attn_in['gamma'], 'L0_attn_beta': _L0_attn_in['beta'], 'L0_ffn_ln1_scale': _L0_ffn_in['ln1_scale'], 'L0_ffn_ln1_shift': _L0_ffn_in['ln1_shift'], 'L0_ffn_wq': _L0_ffn_in['wq'], 'L0_ffn_wk': _L0_ffn_in['wk'], 'L0_ffn_wv': _L0_ffn_in['wv'], 'L0_ffn_wo': _L0_ffn_in['wo'], 'L0_ffn_bo': _L0_ffn_in['bo'], 'L0_ffn_ln2_scale': _L0_ffn_in['ln2_scale'], 'L0_ffn_ln2_shift': _L0_ffn_in['ln2_shift'], 'L0_ffn_gate_w': _L0_ffn_in['gate_w'], 'L0_ffn_w1': _L0_ffn_in['w1'], 'L0_ffn_w2': _L0_ffn_in['w2'], 'L0_ffn_w3': _L0_ffn_in['w3'], 'L1_attn_Wq': _L1_attn_in['Wq'], 'L1_attn_Wk': _L1_attn_in['Wk'], 'L1_attn_Wv': _L1_attn_in['Wv'], 'L1_attn_Wr': _L1_attn_in['Wr'], 'L1_attn_u_bias': _L1_attn_in['u_bias'], 'L1_attn_v_bias': _L1_attn_in['v_bias'], 'L1_ffn_U1': _L1_ffn_in['U1'], 'L1_ffn_V1': _L1_ffn_in['V1'], 'L1_ffn_b1': _L1_ffn_in['b1'], 'L1_ffn_U2': _L1_ffn_in['U2'], 'L1_ffn_V2': _L1_ffn_in['V2'], 'L1_ffn_b2': _L1_ffn_in['b2']}
    _x0 = _d['L0_attn_x']
    _d['L0_attn_x'] = jax.random.normal(jax.random.fold_in(jax.random.key(seed), 1), (8, 512, 128), dtype=_x0.dtype)
    del _x0
    return _d

def reference(L0_attn_x, L0_attn_w_qkv, L0_attn_w_fc, L0_attn_b_fc, L0_attn_gamma, L0_attn_beta, L0_ffn_ln1_scale, L0_ffn_ln1_shift, L0_ffn_wq, L0_ffn_wk, L0_ffn_wv, L0_ffn_wo, L0_ffn_bo, L0_ffn_ln2_scale, L0_ffn_ln2_shift, L0_ffn_gate_w, L0_ffn_w1, L0_ffn_w2, L0_ffn_w3, L1_attn_Wq, L1_attn_Wk, L1_attn_Wv, L1_attn_Wr, L1_attn_u_bias, L1_attn_v_bias, L1_ffn_U1, L1_ffn_V1, L1_ffn_b1, L1_ffn_U2, L1_ffn_V2, L1_ffn_b2):

    def _L0_attn_ref(x, w_qkv, w_fc, b_fc, gamma, beta):
        import jax, jax.numpy as jnp
        import numpy as np
        DIM = 128
        B, S = (8, 256)
        LN_EPS = 1e-05
        scaling = DIM ** (-0.5)
        qkv = jnp.einsum('bsd,ed->bse', x, w_qkv)
        q, k, v = jnp.split(qkv, 3, axis=-1)
        att = jax.nn.softmax(jnp.einsum('bqd,bkd->bqk', q, k) * scaling, axis=-1)
        y = jnp.einsum('bqk,bvd->bqd', att, v)
        y = jnp.einsum('bqd,ed->bqe', y, w_fc) + b_fc
        h = x + y
        mu = jnp.mean(h, axis=-1, keepdims=True)
        var = jnp.var(h, axis=-1, keepdims=True)
        return (h - mu) * jax.lax.rsqrt(var + LN_EPS) * gamma + beta

    def _L0_ffn_ref(x, ln1_scale, ln1_shift, wq, wk, wv, wo, bo, ln2_scale, ln2_shift, gate_w, w1, w2, w3):
        import jax, jax.numpy as jnp
        import numpy as np
        EMB = 128
        HID = 256
        HEADS = 16
        HEAD_DIM = EMB // HEADS
        EXPERTS = 8
        TOPK = 2
        EPS = 1e-05

        def layernorm(x, scale, shift):
            mean = jnp.mean(x, axis=-1, keepdims=True)
            var = jnp.mean((x - mean) ** 2, axis=-1, keepdims=True)
            return scale * (x - mean) / jnp.sqrt(var + EPS) + shift

        def attention(x, wq, wk, wv, wo, bo):
            b, t, _ = x.shape
            q = (x @ wq).reshape(b, t, HEADS, HEAD_DIM)
            k = (x @ wk).reshape(b, t, HEADS, HEAD_DIM)
            v = (x @ wv).reshape(b, t, HEADS, HEAD_DIM)
            scores = jnp.einsum('bqhd,bkhd->bhqk', q, k)
            mask = jnp.arange(t)[:, None] < jnp.arange(t)[None, :]
            scores = jnp.where(mask, -jnp.inf, scores)
            attn = jax.nn.softmax(scores / np.sqrt(HEAD_DIM), axis=-1)
            ctx = jnp.einsum('bhqk,bkhd->bqhd', attn, v).reshape(b, t, EMB)
            return ctx @ wo + bo

        def moe_ff(x, gate_w, w1, w2, w3):
            b, t, d = x.shape
            xf = x.reshape(b * t, d)
            scores = xf @ gate_w
            topk_scores, topk_idx = jax.lax.top_k(scores, TOPK)
            topk_probs = jax.nn.softmax(topk_scores, axis=-1)
            weight = jnp.sum(jax.nn.one_hot(topk_idx, EXPERTS, dtype=xf.dtype) * topk_probs[..., None], axis=1)
            h = jax.nn.silu(jnp.einsum('td,edh->eth', xf, w1)) * jnp.einsum('td,edh->eth', xf, w2)
            out_e = jnp.einsum('eth,ehd->etd', h, w3)
            out = jnp.einsum('etd,te->td', out_e, weight)
            return out.reshape(b, t, d)
        h = layernorm(x, ln1_scale, ln1_shift)
        x = x + attention(h, wq, wk, wv, wo, bo)
        h = layernorm(x, ln2_scale, ln2_shift)
        x = x + moe_ff(h, gate_w, w1, w2, w3)
        return x

    def _L1_attn_ref(w, Wq, Wk, Wv, Wr, u_bias, v_bias):
        import jax, jax.numpy as jnp
        import numpy as np

        def _sin_rpe(Lq, d_model, dtype):
            inv_freq = 1.0 / 10000.0 ** (jnp.arange(0, d_model, 2, dtype=jnp.float32) / d_model)
            pos = jnp.arange(-(Lq - 1), Lq, dtype=jnp.float32)
            ang = pos[:, None] * inv_freq[None, :]
            emb = jnp.zeros((2 * Lq - 1, d_model), dtype=jnp.float32)
            emb = emb.at[:, 0::2].set(jnp.sin(ang)).at[:, 1::2].set(jnp.cos(ang))
            return emb.astype(dtype)

        def _rel_shift(x):
            B, H, Lq, Lr = x.shape
            xp = jnp.concatenate([jnp.zeros((B, H, Lq, 1), x.dtype), x], axis=-1)
            xp = xp.reshape(B, H, Lr + 1, Lq)
            return xp[:, :, 1:].reshape(B, H, Lq, Lr)[..., Lr - Lq:]
        B, Lq, D = w.shape
        H, d_head = u_bias.shape
        scale = 1.0 / np.sqrt(d_head).astype(np.float32)
        r = _sin_rpe(Lq, D, w.dtype)
        q = (w @ Wq.T).reshape(B, Lq, H, d_head).transpose(0, 2, 1, 3)
        k = (w @ Wk.T).reshape(B, Lq, H, d_head).transpose(0, 2, 1, 3)
        v = (w @ Wv.T).reshape(B, Lq, H, d_head).transpose(0, 2, 1, 3)
        rp = (r @ Wr.T).reshape(2 * Lq - 1, H, d_head).transpose(1, 0, 2)
        AC = jnp.einsum('bhid,bhjd->bhij', q + u_bias[None, :, None, :], k)
        BD = jnp.einsum('bhid,hjd->bhij', q + v_bias[None, :, None, :], rp)
        BD = _rel_shift(BD)
        attn = jax.nn.softmax((AC + BD) * scale, axis=-1)
        out = jnp.einsum('bhij,bhjd->bhid', attn, v)
        return out.transpose(0, 2, 1, 3).reshape(B, Lq, D)

    def _L1_ffn_ref(x, U1, V1, b1, U2, V2, b2):
        import jax, jax.numpy as jnp
        import numpy as np
        D_MODEL, D_FF, RANK = (128, 512, 32)
        B, S = (4, 512)
        P = jnp.einsum('bsd,dr->bsr', x, U1)
        H = jax.nn.gelu(jnp.einsum('bsr,rf->bsf', P, V1) + b1)
        Q = jnp.einsum('bsf,fr->bsr', H, U2)
        return jnp.einsum('bsr,rd->bsd', Q, V2) + b2
    x = L0_attn_x
    x = _layernorm(x + _L0_attn_ref(x, L0_attn_w_qkv, L0_attn_w_fc, L0_attn_b_fc, L0_attn_gamma, L0_attn_beta), axis=-1)
    x = _layernorm(x + _L0_ffn_ref(x, L0_ffn_ln1_scale, L0_ffn_ln1_shift, L0_ffn_wq, L0_ffn_wk, L0_ffn_wv, L0_ffn_wo, L0_ffn_bo, L0_ffn_ln2_scale, L0_ffn_ln2_shift, L0_ffn_gate_w, L0_ffn_w1, L0_ffn_w2, L0_ffn_w3), axis=-1)
    x = _layernorm(x + _L1_attn_ref(x, L1_attn_Wq, L1_attn_Wk, L1_attn_Wv, L1_attn_Wr, L1_attn_u_bias, L1_attn_v_bias), axis=-1)
    x = _layernorm(x + _L1_ffn_ref(x, L1_ffn_U1, L1_ffn_V1, L1_ffn_b1, L1_ffn_U2, L1_ffn_V2, L1_ffn_b2), axis=-1)
    return x

_drawn_inputs = setup_inputs


def setup_inputs(seed=0):
    import zlib

    import numpy as np

    out = dict(_drawn_inputs(seed))
    spreads = {'L0_attn_b_fc': (0.0, 0.652),
     'L0_attn_gamma': (1.0, 0.2),
     'L0_attn_beta': (0.0, 0.1),
     'L0_ffn_ln1_scale': (1.0, 0.2),
     'L0_ffn_ln1_shift': (0.0, 0.1),
     'L0_ffn_bo': (0.0, 0.1),
     'L0_ffn_ln2_scale': (1.0, 0.2),
     'L0_ffn_ln2_shift': (0.0, 0.1),
     'L1_ffn_b1': (0.0, 0.8),
     'L1_ffn_b2': (0.0, 0.319)}
    factors = {'L1_attn_Wq': 8.0,
     'L1_attn_Wk': 8.0,
     'L1_attn_Wr': 8.0,
     'L1_attn_u_bias': 57.753,
     'L1_attn_v_bias': 64.0,
     'L1_ffn_U1': 8.0,
     'L1_ffn_V1': 8.0,
     'L1_ffn_U2': 8.0,
     'L1_ffn_V2': 8.0}
    for name, (base, spread) in spreads.items():
        noise = np.random.default_rng([zlib.crc32(name.encode()), seed]).standard_normal(out[name].shape)
        drawn = base * np.exp(spread * noise) if base else spread * noise
        out[name] = jnp.asarray(drawn.astype(out[name].dtype))
    for name, factor in factors.items():
        out[name] = (out[name] * factor).astype(out[name].dtype)
    return out
```

```python
from contextlib import ExitStack

import concourse.bass as bass
from concourse import mybir

F32 = mybir.dt.float32
BF16 = mybir.dt.bfloat16
U32 = mybir.dt.uint32
ACT = mybir.ActivationFunctionType
ALU = mybir.AluOpType
AX_X = mybir.AxisListType.X

P = 128
NB = 8
L = 512
NT = L // P
H = 16
DH = 8
G = 4
NG = H // G
NI = NB * NG
VW = DH + 1
TERMS_Q = (0, 0, 0, 1, 1, 2)
TERMS_K = (0, 1, 2, 0, 1, 0)
SK = DH * len(TERMS_Q)
NE = 8
HID = 256
FF = 512
RANK = 32
EPS = 1e-5
BIG = -1e30


class Chain:

    def __init__(self, eng, sem, n, per):
        self.eng, self.sem, self.n, self.per, self.k = eng, sem, n, per, 0

    def step(self, ins):
        self.k += 1
        ins.then_inc(self.sem, 1)
        self.eng.wait_ge(self.sem, self.n * self.per + self.k)

    def done(self):
        assert self.k == self.per, (self.k, self.per)


class Semaphores:

    def __init__(self, nc, ctx):
        self.nc, self.all = nc, []
        ctx.callback(self.clear)

    def new(self, name):
        self.all.append(self.nc.alloc_semaphore(name))
        return self.all[-1]

    def clear(self):
        self.nc.clear_and_free_semaphores(self.all)
        self.nc.all_engine_barrier()


def row_on_all(v, width=P):
    return bass.AP(tensor=v.tensor, offset=v.offset, ap=[[0, P], [1, width]])


class Norm:

    def __init__(self, ctx, nc, sems, name):
        self.stats = ctx.enter_context(nc.sbuf_tensor(name + "_stats", [P, NT, 6], F32))
        self.mv = ctx.enter_context(nc.sbuf_tensor(name + "_mv", [P, NT, 2], F32))
        self.rstd = ctx.enter_context(nc.sbuf_tensor(name + "_rstd", [P, NT], F32))
        self.var_eps = ctx.enter_context(nc.sbuf_tensor(name + "_var_eps", [P, NT], F32))
        self.consts = ctx.enter_context(nc.sbuf_tensor(name + "_consts", [P, 2, NT], F32))
        self.consts_set = sems.new(name + "_consts_set")
        self.eps_added = sems.new(name + "_eps_added")
        self.passes = sems.new(name + "_passes")
        self.stats_ready = sems.new(name + "_stats_ready")
        self.var_ready = sems.new(name + "_var_ready")
        self.rstd_ready = sems.new(name + "_rstd_ready")

    def moments(self, dve, x, count):
        for t in range(NT):
            last = dve.bn_stats(self.stats[:, t, :], x[:, t, :])
        last.then_inc(self.stats_ready, 1)
        dve.wait_ge(self.stats_ready, count)
        dve.sem_inc(self.passes, 1)
        for t in range(NT):
            last = dve.bn_aggr(self.mv[:, t, :], self.stats[:, t, :])
        last.then_inc(self.var_ready, 1)

    def root(self, pool, count):
        pool.wait_ge(self.var_ready, count)
        pool.tensor_tensor(self.var_eps[:, :], self.mv[:, :, 1], self.consts[:, 0, :], ALU.add)\
            .then_inc(self.eps_added, 1)
        pool.wait_ge(self.eps_added, count)
        pool.tensor_tensor(self.rstd[:, :], self.var_eps[:, :], self.consts[:, 1, :], ALU.pow)\
            .then_inc(self.rstd_ready, 1)

    def constants(self, pool):
        pool.memset(self.consts[:, 0, :], EPS).then_inc(self.consts_set, 1)
        pool.memset(self.consts[:, 1, :], -0.5).then_inc(self.consts_set, 1)
        pool.wait_ge(self.consts_set, 2)

    def apply(self, dve, out, x, count):
        dve.wait_ge(self.rstd_ready, count)
        for t in range(NT):
            last = dve.tensor_scalar(out[:, t, :], x[:, t, :], self.mv[:, t, 0:1], self.rstd[:, t:t + 1],
                                     ALU.subtract, ALU.mult)
        return last


def phase_attention(nc, x_in, w_qkvT, w_fcT, b_fc, gamma, beta, ident_in, x1_out, z1_out):
    SCALE = P ** -0.5
    with ExitStack() as ctx:
        def sb(name, shape, dt=F32):
            return ctx.enter_context(nc.sbuf_tensor("a_" + name, shape, dt))

        sems = Semaphores(nc, ctx)

        def sem(name):
            return sems.new("a_" + name)

        wqkv = sb("wqkv", [P, 3, P])
        wfc = sb("wfc", [P, P])
        ident = sb("ident", [P, P])
        bfc = sb("bfc", [P, P])
        gam = sb("gam", [P, P])
        bet = sb("bet", [P, P])
        x = sb("x", [P, 2, NT, P])
        xb = sb("xb", [P, 2, NT, P])
        xbeta = sb("xbeta", [P, 2, NT, P])
        xT = sb("xT", [P, L])
        qT = sb("qT", [P, L])
        kT = sb("kT", [P, L])
        xsum = sb("xsum", [P, 1])
        vsum = sb("vsum", [P, P])
        mx = sb("mx", [P, NT])
        negm = sb("negm", [P, NT])
        rowsum = sb("rowsum", [P, NT])
        rinv = sb("rinv", [P, NT])
        attsum = sb("attsum", [P, 2, NT])
        probs = sb("probs", [P, 2, NT, L])
        att = sb("att", [P, 2, L])
        h = sb("h", [P, NT, P])
        h2 = sb("h2", [P, NT, P])
        x1 = sb("x1", [P, 2, NT, P])
        z1 = sb("z1", [P, 2, NT, P])
        norm = Norm(ctx, nc, sems, "a_norm")
        ps = [ctx.enter_context(nc.psum_tensor(f"a_ps{i}", [P, 512], F32)) for i in range(8)]

        consts = sem("consts")
        x_in_s = [sem("x_loaded0"), sem("x_loaded1")]
        x_free = sem("x_free")
        xb_ready = sem("xb_ready")
        xT_ps = sem("xT_ps")
        xT_sb = sem("xT_sb")
        qkv_ps = sem("qkv_ps")
        q_sb = sem("q_sb")
        k_sb = sem("k_sb")
        vsum_sb = sem("vsum_sb")
        s_ps = sem("scores_ps")
        negm_ready = sem("negm_ready")
        p_sb = sem("probs_sb")
        rinv_ready = sem("rinv_ready")
        att_done = sem("att_done")
        fc_ps = sem("fc_ps")
        fc_read = sem("fc_read")
        chain_s = sem("dve_chain")
        max_ready = sem("max_ready")
        marks = sem("marks")
        x1_ready = sem("x1_ready")
        z1_ready = sem("z1_ready")
        stored = [sem("stored0"), sem("stored1")]
        block = ctx.enter_context(nc.Block())

        @block.sync
        def _(sp):
            sp.dma_start(wqkv[:, :, :], w_qkvT.rearrange("d (c e) -> d c e", c=3)).then_inc(consts, 16)
            sp.dma_start(wfc[:, :], w_fcT).then_inc(consts, 16)
            sp.dma_start(ident[:, :], ident_in).then_inc(consts, 16)
            sp.dma_start(bfc[:, :], row_on_all(b_fc)).then_inc(consts, 16)
            sp.dma_start(gam[:, :], row_on_all(gamma)).then_inc(consts, 16)
            sp.dma_start(bet[:, :], row_on_all(beta)).then_inc(consts, 16)
            for s in range(2):
                sp.dma_start(x[:, s, :, :], x_in[s].rearrange("(t p) d -> p t d", p=P)).then_inc(x_in_s[s], 16)
            for s in range(2):
                sp.sem_inc(stored[s], 32)
            with sp.Fori(0, NB // 2) as it:
                for s in range(2):
                    n = 2 * it + s
                    sp.wait_ge(x1_ready, n + 1)
                    sp.dma_start(x1_out[n], x1[:, s, :, :]).then_inc(stored[s], 16)
                    sp.wait_ge(z1_ready, n + 3)
                    sp.dma_start(z1_out[n], z1[:, s, :, :]).then_inc(stored[s], 16)
                    sp.dma_start(x[:, s, :, :], x_in[(n + 2) % NB].rearrange("(t p) d -> p t d", p=P))\
                        .then_inc(x_in_s[s], 16)
            for s in range(2):
                sp.wait_ge(stored[s], 32 * (NB // 2 + 1))
                sp.wait_ge(x_in_s[s], 16 * (NB // 2 + 1))

        @block.gpsimd
        def _(pool):
            norm.constants(pool)
            pool.wait_ge(consts, 96)
            with pool.Fori(0, NB // 2) as it:
                for s in range(2):
                    n = 2 * it + s
                    pool.wait_ge(x_in_s[s], 16 * it + 16)
                    pool.wait_ge(z1_ready, n + 1)
                    bf = bfc[:, :].unsqueeze(1).broadcast_to([P, NT, P])
                    bt = bet[:, :].unsqueeze(1).broadcast_to([P, NT, P])
                    pool.wait_ge(xT_ps, n + 1)
                    pool.tensor_tensor(xb[:, s, :, :], x[:, s, :, :], bf, ALU.add).then_inc(xb_ready, 1)
                    pool.tensor_tensor(xbeta[:, s, :, :], x[:, s, :, :], bt, ALU.add).then_inc(x_free, 1)
                    for c in range(3):
                        norm.root(pool, 3 * n + c + 1)

        @block.tensor
        def _(pe):
            pe.wait_ge(consts, 96)
            with pe.Fori(0, NB // 2) as it:
                for s in range(2):
                    n = 2 * it + s
                    pe.wait_ge(x_in_s[s], 16 * it + 16)
                    for t in range(NT):
                        last = pe.transpose(ps[0][:, t * P:(t + 1) * P], x[:, s, t, :], ident[:, :])
                    last.then_inc(xT_ps, 1)
                    pe.wait_ge(xT_sb, n + 1)
                    pe.matmul(ps[1][:, :], wqkv[:, 0, :], xT[:, :], start=True, stop=True).then_inc(qkv_ps, 1)
                    pe.matmul(ps[2][:, :], wqkv[:, 1, :], xT[:, :], start=True, stop=True).then_inc(qkv_ps, 1)
                    pe.wait_ge(q_sb, n + 1)
                    pe.wait_ge(k_sb, n + 1)
                    for i in range(NT):
                        pe.wait_ge(p_sb, NT * n + i + 1)
                        pe.matmul(ps[4 + i][:, :], qT[:, i * P:(i + 1) * P], kT[:, :], start=True, stop=True)\
                            .then_inc(s_ps, 1)
                    pe.wait_ge(fc_read, n + 1)
                    pe.matmul(ps[3][:, 0:1], wqkv[:, 2, :], xsum[:, :], start=True, stop=True).then_inc(qkv_ps, 1)
                    pe.wait_ge(vsum_sb, n + 1)
                    pe.matmul(ps[3][:, P:2 * P], vsum[:, :], wfc[:, :], start=True, stop=True).then_inc(fc_ps, 1)

        @block.scalar
        def _(act):
            act.sem_inc(p_sb, NT)
            act.sem_inc(att_done, 2)
            with act.Fori(0, NB // 2) as it:
                for s in range(2):
                    n = 2 * it + s
                    act.wait_ge(xT_ps, n + 1)
                    act.activation(xT[:, :], ps[0][:, :], ACT.Copy, accum_out=xsum[:, :]).then_inc(xT_sb, 1)
                    act.wait_ge(qkv_ps, 3 * n + 1)
                    act.activation(qT[:, :], ps[1][:, :], ACT.Copy).then_inc(q_sb, 1)
                    act.wait_ge(qkv_ps, 3 * n + 2)
                    act.activation(kT[:, :], ps[2][:, :], ACT.Copy).then_inc(k_sb, 1)
                    for i in range(NT):
                        act.wait_ge(negm_ready, NT * n + i + 1)
                        act.activation(probs[:, s, i, :], ps[4 + i][:, :], ACT.Exp, bias=negm[:, i:i + 1],
                                       scale=SCALE, accum_out=rowsum[:, i:i + 1]).then_inc(p_sb, 1)
                    act.wait_ge(qkv_ps, 3 * n + 3)
                    act.activation(vsum[:, :], ps[3][:, 0:1].broadcast_to([P, P]), ACT.Copy).then_inc(vsum_sb, 1)
                    act.wait_ge(rinv_ready, n + 1)
                    for i in range(NT):
                        act.wait_ge(att_done, NT * n + i + 1)
                        act.activation(att[:, i % 2, :], probs[:, s, i, :], ACT.Copy, scale=rinv[:, i:i + 1],
                                       accum_out=attsum[:, s, i:i + 1]).then_inc(att_done, 1)

        @block.vector
        def _(dve):
            def maxima(n, i):
                dve.wait_ge(s_ps, NT * n + i + 1)
                dve.tensor_reduce(mx[:, i:i + 1], ps[4 + i][:, :], AX_X, ALU.max).then_inc(max_ready, 1)
                dve.wait_ge(max_ready, NT * n + i + 1)
                dve.tensor_scalar(negm[:, i:i + 1], mx[:, i:i + 1], -SCALE, None, ALU.mult)\
                    .then_inc(negm_ready, 1)

            def sequence(it, s, ahead):
                n = 2 * it + s
                chain = Chain(dve, chain_s, n, 4)
                dve.wait_ge(p_sb, NT * (n + 2))
                dve.reciprocal(rinv[:, :], rowsum[:, :]).then_inc(rinv_ready, 1)
                if ahead:
                    maxima(n + 1, 0)
                    maxima(n + 1, 1)
                dve.wait_ge(fc_ps, n + 1)
                dve.wait_ge(xb_ready, n + 1)
                dve.sem_inc(marks, 1)
                dve.wait_ge(att_done, NT * (n + 1) + 2)
                for t in range(NT):
                    last = dve.scalar_tensor_tensor(out=h[:, t, :], in0=ps[3][:, P:2 * P],
                                                    scalar=attsum[:, s, t:t + 1], in1=xb[:, s, t, :],
                                                    op0=ALU.mult, op1=ALU.add)
                chain.step(last)
                dve.sem_inc(fc_read, 1)
                norm.moments(dve, h, 3 * n + 1)
                if ahead:
                    maxima(n + 1, 2)
                chain.step(norm.apply(dve, h2, h, 3 * n + 1))
                gm = gam[:, :].unsqueeze(1).broadcast_to([P, NT, P])
                chain.step(dve.tensor_tensor(h[:, :, :], h2[:, :, :], gm, ALU.mult))
                dve.wait_ge(x_free, n + 1)
                chain.step(dve.tensor_tensor(h2[:, :, :], h[:, :, :], xbeta[:, s, :, :], ALU.add))
                norm.moments(dve, h2, 3 * n + 2)
                if ahead:
                    maxima(n + 1, 3)
                dve.wait_ge(stored[s], 32 * it + 32)
                norm.apply(dve, x1[:, s, :, :], h2, 3 * n + 2).then_inc(x1_ready, 1)
                dve.wait_ge(x1_ready, n + 1)
                norm.moments(dve, x1[:, s, :, :], 3 * n + 3)
                norm.apply(dve, z1[:, s, :, :], x1[:, s, :, :], 3 * n + 3).then_inc(z1_ready, 1)
                chain.done()

            dve.sem_inc(fc_read, 1)
            dve.sem_inc(z1_ready, 2)
            dve.wait_ge(consts, 96)
            for i in range(NT):
                maxima(0, i)
            with dve.Fori(0, NB // 2 - 1) as it:
                for s in range(2):
                    sequence(it, s, True)
            for s in range(2):
                sequence(NB // 2 - 1, s, s == 0)


def phase_project(nc, z_in, scale, shift, w_in, biases, tables, ident_in, stacks_out, v9_out, name):
    NC = len(w_in) - 1
    with ExitStack() as ctx:
        def sb(nm, shape, dt=F32):
            return ctx.enter_context(nc.sbuf_tensor(f"{name}_{nm}", shape, dt))

        sems = Semaphores(nc, ctx)

        def sem(nm):
            return sems.new(f"{name}_{nm}")

        w = sb("w", [P, NC + 1, P])
        sc = sb("scale", [P, 2])
        bias = sb("bias", [P, NC])
        ident = sb("ident", [P, P])
        z = sb("z", [P, 2, NT, P])
        zT = sb("zT", [P, L])
        part1 = sb("part1", [P, 2, NC, L], BF16)
        part2 = sb("part2", [P, 2, NC, L], BF16)
        part3 = sb("part3", [P, 2, NC, L], BF16)
        rest1 = sb("rest1", [P, NC, L])
        v9 = sb("v9", [P, 2, NT, H * VW])
        ps_zT = ctx.enter_context(nc.psum_tensor(f"{name}_ps_zT", [P, L], F32))
        ps_c = [ctx.enter_context(nc.psum_tensor(f"{name}_ps_c{c}", [P, L], F32)) for c in range(NC)]
        ps_v = ctx.enter_context(nc.psum_tensor(f"{name}_ps_v", [P, NT * P], F32))

        consts = sem("consts")
        z_loaded = [sem("z_loaded0"), sem("z_loaded1")]
        zT_ps = sem("zT_ps")
        zT_sb = sem("zT_sb")
        c_ps = sem("operands_ps")
        v_ps = sem("v_ps")
        v_sb = sem("v_sb")
        ones_set = sem("ones_set")
        part1_ready = sem("part1_ready")
        rest1_ready = sem("rest1_ready")
        part2_ready = sem("part2_ready")
        part3_ready = sem("part3_ready")
        stored = [sem("stored0"), sem("stored1")]
        v_stored = [sem("v_stored0"), sem("v_stored1")]
        n_const = 16 * (NC + 2 + (2 if scale is not None else 0) + sum(b is not None for b in biases))
        n_set = 1 + sum(b is None for b in biases)
        STORES = 16 * len(TERMS_Q) * NC
        block = ctx.enter_context(nc.Block())

        def term_stores(eng, n, s, c):
            parts = (part1, part2, part3)
            for t, which in enumerate(tables[c]):
                dst = stacks_out[c][n, DH * t:DH * t + DH, :, :].rearrange("d h n -> h d n")
                eng.dma_start(dst, parts[which][:, s, c, :]).then_inc(stored[s], 16)

        @block.sync
        def _(sp):
            for c in range(NC + 1):
                sp.dma_start(w[:, c, :], w_in[c]).then_inc(consts, 16)
            sp.dma_start(ident[:, :], ident_in).then_inc(consts, 16)
            if scale is not None:
                sp.dma_start(sc[:, 0:1], scale.rearrange("(d o) -> d o", o=1)).then_inc(consts, 16)
                sp.dma_start(sc[:, 1:2], shift.rearrange("(d o) -> d o", o=1)).then_inc(consts, 16)
            for c in range(NC):
                if biases[c] is not None:
                    sp.dma_start(bias[:, c:c + 1], biases[c].rearrange("(d o) -> d o", o=1)).then_inc(consts, 16)
            for s in range(2):
                sp.dma_start(z[:, s, :, :], z_in[s]).then_inc(z_loaded[s], 16)
                sp.sem_inc(stored[s], STORES)
                sp.sem_inc(v_stored[s], 16)
            with sp.Fori(0, NB // 2) as it:
                for s in range(2):
                    n = 2 * it + s
                    sp.wait_ge(zT_ps, n + 1)
                    sp.dma_start(z[:, s, :, :], z_in[(n + 2) % NB]).then_inc(z_loaded[s], 16)
                    sp.wait_ge(v_sb, n + 1)
                    sp.dma_start(v9_out[n], v9[:, s, :, :]).then_inc(v_stored[s], 16)
                    for c in range(NC):
                        sp.wait_ge(part3_ready, NC * (n + 1) + c + 1)
                        term_stores(sp, n, s, c)
            for s in range(2):
                sp.wait_ge(stored[s], STORES * (NB // 2 + 1))
                sp.wait_ge(v_stored[s], 16 * (NB // 2 + 1))
                sp.wait_ge(z_loaded[s], 16 * (NB // 2 + 1))

        @block.gpsimd
        def _(pool):
            for c in range(NC):
                if biases[c] is None:
                    pool.memset(bias[:, c:c + 1], 0.0).then_inc(ones_set, 1)
            pool.memset(v9[:, :, :, :], 1.0).then_inc(ones_set, 1)

        @block.tensor
        def _(pe):
            pe.wait_ge(consts, n_const)
            with pe.Fori(0, NB // 2) as it:
                for s in range(2):
                    n = 2 * it + s
                    pe.wait_ge(z_loaded[s], 16 * it + 16)
                    for t in range(NT):
                        last = pe.transpose(ps_zT[:, t * P:(t + 1) * P], z[:, s, t, :], ident[:, :])
                    last.then_inc(zT_ps, 1)
                    pe.wait_ge(zT_sb, n + 1)
                    for c in range(NC):
                        pe.wait_ge(rest1_ready, NC * n + c + 1)
                        pe.matmul(ps_c[c][:, :], w[:, c, :], zT[:, :], start=True, stop=True).then_inc(c_ps, 1)
                    for t in range(NT):
                        last = pe.matmul(ps_v[:, t * P:(t + 1) * P], zT[:, t * P:(t + 1) * P], w[:, NC, :],
                                         start=True, stop=True)
                    last.then_inc(v_ps, 1)

        @block.scalar
        def _(act):
            act.wait_ge(consts, n_const)
            act.wait_ge(ones_set, n_set)
            with act.Fori(0, NB // 2) as it:
                for s in range(2):
                    n = 2 * it + s
                    act.wait_ge(zT_ps, n + 1)
                    if scale is not None:
                        act.activation(zT[:, :], ps_zT[:, :], ACT.Identity, bias=sc[:, 1:2], scale=sc[:, 0:1])\
                            .then_inc(zT_sb, 1)
                    else:
                        act.activation(zT[:, :], ps_zT[:, :], ACT.Copy).then_inc(zT_sb, 1)
                    act.wait_ge(stored[s], STORES * (it + 1))
                    for c in range(NC):
                        act.wait_ge(c_ps, NC * n + c + 1)
                        act.activation(part1[:, s, c, :], ps_c[c][:, :], ACT.Identity, bias=bias[:, c:c + 1])\
                            .then_inc(part1_ready, 1)
                    act.wait_ge(v_ps, n + 1)
                    act.wait_ge(v_stored[s], 16 * (it + 1))
                    act.activation(v9[:, s, :, :].rearrange("p t (h v) -> p (t h) v", v=VW)[:, :, 0:DH],
                                   ps_v[:, :].rearrange("p (g d) -> p g d", d=DH), ACT.Copy).then_inc(v_sb, 1)
                    for c in range(NC):
                        act.wait_ge(rest1_ready, NC * (n + 1) + c + 1)
                        act.activation(part2[:, s, c, :], rest1[:, c, :], ACT.Copy).then_inc(part2_ready, 1)

        @block.vector
        def _(dve):
            dve.sem_inc(rest1_ready, NC)
            dve.sem_inc(part3_ready, NC)
            dve.wait_ge(consts, n_const)
            dve.wait_ge(ones_set, n_set)
            with dve.Fori(0, NB // 2) as it:
                for s in range(2):
                    n = 2 * it + s
                    dve.wait_ge(part3_ready, NC * (n + 1))
                    for c in range(NC):
                        dve.wait_ge(part1_ready, NC * n + c + 1)
                        dve.scalar_tensor_tensor(out=rest1[:, c, :], in0=ps_c[c][:, :], scalar=bias[:, c:c + 1],
                                                 in1=part1[:, s, c, :], op0=ALU.add, op1=ALU.subtract)\
                            .then_inc(rest1_ready, 1)
                    for c in range(NC):
                        dve.wait_ge(part2_ready, NC * n + c + 1)
                        dve.tensor_tensor(part3[:, s, c, :], rest1[:, c, :], part2[:, s, c, :], ALU.subtract)\
                            .then_inc(part3_ready, 1)


def phase_causal(nc, q_stacks, k_stacks, v9_in, mask_in, maskT_in, ident_in, ctx_out):
    SCALE = DH ** -0.5
    M0 = 64
    TILES = ((0,), (1, 3), (2,))
    OFF = {0: 0, 1: 512, 3: 896, 2: 1024}
    WIDTH = {0: 512, 1: 384, 2: 256, 3: 128}
    NTILE = len(TILES)
    with ExitStack() as ctx:
        def sb(name, shape, dt=F32):
            return ctx.enter_context(nc.sbuf_tensor("c_" + name, shape, dt))

        sems = Semaphores(nc, ctx)

        def sem(name):
            return sems.new("c_" + name)

        def bank(name):
            return ctx.enter_context(nc.psum_tensor("c_" + name, [P, 512], F32))

        q = sb("q", [P, 2, G, L], BF16)
        k = sb("k", [P, 2, G, L], BF16)
        v9 = sb("v9", [P, 2, NT, G * VW])
        mask32 = sb("mask32", [P, P])
        maskT32 = sb("maskT32", [P, P])
        mask = sb("mask", [P, P], BF16)
        maskT = sb("maskT", [P, P], BF16)
        identb = sb("identb", [P, P], BF16)
        ident = sb("ident", [P, P])
        zeros = sb("zeros", [P, 512], BF16)
        mx = sb("mx", [P, G * NT])
        mrow = sb("mrow", [G * NT, 2, P], BF16)
        probs = sb("probs", [P, 2, 1280])
        osb = sb("osb", [P, 2, G, P])
        ps_rows = [bank("ps_rows0"), bank("ps_rows1")]
        ps_m = bank("ps_m")
        ps_keys = [bank(f"ps_keys{i}") for i in range(4)]
        ps_out = bank("ps_out")

        consts = sem("consts")
        preset = sem("preset")
        minus_ones = sem("minus_ones")
        loaded = [sem("loaded0"), sem("loaded1")]
        rows_ps = sem("rows_ps")
        max_read = sem("max_read")
        m_ps = sem("m_ps")
        m_first = sem("m_first")
        m_split = sem("m_split")
        m_loaded = [sem("m_loaded0"), sem("m_loaded1")]
        keys_ps = sem("keys_ps")
        exp_done = sem("exp_done")
        head_done = sem("head_done")
        out_sb = sem("out_sb")
        stored = [sem("stored0"), sem("stored1")]
        block = ctx.enter_context(nc.Block())

        def load(eng, n, s):
            b, g = n // NG, n % NG
            eng.dma_start(q[0:SK, s, :, :], q_stacks.rearrange("b r (g h) t -> b g r h t", h=G)[b, g])\
                .then_inc(loaded[s], 16)
            eng.dma_start(k[0:SK, s, :, :], k_stacks.rearrange("b r (g h) t -> b g r h t", h=G)[b, g])\
                .then_inc(loaded[s], 16)
            eng.dma_start(v9[:, s, :, :], v9_in.rearrange("b p t (g v) -> b g p t v", g=NG)[b, g])\
                .then_inc(loaded[s], 16)

        def load_maxima(eng, s):
            for r in range(2):
                eng.dma_start(q[M0 + r:M0 + r + 1, s, :, :], mrow[:, r, :]).then_inc(m_loaded[s], 16)

        @block.sync
        def _(sp):
            for dst, src in ((mask32, mask_in), (maskT32, maskT_in), (ident, ident_in)):
                sp.dma_start(dst[:, :], src).then_inc(consts, 16)
            sp.wait_ge(preset, 2)
            sp.wait_ge(minus_ones, 1)
            load(sp, 0, 0)
            load(sp, 1, 1)
            for s in range(2):
                sp.sem_inc(stored[s], 64)
            sp.wait_ge(m_split, 1)
            load_maxima(sp, 0)
            with sp.Fori(0, NI // 2) as it:
                for s in range(2):
                    n = 2 * it + s
                    sp.wait_ge(m_split, n + 2)
                    load_maxima(sp, 1 - s)
                    sp.wait_ge(head_done, G * (n + 1) + 2)
                    load(sp, (n + 2) % NI, s)
                    sp.wait_ge(out_sb, n + 2)
                    for b in range(NT):
                        sp.dma_start(ctx_out[n, :, :, b * P:(b + 1) * P].rearrange("h r i -> r h i"),
                                     osb[32 * b:32 * b + VW, s, :, :]).then_inc(stored[s], 16)
            for s in range(2):
                sp.wait_ge(loaded[s], 48 * (NI // 2 + 1))
                sp.wait_ge(m_loaded[s], 32 * (NI // 2 + 1 - s))
                sp.wait_ge(stored[s], 64 * (NI // 2 + 1))

        @block.gpsimd
        def _(pool):
            pool.wait_ge(preset, 1)
            pool.memset(k[M0:M0 + 2, :, :, :], -1.0).then_inc(minus_ones, 1)

        @block.tensor
        def _(pe):
            def max_head(s, h, tile):
                for b in range(NT):
                    ps = ps_rows[b % 2]
                    if not isinstance(tile, int) or tile + b >= 2:
                        pe.wait_ge(max_read, tile + b - 1)
                    pe.matmul(ps[:, 0:(b + 1) * P], q[0:M0, s, h, b * P:(b + 1) * P], k[0:M0, s, h, 0:(b + 1) * P],
                              start=True, stop=False)
                    pe.matmul(ps[:, b * P:(b + 1) * P], identb[:, :], mask[:, :], start=False, stop=True)\
                        .then_inc(rows_ps, 1)

            def turn_maxima(n):
                pe.wait_ge(max_read, G * NT * (n + 1))
                pe.transpose(ps_m[0:G * NT, 0:P], mx[:, :], ident[:, :]).then_inc(m_ps, 1)

            def key_head(n, s, h):
                for c, blocks in enumerate(TILES):
                    tile = NTILE * (G * n + h) + c
                    ps = ps_keys[(NTILE * h + c) % 4]
                    pe.wait_ge(exp_done, tile + 1)
                    at = 0
                    for j in blocks:
                        pe.matmul(ps[:, at:at + WIDTH[j]], k[:, s, h, j * P:(j + 1) * P], q[:, s, h, j * P:L],
                                  start=True, stop=False)
                        last = pe.matmul(ps[:, at:at + P], identb[:, :], maskT[:, :], start=False, stop=True)
                        at += WIDTH[j]
                    last.then_inc(keys_ps, 1)

            def value_head(n, s, h):
                pe.wait_ge(exp_done, NTILE * (G * n + h + 1) + 4)
                if h == 0:
                    pe.wait_ge(out_sb, n + 1)
                for j in range(NT):
                    for b in range(j, NT):
                        last = pe.matmul(ps_out[32 * b:32 * b + VW, h * P:(h + 1) * P],
                                         v9[:, s, j, h * VW:(h + 1) * VW],
                                         probs[:, h % 2, OFF[j] + (b - j) * P:OFF[j] + (b - j + 1) * P],
                                         start=(j == 0), stop=(j == b), skip_group_check=True)
                last.then_inc(head_done, 1)

            pe.wait_ge(consts, 48)
            pe.wait_ge(preset, 6)
            pe.wait_ge(minus_ones, 1)
            pe.matmul(ps_out[:, :], zeros[:, 0:P], zeros[:, :], start=True, stop=True)
            pe.wait_ge(loaded[0], 48)
            for h in range(G):
                max_head(0, h, NT * h)
            turn_maxima(0)
            with pe.Fori(0, NI // 2) as it:
                for s in range(2):
                    n = 2 * it + s
                    pe.wait_ge(loaded[1 - s], 48 * (it + 1 + s))
                    for h in range(G):
                        if h < 2:
                            for hh in (2 * h, 2 * h + 1):
                                max_head(1 - s, hh, NT * (G * (n + 1) + hh))
                        if h == 0:
                            pe.wait_ge(m_loaded[s], 32 * (it + 1))
                        key_head(n, s, h)
                        if h == G - 1:
                            turn_maxima(n + 1)
                        if h:
                            value_head(n, s, h - 1)
                    value_head(n, s, G - 1)

        @block.scalar
        def _(act):
            act.sem_inc(exp_done, 4)
            act.sem_inc(out_sb, 1)
            with act.Fori(0, NI // 2) as it:
                for s in range(2):
                    n = 2 * it + s
                    for h in range(G):
                        act.wait_ge(head_done, G * n + h + 1)
                        for c, blocks in enumerate(TILES):
                            width = sum(WIDTH[j] for j in blocks)
                            act.wait_ge(keys_ps, NTILE * (G * n + h) + c + 1)
                            act.activation(probs[:, h % 2, OFF[blocks[0]]:OFF[blocks[0]] + width],
                                           ps_keys[(NTILE * h + c) % 4][:, 0:width], ACT.Exp, scale=SCALE)\
                                .then_inc(exp_done, 1)
                    act.wait_ge(head_done, G * (n + 1) + 2)
                    act.wait_ge(stored[s], 64 * (it + 1))
                    act.activation(osb[:, s, :, :].rearrange("p h i -> p (h i)"), ps_out[:, :], ACT.Copy)\
                        .then_inc(out_sb, 1)

        @block.vector
        def _(dve):
            def maxima(tile):
                for m in range(G * NT):
                    dve.wait_ge(rows_ps, tile + m + 1)
                    dve.tensor_reduce(mx[:, m:m + 1], ps_rows[m % 2][:, 0:(m % NT + 1) * P], AX_X, ALU.max)\
                        .then_inc(max_read, 1)

            def split_maxima(n):
                dve.wait_ge(m_ps, n + 1)
                dve.tensor_copy(mrow[:, 0, :], ps_m[0:G * NT, 0:P]).then_inc(m_first, 1)
                dve.wait_ge(m_first, n + 1)
                dve.tensor_tensor(mrow[:, 1, :], ps_m[0:G * NT, 0:P], mrow[:, 0, :], ALU.subtract)\
                    .then_inc(m_split, 1)

            dve.memset(k[:, :, :, :].rearrange("p s h t -> p (s h t)").bitcast(F32), 0.0).then_inc(preset, 1)
            dve.memset(q[:, :, :, :].rearrange("p s h t -> p (s h t)").bitcast(F32), 0.0).then_inc(preset, 1)
            dve.memset(zeros[:, :].bitcast(F32), 0.0).then_inc(preset, 1)
            dve.wait_ge(consts, 48)
            for narrow, full in ((mask, mask32), (maskT, maskT32), (identb, ident)):
                dve.tensor_copy(narrow[:, :], full[:, :]).then_inc(preset, 1)
            dve.sem_inc(head_done, 2)
            maxima(0)
            split_maxima(0)
            with dve.Fori(0, NI // 2) as it:
                for s in range(2):
                    n = 2 * it + s
                    maxima(G * NT * (n + 1))
                    split_maxima(n + 1)


def phase_merge(nc, ctx_in, x_in, w_in, b_in, base_out, z_out, name):
    with ExitStack() as ctx:
        def sb(nm, shape, dt=F32):
            return ctx.enter_context(nc.sbuf_tensor(f"{name}_{nm}", shape, dt))

        sems = Semaphores(nc, ctx)

        def sem(nm):
            return sems.new(f"{name}_{nm}")

        w = sb("w", [P, P])
        bo = sb("bo", [P, P])
        num = sb("num", [P, 2, L])
        den = sb("den", [P, 2, L])
        x = sb("x", [P, 2, NT, P])
        xb = sb("xb", [P, 2, NT, P])
        rec = sb("rec", [P, L])
        cT = sb("cT", [P, 2, L])
        xa = sb("xa", [P, 2, NT, P])
        base = sb("base", [P, 2, NT, P])
        z = sb("z", [P, 2, NT, P])
        norm = Norm(ctx, nc, sems, name + "_norm")
        ps = [ctx.enter_context(nc.psum_tensor(f"{name}_ps{i}", [P, L], F32)) for i in range(2)]

        consts = sem("consts")
        loaded = [sem("loaded0"), sem("loaded1")]
        rec_ready = sem("rec_ready")
        cT_ready = sem("cT_ready")
        a_ps = sem("a_ps")
        xb_ready = sem("xb_ready")
        xa_ready = sem("xa_ready")
        base_ready = sem("base_ready")
        z_ready = sem("z_ready")
        stored = [sem("stored0"), sem("stored1")]
        n_const = 16 + 16 * (b_in is not None)
        n_out = 16 + 16 * (base_out is not None)
        block = ctx.enter_context(nc.Block())

        def load(eng, n, s):
            sums = ctx_in[NG * n:NG * n + NG] if isinstance(n, int) else ctx_in.rearrange(
                "(b g) h r t -> b g h r t", g=NG)[n]
            sums = sums.rearrange("g h r t -> (g h) r t")
            eng.dma_start(num[:, s, :], sums[:, 0:DH, :]).then_inc(loaded[s], 16)
            eng.dma_start(den[:, s, :], sums[:, DH:DH + 1, :].broadcast_to([H, DH, L])).then_inc(loaded[s], 16)
            eng.dma_start(x[:, s, :, :], x_in[n]).then_inc(loaded[s], 16)

        @block.sync
        def _(sp):
            sp.dma_start(w[:, :], w_in).then_inc(consts, 16)
            if b_in is not None:
                sp.dma_start(bo[:, :], row_on_all(b_in)).then_inc(consts, 16)
            for s in range(2):
                sp.sem_inc(stored[s], n_out)
                load(sp, s, s)
            with sp.Fori(0, NB // 2) as it:
                for s in range(2):
                    n = 2 * it + s
                    sp.wait_ge(z_ready, n + 1)
                    sp.wait_ge(base_ready, n + 1)
                    load(sp, (n + 2) % NB, s)
                    sp.dma_start(z_out[n], z[:, s, :, :]).then_inc(stored[s], 16)
                    if base_out is not None:
                        sp.dma_start(base_out[n], base[:, s, :, :]).then_inc(stored[s], 16)
            for s in range(2):
                sp.wait_ge(loaded[s], 48 * (NB // 2 + 1))
                sp.wait_ge(stored[s], n_out * (NB // 2 + 1))

        @block.gpsimd
        def _(pool):
            norm.constants(pool)
            pool.wait_ge(consts, n_const)
            with pool.Fori(0, NB // 2) as it:
                for s in range(2):
                    n = 2 * it + s
                    if b_in is not None:
                        pool.wait_ge(loaded[s], 48 * (it + 1))
                        pool.wait_ge(xa_ready, n + 1)
                        pool.tensor_tensor(xb[:, s, :, :], x[:, s, :, :],
                                           bo[:, :].unsqueeze(1).broadcast_to([P, NT, P]), ALU.add)\
                            .then_inc(xb_ready, 1)
                    norm.root(pool, n + 1)
                    pool.wait_ge(xa_ready, n + 3)
                    pool.wait_ge(stored[s], n_out * (it + 1))
                    pool.tensor_tensor(base[:, s, :, :], xa[:, s, :, :], x[:, s, :, :], ALU.add)\
                        .then_inc(base_ready, 1)

        @block.tensor
        def _(pe):
            pe.wait_ge(consts, n_const)
            with pe.Fori(0, NB // 2) as it:
                for s in range(2):
                    n = 2 * it + s
                    pe.wait_ge(cT_ready, n + 1)
                    pe.wait_ge(xa_ready, n + 1)
                    for t in range(NT):
                        last = pe.matmul(ps[s][:, t * P:(t + 1) * P], cT[:, s, t * P:(t + 1) * P], w[:, :],
                                         start=True, stop=True)
                    last.then_inc(a_ps, 1)

        @block.vector
        def _(dve):
            dve.sem_inc(xa_ready, 2)
            with dve.Fori(0, NB // 2) as it:
                for s in range(2):
                    n = 2 * it + s
                    dve.wait_ge(loaded[s], 48 * (it + 1))
                    dve.reciprocal(rec[:, :], den[:, s, :]).then_inc(rec_ready, 1)
                    dve.wait_ge(rec_ready, n + 1)
                    dve.tensor_tensor(cT[:, s, :], num[:, s, :], rec[:, :], ALU.mult).then_inc(cT_ready, 1)
                    dve.wait_ge(a_ps, n + 1)
                    if b_in is not None:
                        dve.wait_ge(xb_ready, n + 1)
                    dve.wait_ge(stored[s], n_out * (it + 1))
                    src = xb if b_in is not None else x
                    dve.tensor_tensor(xa[:, s, :, :], ps[s][:, :].rearrange("p (t d) -> p t d", t=NT),
                                      src[:, s, :, :], ALU.add).then_inc(xa_ready, 1)
                    dve.wait_ge(xa_ready, n + 3)
                    norm.moments(dve, xa[:, s, :, :], n + 1)
                    norm.apply(dve, z[:, s, :, :], xa[:, s, :, :], n + 1).then_inc(z_ready, 1)


def phase_experts(nc, z_in, base_in, scale, shift, gate_in, w1_in, w2_in, w3_in, iota_in, ident_in, x_out):
    with ExitStack() as ctx:
        def sb(name, shape, dt=F32):
            return ctx.enter_context(nc.sbuf_tensor("e_" + name, shape, dt))

        sems = Semaphores(nc, ctx)

        def sem(name):
            return sems.new("e_" + name)

        KH = HID // P
        w1 = sb("w1", [P, NE, HID])
        w2 = sb("w2", [P, NE, HID])
        w3 = sb("w3", [P, NE, KH, P])
        gate = sb("gate", [P, NE])
        sc = sb("scale", [P, 2])
        ident = sb("ident", [P, P])
        iota = sb("iota", [P, NE])
        z = sb("z", [P, 2, NT, P])
        base = sb("base", [P, 2, NT, P])
        hT = sb("hT", [P, 2, L])
        scores = sb("scores", [P, NT, NE])
        top = sb("top", [P, NT, 8])
        idx = sb("idx", [P, NT, 8], U32)
        idxf = sb("idxf", [P, NT, 8])
        diff = sb("diff", [P, NT])
        ediff = sb("ediff", [P, NT])
        denom = sb("denom", [P, NT])
        pr = sb("pr", [P, 2, NT])
        hot = sb("hot", [P, 2, NT, NE])
        weight = sb("weight", [P, NT, NE])
        silu = sb("silu", [P, KH, L])
        gu = sb("gu", [P, 2, KH, L])
        acc = sb("acc", [P, NT, P])
        xo = sb("xo", [P, 2, NT, P])
        norm = Norm(ctx, nc, sems, "e_norm")
        ps_zT = ctx.enter_context(nc.psum_tensor("e_ps_zT", [P, L], F32))
        ps_s = ctx.enter_context(nc.psum_tensor("e_ps_s", [P, 512], F32))
        ps_a = ctx.enter_context(nc.psum_tensor("e_ps_a", [P, KH, L], F32))
        ps_b = ctx.enter_context(nc.psum_tensor("e_ps_b", [P, KH, L], F32))
        ps_o = [ctx.enter_context(nc.psum_tensor(f"e_ps_o{i}", [P, L], F32)) for i in range(2)]

        consts = sem("consts")
        loaded = [sem("loaded0"), sem("loaded1")]
        zT_ps = sem("zT_ps")
        hT_sb = sem("hT_sb")
        s_ps = sem("scores_ps")
        diff_ready = sem("diff_ready")
        exp_ready = sem("exp_ready")
        chain_s = sem("chain")
        weight_ready = sem("weight_ready")
        marks = sem("marks")
        a_ps = sem("a_ps")
        b_ps = sem("b_ps")
        silu_sb = sem("silu_sb")
        gu_sb = sem("gu_sb")
        o_ps = sem("o_ps")
        o_read = sem("o_read")
        base_free = sem("base_free")
        x_ready = sem("x_ready")
        stored = [sem("stored0"), sem("stored1")]
        n_const = 16 * 8
        block = ctx.enter_context(nc.Block())

        def load(eng, n, s):
            eng.dma_start(z[:, s, :, :], z_in[n]).then_inc(loaded[s], 16)
            eng.dma_start(base[:, s, :, :], base_in[n]).then_inc(loaded[s], 16)

        @block.sync
        def _(sp):
            sp.dma_start(gate[:, :], gate_in).then_inc(consts, 16)
            sp.dma_start(sc[:, 0:1], scale.rearrange("(d o) -> d o", o=1)).then_inc(consts, 16)
            sp.dma_start(sc[:, 1:2], shift.rearrange("(d o) -> d o", o=1)).then_inc(consts, 16)
            sp.dma_start(ident[:, :], ident_in).then_inc(consts, 16)
            sp.dma_start(iota[:, :], row_on_all(iota_in, NE)).then_inc(consts, 16)
            for s in range(2):
                sp.sem_inc(stored[s], 16)
                load(sp, s, s)
            sp.dma_start(w1[:, :, :], w1_in.rearrange("e d h -> d e h")).then_inc(consts, 16)
            sp.dma_start(w2[:, :, :], w2_in.rearrange("e d h -> d e h")).then_inc(consts, 16)
            sp.dma_start(w3[:, :, :, :].rearrange("p e k d -> p (e k) d"),
                         w3_in.rearrange("e (k p) d -> p (e k) d", p=P)).then_inc(consts, 16)
            with sp.Fori(0, NB // 2) as it:
                for s in range(2):
                    n = 2 * it + s
                    sp.wait_ge(base_free, n + 1)
                    load(sp, (n + 2) % NB, s)
                    sp.wait_ge(x_ready, n + 1)
                    sp.dma_start(x_out[n], xo[:, s, :, :]).then_inc(stored[s], 16)
            for s in range(2):
                sp.wait_ge(loaded[s], 32 * (NB // 2 + 1))
                sp.wait_ge(stored[s], 16 * (NB // 2 + 1))

        @block.gpsimd
        def _(pool):
            norm.constants(pool)
            with pool.Fori(0, NB) as n:
                norm.root(pool, n + 1)

        @block.tensor
        def _(pe):
            def route(n, s, load_count):
                pe.wait_ge(loaded[s], load_count)
                for t in range(NT):
                    last = pe.transpose(ps_zT[:, t * P:(t + 1) * P], z[:, s, t, :], ident[:, :])
                last.then_inc(zT_ps, 1)
                pe.wait_ge(hT_sb, n + 1)
                for t in range(NT):
                    last = pe.matmul(ps_s[:, t * NE:(t + 1) * NE], hT[:, s, t * P:(t + 1) * P], gate[:, :],
                                     start=True, stop=True)
                last.then_inc(s_ps, 1)

            def up(w, ps, e, s, ready):
                for k in range(KH):
                    last = pe.matmul(ps[:, k, :], w[:, e, k * P:(k + 1) * P], hT[:, s, :], start=True, stop=True)
                last.then_inc(ready, 1)

            def down(m, e, parity):
                pe.wait_ge(gu_sb, m + 2)
                pe.wait_ge(o_read, m + 1)
                for t in range(NT):
                    for k in range(KH):
                        last = pe.matmul(ps_o[parity][:, t * P:(t + 1) * P], gu[:, parity, k, t * P:(t + 1) * P],
                                         w3[:, e, k, :], start=(k == 0), stop=(k == KH - 1))
                last.then_inc(o_ps, 1)

            pe.wait_ge(consts, n_const)
            route(0, 0, 32)
            with pe.Fori(0, NB // 2) as it:
                for s in range(2):
                    n = 2 * it + s
                    for e in range(NE):
                        m = NE * n + e
                        pe.wait_ge(silu_sb, m + 1)
                        up(w1, ps_a, e, s, a_ps)
                        pe.wait_ge(gu_sb, m + 1)
                        up(w2, ps_b, e, s, b_ps)
                        if e == 0:
                            route(n + 1, 1 - s, 32 * (it + 1 + s))
                        if e:
                            down(m - 1, e - 1, (e - 1) % 2)
                    down(NE * (n + 1) - 1, NE - 1, (NE - 1) % 2)

        @block.scalar
        def _(act):
            def turn(n, s):
                act.wait_ge(zT_ps, n + 1)
                act.activation(hT[:, s, :], ps_zT[:, :], ACT.Identity, bias=sc[:, 1:2], scale=sc[:, 0:1])\
                    .then_inc(hT_sb, 1)

            def weigh(n):
                act.wait_ge(diff_ready, n + 1)
                act.activation(ediff[:, :], diff[:, :], ACT.Exp).then_inc(exp_ready, 1)

            act.sem_inc(silu_sb, 1)
            act.wait_ge(consts, n_const)
            turn(0, 0)
            weigh(0)
            with act.Fori(0, NB // 2) as it:
                for s in range(2):
                    n = 2 * it + s
                    for e in range(NE):
                        m = NE * n + e
                        act.wait_ge(a_ps, m + 1)
                        act.wait_ge(gu_sb, m + 1)
                        act.activation(silu[:, :, :], ps_a[:, :, :], ACT.Silu).then_inc(silu_sb, 1)
                        if e == 0:
                            turn(n + 1, 1 - s)
                    weigh(n + 1)

        @block.vector
        def _(dve):
            def choose(n):
                chain = Chain(dve, chain_s, n, 8)
                dve.wait_ge(s_ps, n + 1)
                chain.step(dve.tensor_copy(scores[:, :, :].rearrange("p t e -> p (t e)"), ps_s[:, 0:NT * NE]))
                dve.sem_inc(marks, 1)
                for t in range(NT):
                    last = dve.max(top[:, t, :], scores[:, t, :])
                chain.step(last)
                dve.tensor_tensor(diff[:, :], top[:, :, 1], top[:, :, 0], ALU.subtract).then_inc(diff_ready, 1)
                for t in range(NT):
                    last = dve.max_index(idx[:, t, :], top[:, t, :], scores[:, t, :])
                chain.step(last)
                chain.step(dve.tensor_copy(idxf[:, :, :], idx[:, :, :]))
                dve.wait_ge(exp_ready, n + 1)
                chain.step(dve.tensor_scalar(denom[:, :], ediff[:, :], 1.0, None, ALU.add))
                chain.step(dve.reciprocal(pr[:, 0, :], denom[:, :]))
                chain.step(dve.tensor_tensor(pr[:, 1, :], pr[:, 0, :], ediff[:, :], ALU.mult))
                for t in range(NT):
                    for r in range(2):
                        last = dve.tensor_scalar(hot[:, r, t, :], iota[:, :], idxf[:, t, r:r + 1],
                                                 pr[:, r, t:t + 1], ALU.is_equal, ALU.mult)
                chain.step(last)
                dve.tensor_tensor(weight[:, :, :], hot[:, 0, :, :], hot[:, 1, :, :], ALU.add)\
                    .then_inc(weight_ready, 1)
                chain.done()

            def add_expert(n, m, s, e):
                dve.wait_ge(o_ps, m + 1)
                if e == 0:
                    dve.wait_ge(weight_ready, n + 1)
                dve.wait_ge(o_read, m + 1)
                for t in range(NT):
                    prev = base[:, s, t, :] if e == 0 else acc[:, t, :]
                    last = dve.scalar_tensor_tensor(out=acc[:, t, :], in0=ps_o[e % 2][:, t * P:(t + 1) * P],
                                                    scalar=weight[:, t, e:e + 1], in1=prev,
                                                    op0=ALU.mult, op1=ALU.add)
                last.then_inc(o_read, 1)
                if e == 0:
                    dve.wait_ge(o_read, m + 2)
                    dve.sem_inc(base_free, 1)

            dve.sem_inc(gu_sb, 1)
            dve.sem_inc(o_read, 1)
            dve.wait_ge(consts, n_const)
            choose(0)
            with dve.Fori(0, NB // 2) as it:
                for s in range(2):
                    n = 2 * it + s
                    for e in range(NE):
                        m = NE * n + e
                        dve.wait_ge(silu_sb, m + 2)
                        dve.wait_ge(b_ps, m + 1)
                        dve.tensor_tensor(gu[:, e % 2, :, :], silu[:, :, :], ps_b[:, :, :], ALU.mult)\
                            .then_inc(gu_sb, 1)
                        if e:
                            add_expert(n, m - 1, s, e - 1)
                    add_expert(n, NE * (n + 1) - 1, s, NE - 1)
                    dve.wait_ge(o_read, NE * (n + 1) + 1)
                    norm.moments(dve, acc, n + 1)
                    dve.wait_ge(stored[s], 16 * (it + 1))
                    norm.apply(dve, xo[:, s, :, :], acc, n + 1).then_inc(x_ready, 1)
                    dve.wait_ge(x_ready, n + 1)
                    choose(n + 1)


def phase_last(nc, x_in, u1_in, v1_in, b1_in, u2_in, v2_in, b2_in, ident_in, out):
    KF = FF // P
    with ExitStack() as ctx:
        def sb(name, shape, dt=F32):
            return ctx.enter_context(nc.sbuf_tensor("f_" + name, shape, dt))

        sems = Semaphores(nc, ctx)

        def sem(name):
            return sems.new("f_" + name)

        u1 = sb("u1", [P, RANK])
        v1 = sb("v1", [RANK, FF])
        b1 = sb("b1", [P, KF])
        u2 = sb("u2", [P, KF, RANK])
        v2 = sb("v2", [RANK, P])
        b2 = sb("b2", [P, P])
        ident = sb("ident", [P, P])
        x = sb("x", [P, 2, NT, P])
        xb = sb("xb", [P, 2, NT, P])
        xT = sb("xT", [P, L])
        pT = sb("pT", [RANK, L])
        hT = sb("hT", [P, KF, L])
        qT = sb("qT", [RANK, L])
        t1 = sb("t1", [P, NT, P])
        y = sb("y", [P, 2, NT, P])
        norm = Norm(ctx, nc, sems, "f_norm")
        ps_xT = ctx.enter_context(nc.psum_tensor("f_ps_xT", [P, L], F32))
        ps_pq = ctx.enter_context(nc.psum_tensor("f_ps_pq", [P, L], F32))
        ps_h = [ctx.enter_context(nc.psum_tensor(f"f_ps_h{i}", [P, L], F32)) for i in range(KF)]
        ps_y = ctx.enter_context(nc.psum_tensor("f_ps_y", [P, L], F32))

        consts = sem("consts")
        loaded = [sem("loaded0"), sem("loaded1")]
        xT_ps = sem("xT_ps")
        xT_sb = sem("xT_sb")
        p_ps = sem("p_ps")
        p_sb = sem("p_sb")
        h_ps = sem("h_ps")
        h_sb = sem("h_sb")
        q_ps = sem("q_ps")
        q_sb = sem("q_sb")
        y_ps = sem("y_ps")
        y_read = sem("y_read")
        xb_ready = sem("xb_ready")
        out_ready = sem("out_ready")
        stored = [sem("stored0"), sem("stored1")]
        block = ctx.enter_context(nc.Block())

        @block.sync
        def _(sp):
            sp.dma_start(u1[:, :], u1_in).then_inc(consts, 16)
            sp.dma_start(v1[:, :], v1_in).then_inc(consts, 16)
            sp.dma_start(b1[:, :], b1_in).then_inc(consts, 16)
            sp.dma_start(u2[:, :, :], u2_in.rearrange("(k p) r -> p k r", p=P)).then_inc(consts, 16)
            sp.dma_start(v2[:, :], v2_in).then_inc(consts, 16)
            sp.dma_start(b2[:, :], row_on_all(b2_in)).then_inc(consts, 16)
            sp.dma_start(ident[:, :], ident_in).then_inc(consts, 16)
            for s in range(2):
                sp.sem_inc(stored[s], 16)
                sp.dma_start(x[:, s, :, :], x_in[s]).then_inc(loaded[s], 16)
            with sp.Fori(0, NB // 2) as it:
                for s in range(2):
                    n = 2 * it + s
                    sp.wait_ge(xb_ready, n + 1)
                    sp.dma_start(x[:, s, :, :], x_in[(n + 2) % NB]).then_inc(loaded[s], 16)
                    sp.wait_ge(out_ready, n + 1)
                    sp.dma_start(out[n].rearrange("(t p) d -> p t d", p=P), y[:, s, :, :]).then_inc(stored[s], 16)
            for s in range(2):
                sp.wait_ge(loaded[s], 16 * (NB // 2 + 1))
                sp.wait_ge(stored[s], 16 * (NB // 2 + 1))

        @block.gpsimd
        def _(pool):
            norm.constants(pool)
            pool.wait_ge(consts, 112)
            with pool.Fori(0, NB // 2) as it:
                for s in range(2):
                    n = 2 * it + s
                    pool.wait_ge(xT_ps, n + 1)
                    pool.wait_ge(y_read, n + 1)
                    pool.tensor_tensor(xb[:, s, :, :], x[:, s, :, :],
                                       b2[:, :].unsqueeze(1).broadcast_to([P, NT, P]), ALU.add)\
                        .then_inc(xb_ready, 1)
                    norm.root(pool, n + 1)

        @block.tensor
        def _(pe):
            pe.wait_ge(consts, 112)
            with pe.Fori(0, NB // 2) as it:
                for s in range(2):
                    n = 2 * it + s
                    pe.wait_ge(loaded[s], 16 * (it + 1))
                    for t in range(NT):
                        last = pe.transpose(ps_xT[:, t * P:(t + 1) * P], x[:, s, t, :], ident[:, :])
                    last.then_inc(xT_ps, 1)
                    pe.wait_ge(xT_sb, n + 1)
                    pe.matmul(ps_pq[0:RANK, :], u1[:, :], xT[:, :], start=True, stop=True).then_inc(p_ps, 1)
                    pe.wait_ge(p_sb, n + 1)
                    for k in range(KF):
                        pe.matmul(ps_h[k][:, :], v1[:, k * P:(k + 1) * P], pT[:, :], start=True, stop=True)\
                            .then_inc(h_ps, 1)
                    for k in range(KF):
                        pe.wait_ge(h_sb, KF * n + k + 1)
                        last = pe.matmul(ps_pq[0:RANK, :], u2[:, k, :], hT[:, k, :], start=(k == 0),
                                         stop=(k == KF - 1))
                    last.then_inc(q_ps, 1)
                    pe.wait_ge(q_sb, n + 1)
                    pe.wait_ge(y_read, n + 2)
                    for t in range(NT):
                        last = pe.matmul(ps_y[:, t * P:(t + 1) * P], qT[:, t * P:(t + 1) * P], v2[:, :],
                                         start=True, stop=True)
                    last.then_inc(y_ps, 1)

        @block.scalar
        def _(act):
            act.wait_ge(consts, 112)
            with act.Fori(0, NB) as n:
                for k in range(KF):
                    act.wait_ge(h_ps, KF * n + k + 1)
                    act.activation(hT[:, k, :], ps_h[k][:, :], ACT.Gelu_apprx_tanh, bias=b1[:, k:k + 1])\
                        .then_inc(h_sb, 1)

        @block.vector
        def _(dve):
            dve.sem_inc(y_read, 2)
            with dve.Fori(0, NB // 2) as it:
                for s in range(2):
                    n = 2 * it + s
                    dve.wait_ge(xT_ps, n + 1)
                    dve.tensor_copy(xT[:, :], ps_xT[:, :]).then_inc(xT_sb, 1)
                    dve.wait_ge(p_ps, n + 1)
                    dve.tensor_copy(pT[:, :], ps_pq[0:RANK, :]).then_inc(p_sb, 1)
                    dve.wait_ge(q_ps, n + 1)
                    dve.tensor_copy(qT[:, :], ps_pq[0:RANK, :]).then_inc(q_sb, 1)
                    dve.wait_ge(y_ps, n + 1)
                    dve.wait_ge(xb_ready, n + 1)
                    dve.tensor_tensor(t1[:, :, :], ps_y[:, :].rearrange("p (t d) -> p t d", t=NT),
                                      xb[:, s, :, :], ALU.add).then_inc(y_read, 1)
                    dve.wait_ge(y_read, n + 3)
                    norm.moments(dve, t1, n + 1)
                    dve.wait_ge(stored[s], 16 * (it + 1))
                    norm.apply(dve, y[:, s, :, :], t1, n + 1).then_inc(out_ready, 1)


def phase_positions(nc, w_rT, r_in, stack_out):
    with ExitStack() as ctx:
        def sb(name, shape, dt=F32):
            return ctx.enter_context(nc.sbuf_tensor("p_" + name, shape, dt))

        sems = Semaphores(nc, ctx)

        def sem(name):
            return sems.new("p_" + name)

        w = sb("w", [P, P])
        r = sb("r", [P, 2, L])
        part = [sb(f"part{i}", [P, 2, L], BF16) for i in range(3)]
        rest = sb("rest", [P, 2, L])
        ps = ctx.enter_context(nc.psum_tensor("p_ps", [P, 2, L], F32))
        loaded = sem("loaded")
        done_ps = sem("done_ps")
        step = sem("step")
        stored = sem("stored")
        block = ctx.enter_context(nc.Block())

        @block.sync
        def _(sp):
            sp.dma_start(w[:, :], w_rT).then_inc(loaded, 16)
            sp.dma_start(r[:, :, :].rearrange("p a t -> p (a t)"), r_in).then_inc(loaded, 16)
            sp.wait_ge(step, 5)
            for t, which in enumerate(TERMS_K):
                sp.dma_start(stack_out[DH * t:DH * t + DH, :, :].rearrange("d h n -> h d n"),
                             part[which][:, :, :].rearrange("p a t -> p (a t)")).then_inc(stored, 16)
            sp.wait_ge(stored, 16 * len(TERMS_K))

        @block.tensor
        def _(pe):
            pe.wait_ge(loaded, 32)
            for a in range(2):
                last = pe.matmul(ps[:, a, :], w[:, :], r[:, a, :], start=True, stop=True)
            last.then_inc(done_ps, 1)

        @block.vector
        def _(dve):
            dve.wait_ge(done_ps, 1)
            dve.tensor_copy(part[0][:, :, :], ps[:, :, :]).then_inc(step, 1)
            dve.wait_ge(step, 1)
            dve.tensor_tensor(rest[:, :, :], ps[:, :, :], part[0][:, :, :], ALU.subtract).then_inc(step, 1)
            dve.wait_ge(step, 2)
            dve.tensor_copy(part[1][:, :, :], rest[:, :, :]).then_inc(step, 1)
            dve.wait_ge(step, 3)
            dve.tensor_tensor(rest[:, :, :], rest[:, :, :], part[1][:, :, :], ALU.subtract).then_inc(step, 1)
            dve.wait_ge(step, 4)
            dve.tensor_copy(part[2][:, :, :], rest[:, :, :]).then_inc(step, 1)


def phase_relative(nc, qu_stacks, qv_stacks, k_stacks, v9_in, r_stack, ident_in, ctx_out):
    SCALE = DH ** -0.5
    Q = 32
    W = L + Q
    TG = G * NT
    LOWEST = -3.0e38
    with ExitStack() as ctx:
        def sb(name, shape, dt=F32):
            return ctx.enter_context(nc.sbuf_tensor("r_" + name, shape, dt))

        sems = Semaphores(nc, ctx)

        def sem(name):
            return sems.new("r_" + name)

        def bank(name):
            return ctx.enter_context(nc.psum_tensor("r_" + name, [P, 512], F32))

        qu = sb("qu", [P, 2, G, L], BF16)
        qv = sb("qv", [P, 2, G, L + 2], BF16)
        k = sb("k", [P, 2, G, L], BF16)
        r = sb("r", [P, 2, G, 2 * L], BF16)
        v9 = sb("v9", [P, 2, NT, G * VW])
        ident = sb("ident", [P, P])
        wide = sb("wide", [P, 2, TG, W])
        shifted = sb("shifted", [P, 2, TG, L])
        scores = sb("scores", [P, 2, L])
        mx = sb("mx", [P, TG])
        probs = sb("probs", [P, 2, NT, L])
        osb = sb("osb", [P, G, P])
        ps_wide = [bank("ps_wide0"), bank("ps_wide1")]
        ps_tail = bank("ps_tail")
        ps_ac = [bank("ps_ac0"), bank("ps_ac1")]
        ps_keys = [bank("ps_keys0"), bank("ps_keys1")]
        ps_out = bank("ps_out")

        consts = sem("consts")
        pad_set = sem("pad_set")
        loaded = [sem("loaded0"), sem("loaded1")]
        pos_loaded = [sem("pos_loaded0"), sem("pos_loaded1")]
        wide_ps = sem("wide_ps")
        wide_sb = sem("wide_sb")
        tail_sb = sem("tail_sb")
        skewed = [sem("skewed0"), sem("skewed1")]
        shifted_used = sem("shifted_used")
        ac_ps = sem("ac_ps")
        ac_used = sem("ac_used")
        marks = sem("marks")
        s_ready = sem("scores_ready")
        keys_ps = sem("keys_ps")
        exp_done = sem("exp_done")
        head_done = sem("head_done")
        out_sb = sem("out_sb")
        stored = sem("stored")
        block = ctx.enter_context(nc.Block())
        SKEW = 16 * Q

        @block.sync
        def _(sp):
            def load(n, s):
                b, g = n // NG, n % NG
                for dst, src in ((qu, qu_stacks), (k, k_stacks)):
                    sp.dma_start(dst[0:SK, s, :, :], src.rearrange("b r (g h) t -> b g r h t", h=G)[b, g])\
                        .then_inc(loaded[s], 16)
                sp.dma_start(v9[:, s, :, :], v9_in.rearrange("b p t (g v) -> b g p t v", g=NG)[b, g])\
                    .then_inc(loaded[s], 16)

            def load_positions(n, s):
                b, g = n // NG, n % NG
                sp.dma_start(qv[0:SK, s, :, 0:L], qv_stacks.rearrange("b r (g h) t -> b g r h t", h=G)[b, g])\
                    .then_inc(pos_loaded[s], 16)
                sp.dma_start(r[0:SK, s, :, :], r_stack.rearrange("r (g h) t -> g r h t", h=G)[g])\
                    .then_inc(pos_loaded[s], 16)

            def skew(n, s):
                sp.wait_ge(wide_sb, TG * (n + 1))
                sp.wait_ge(tail_sb, n + 1)
                sp.wait_ge(shifted_used, n + 1)
                for i in range(Q):
                    sp.dma_start(shifted[i:i + 97:Q, s, :, :], wide[i:i + 97:Q, s, :, Q - 1 - i:Q - 1 - i + L])\
                        .then_inc(skewed[s], 16)

            sp.dma_start(ident[:, :], ident_in).then_inc(consts, 16)
            sp.wait_ge(pad_set, 4)
            for s in range(2):
                load_positions(s, s)
            for s in range(2):
                load(s, s)
            for s in range(2):
                sp.wait_ge(wide_ps, TG * (s + 1))
                load_positions(s + 2, s)
            sp.sem_inc(stored, 64)
            skew(0, 0)
            with sp.Fori(0, NI // 2) as it:
                for s in range(2):
                    n = 2 * it + s
                    skew(n + 1, 1 - s)
                    sp.wait_ge(wide_ps, TG * (n + 3))
                    load_positions((n + 4) % NI, s)
                    sp.wait_ge(head_done, G * (n + 1) + 2)
                    load((n + 2) % NI, s)
                    sp.wait_ge(out_sb, n + 2)
                    for b in range(NT):
                        sp.dma_start(ctx_out[n, :, :, b * P:(b + 1) * P].rearrange("h r i -> r h i"),
                                     osb[Q * b:Q * b + VW, :, :]).then_inc(stored, 16)
            for s in range(2):
                sp.wait_ge(loaded[s], 48 * (NI // 2 + 1))
                sp.wait_ge(pos_loaded[s], 32 * (NI // 2 + 2))
                sp.wait_ge(skewed[s], SKEW * (NI // 2 + 1 - s))
            sp.wait_ge(stored, 64 * (NI + 1))

        @block.tensor
        def _(pe):
            def wide_tile(n, s, u):
                h, b = u // NT, u % NT
                tile = TG * n + u
                ps = ps_wide[u % 2]
                if not isinstance(tile, int) or tile >= 2:
                    pe.wait_ge(wide_sb, tile - 1)
                if u == 0 and (not isinstance(n, int) or n):
                    pe.wait_ge(tail_sb, n)
                mains, tails = [], []
                for a in range(P // Q):
                    q0 = b * P + a * Q
                    low = (qv[:, s, h, q0:q0 + Q], a)
                    high = (qv[:, s, h, q0 + 1:q0 + 1 + Q], a)
                    n_low = min(q0 + Q + 1, L)
                    mains.append((low, 0, n_low, L - Q - q0))
                    if n_low < L:
                        mains.append((high, n_low, L, L + 1))
                    if q0 + Q + 1 <= L:
                        tails.append((high, 0, Q, 2 * L - Q - q0))
                    else:
                        tails.append((low, 0, 1, L))
                        tails.append((high, 1, Q, L + 1))
                for (lhs, a), lo, hi, at in mains:
                    pe.matmul(ps[Q * a:Q * a + Q, lo:hi], lhs, r[:, s, h, at:at + hi - lo], start=True, stop=True)
                for (lhs, a), lo, hi, at in tails:
                    last = pe.matmul(ps_tail[Q * a:Q * a + Q, Q * u + lo:Q * u + hi], lhs,
                                     r[:, s, h, at:at + hi - lo], start=True, stop=True)
                last.then_inc(wide_ps, 1)

            def content_tile(n, s, u):
                h, b = u // NT, u % NT
                pe.wait_ge(ac_used, TG * n + u + 1)
                pe.matmul(ps_ac[u % 2][:, :], qu[:, s, h, b * P:(b + 1) * P], k[:, s, h, :], start=True, stop=True)\
                    .then_inc(ac_ps, 1)

            def turn_tile(n, u):
                pe.wait_ge(s_ready, TG * n + u + 1)
                pe.wait_ge(exp_done, TG * n + u + 1)
                for j in range(NT):
                    last = pe.transpose(ps_keys[u % 2][:, j * P:(j + 1) * P],
                                        scores[:, u % 2, j * P:(j + 1) * P], ident[:, :])
                last.then_inc(keys_ps, 1)

            def value_head(n, s, h):
                pe.wait_ge(exp_done, TG * n + NT * (h + 1) + 2)
                if h == 0:
                    pe.wait_ge(out_sb, n + 1)
                for j in range(NT):
                    for b in range(NT):
                        last = pe.matmul(ps_out[Q * b:Q * b + VW, h * P:(h + 1) * P],
                                         v9[:, s, j, h * VW:(h + 1) * VW], probs[:, h % 2, j, b * P:(b + 1) * P],
                                         start=(j == 0), stop=(j == NT - 1), skip_group_check=True)
                last.then_inc(head_done, 1)

            pe.wait_ge(consts, 16)
            pe.sem_inc(keys_ps, 2)
            for j in range(NT):
                last = pe.transpose(ps_out[:, j * P:(j + 1) * P], ident[:, :], ident[:, :])
            for n in range(2):
                pe.wait_ge(pos_loaded[n], 32)
                for u in range(TG):
                    wide_tile(n, n, u)
            pe.wait_ge(loaded[0], 48)
            content_tile(0, 0, 0)
            content_tile(0, 0, 1)
            with pe.Fori(0, NI // 2) as it:
                for s in range(2):
                    n = 2 * it + s
                    pe.wait_ge(pos_loaded[s], 32 * (it + 2))
                    for u in range(TG):
                        if u + 2 < TG:
                            content_tile(n, s, u + 2)
                        else:
                            if u + 2 == TG:
                                pe.wait_ge(loaded[1 - s], 48 * (it + 1 + s))
                            content_tile(n + 1, 1 - s, u + 2 - TG)
                        turn_tile(n, u)
                        wide_tile(n + 2, s, u)
                        if u >= NT and u % NT == 0:
                            value_head(n, s, u // NT - 1)
                    value_head(n, s, G - 1)

        @block.scalar
        def _(act):
            def copy_wide(n, s, u):
                act.wait_ge(wide_ps, TG * n + u + 1)
                act.activation(wide[:, s, u, 0:L], ps_wide[u % 2][:, :], ACT.Copy).then_inc(wide_sb, 1)

            def copy_tail(s):
                act.activation(wide[:, s, :, L:W], ps_tail[:, :].rearrange("p (u w) -> p u w", w=Q), ACT.Copy)\
                    .then_inc(tail_sb, 1)

            act.sem_inc(exp_done, 2)
            act.sem_inc(out_sb, 1)
            for n in range(2):
                for u in range(TG):
                    copy_wide(n, n, u)
                copy_tail(n)
            with act.Fori(0, NI // 2) as it:
                for s in range(2):
                    n = 2 * it + s
                    act.wait_ge(skewed[s], SKEW * (it + 1))
                    for u in range(TG):
                        h, b = u // NT, u % NT
                        if b == 0:
                            act.wait_ge(head_done, G * n + h + 1)
                        act.wait_ge(keys_ps, TG * n + u + 3)
                        act.activation(probs[:, h % 2, :, b * P:(b + 1) * P],
                                       ps_keys[u % 2][:, :].rearrange("p (j i) -> p j i", j=NT), ACT.Exp,
                                       scale=SCALE).then_inc(exp_done, 1)
                        copy_wide(n + 2, s, u)
                    copy_tail(s)
                    act.wait_ge(head_done, G * (n + 1) + 2)
                    act.wait_ge(stored, 64 * (n + 1))
                    act.activation(osb[:, :, :].rearrange("p h i -> p (h i)"), ps_out[:, :], ACT.Copy)\
                        .then_inc(out_sb, 1)

        @block.vector
        def _(dve):
            for stack in (qv, r, qu, k):
                dve.memset(stack[:, :, :, :].rearrange("p s h t -> p (s h t)").bitcast(F32), 0.0)\
                    .then_inc(pad_set, 1)
            dve.sem_inc(head_done, 2)
            dve.sem_inc(ac_used, 2)
            dve.sem_inc(shifted_used, 2)
            with dve.Fori(0, NI // 2) as it:
                for s in range(2):
                    n = 2 * it + s
                    dve.wait_ge(skewed[s], SKEW * (it + 1))
                    for u in range(TG):
                        dve.wait_ge(ac_ps, TG * n + u + 1)
                        dve.wait_ge(keys_ps, TG * n + u + 1)
                        dve.sem_inc(marks, 1)
                        dve.tensor_tensor_reduce(out=scores[:, u % 2, :], in0=ps_ac[u % 2][:, :],
                                                 in1=shifted[:, s, u, :], scale=1.0, scalar=LOWEST,
                                                 op0=ALU.add, op1=ALU.max, accum_out=mx[:, u:u + 1])\
                            .then_inc(ac_used, 1)
                        dve.wait_ge(ac_used, TG * n + u + 3)
                        dve.tensor_scalar(scores[:, u % 2, :], scores[:, u % 2, :], mx[:, u:u + 1], None,
                                          ALU.subtract).then_inc(s_ready, 1)
                    dve.sem_inc(shifted_used, 1)


def program(nc, x, w_qkvT, w_fcT, b_fc, gamma, beta, ln1_scale, ln1_shift, wq, wk, wv, wo, bo, ln2_scale,
            ln2_shift, gate_w, w1, w2, w3, rel_wqT, rel_wkT, rel_wvT, rel_wrT, u_bias, v_bias, u1, v1, b1, u2,
            v2, b2, ident, mask, maskT, iota, positions, out):
    def dram(name, shape, dt=F32):
        return nc.dram_tensor(name, shape, dt, kind="Internal").ap()

    tokens = (NB, P, NT, P)
    x1, z1, base, z2, x2, x3 = (dram(name, tokens) for name in ("x1", "z1", "base", "z2", "x2", "x3"))
    stacks = [dram(f"stack{i}", (NB, SK, H, L), BF16) for i in range(5)]
    v9 = [dram(f"v9_{i}", (NB, P, NT, H * VW)) for i in range(2)]
    sums = [dram(f"sums{i}", (NI, G, VW, L)) for i in range(2)]
    r_stack = dram("r_stack", (SK, H, 2 * L), BF16)

    phase_attention(nc, x, w_qkvT, w_fcT, b_fc, gamma, beta, ident, x1, z1)
    phase_project(nc, z1, ln1_scale, ln1_shift, [wq, wk, wv], [None, None], [TERMS_Q, TERMS_K], ident,
                  stacks[0:2], v9[0], "b")
    phase_causal(nc, stacks[0], stacks[1], v9[0], mask, maskT, ident, sums[0])
    phase_merge(nc, sums[0], x1, wo, bo, base, z2, "m")
    phase_experts(nc, z2, base, ln2_scale, ln2_shift, gate_w, w1, w2, w3, iota, ident, x2)
    phase_positions(nc, rel_wrT, positions, r_stack)
    phase_project(nc, x2, None, None, [rel_wqT, rel_wqT, rel_wkT, rel_wvT], [u_bias, v_bias, None],
                  [TERMS_Q, TERMS_Q, TERMS_K], ident, stacks[2:5], v9[1], "d")
    phase_relative(nc, stacks[2], stacks[3], stacks[4], v9[1], r_stack, ident, sums[1])
    phase_merge(nc, sums[1], x2, ident, None, None, x3, "n")
    phase_last(nc, x3, u1, v1, b1, u2, v2, b2, ident, out)


_PLAIN = ("L0_attn_x", "L0_attn_b_fc", "L0_attn_gamma", "L0_attn_beta", "L0_ffn_ln1_scale", "L0_ffn_ln1_shift",
          "L0_ffn_wq", "L0_ffn_wk", "L0_ffn_wv", "L0_ffn_wo", "L0_ffn_bo", "L0_ffn_ln2_scale",
          "L0_ffn_ln2_shift", "L0_ffn_gate_w", "L0_ffn_w1", "L0_ffn_w2", "L0_ffn_w3", "L1_ffn_U1", "L1_ffn_V1",
          "L1_ffn_U2", "L1_ffn_V2", "L1_ffn_b2")
_TURNED = ("L0_attn_w_qkv", "L0_attn_w_fc", "L1_attn_Wq", "L1_attn_Wk", "L1_attn_Wv", "L1_attn_Wr")
_FLAT = ("L1_attn_u_bias", "L1_attn_v_bias")
_ORDER = ("L0_attn_x", "L0_attn_w_qkv", "L0_attn_w_fc", "L0_attn_b_fc", "L0_attn_gamma", "L0_attn_beta",
          "L0_ffn_ln1_scale", "L0_ffn_ln1_shift", "L0_ffn_wq", "L0_ffn_wk", "L0_ffn_wv", "L0_ffn_wo",
          "L0_ffn_bo", "L0_ffn_ln2_scale", "L0_ffn_ln2_shift", "L0_ffn_gate_w", "L0_ffn_w1", "L0_ffn_w2",
          "L0_ffn_w3", "L1_attn_Wq", "L1_attn_Wk", "L1_attn_Wv", "L1_attn_Wr", "L1_attn_u_bias",
          "L1_attn_v_bias", "L1_ffn_U1", "L1_ffn_V1", "L1_ffn_b1", "L1_ffn_U2", "L1_ffn_V2", "L1_ffn_b2",
          "ident", "mask", "maskT", "iota", "positions")


def constants():
    import numpy as np

    i = np.arange(P)
    mask = np.where(i[None, :] > i[:, None], np.float32(BIG), np.float32(0))
    freq = (np.float32(1) / np.float32(10000) ** (np.arange(0, P, 2, dtype=np.float32) / np.float32(P)))
    angle = np.arange(-(L - 1), L, dtype=np.float32)[:, None] * freq.astype(np.float32)[None, :]
    r = np.zeros((2 * L - 1, P), np.float32)
    r[:, 0::2] = np.sin(angle)
    r[:, 1::2] = np.cos(angle)
    rows = np.zeros((2 * L, P), np.float32)
    rows[0:L] = r[L - 1:]
    rows[L + 1:] = r[:L - 1]
    return {"ident": np.eye(P, dtype=np.float32), "mask": mask, "maskT": np.ascontiguousarray(mask.T),
            "iota": np.arange(NE, dtype=np.float32), "positions": np.ascontiguousarray(rows.T)}


def kernel(**inputs):
    import numpy as _np
    import concourse.bacc as _bacc
    from concourse import mybir as _mybir
    from concourse.bass_utils import run_bass_kernel_spmd as _run

    laid = dict(constants())
    for name in _PLAIN:
        laid[name] = _np.ascontiguousarray(inputs[name])
    for name in _TURNED:
        laid[name] = _np.ascontiguousarray(_np.asarray(inputs[name]).T)
    for name in _FLAT:
        laid[name] = _np.ascontiguousarray(inputs[name]).reshape(P)
    laid["L1_ffn_b1"] = _np.ascontiguousarray(_np.asarray(inputs["L1_ffn_b1"]).reshape(FF // P, P).T)

    nc = _bacc.Bacc("TRN2", target_bir_lowering=False, num_devices=1)
    arrays, args = {}, []
    for name in _ORDER:
        a = laid[name]
        arrays[f"in_{name}_dram"] = a
        args.append(nc.dram_tensor(f"in_{name}_dram", a.shape, _mybir.dt.from_np(a.dtype),
                                   kind="ExternalInput").ap())
    args.append(nc.dram_tensor("out_0_dram", (NB, L, P), F32, kind="ExternalOutput").ap())
    program(nc, *args)
    r = _run(nc, [arrays], core_ids=[0])
    return r.results[0]["out_0_dram"]
```

```python
from contextlib import ExitStack

import concourse.bass as bass
from concourse import mybir

F32 = mybir.dt.float32
BF16 = mybir.dt.bfloat16
U32 = mybir.dt.uint32
ACT = mybir.ActivationFunctionType
ALU = mybir.AluOpType
AX_X = mybir.AxisListType.X

P = 128
NB = 8
L = 512
NT = L // P
H = 16
DH = 8
G = 4
NG = H // G
NI = NB * NG
VW = DH + 1
TERMS_Q = (0, 0, 0, 1, 1, 2)
TERMS_K = (0, 1, 2, 0, 1, 0)
SK = DH * len(TERMS_Q)
NE = 8
HID = 256
FF = 512
RANK = 32
EPS = 1e-5
HW = 16
BIG = -1e30


class Chain:

    def __init__(self, eng, sem, n, per):
        self.eng, self.sem, self.n, self.per, self.k = eng, sem, n, per, 0

    def step(self, ins):
        self.k += 1
        ins.then_inc(self.sem, 1)
        self.eng.wait_ge(self.sem, self.n * self.per + self.k)

    def done(self):
        assert self.k == self.per, (self.k, self.per)


class Semaphores:

    def __init__(self, nc, ctx):
        self.nc, self.all = nc, []
        ctx.callback(self.clear)

    def new(self, name):
        self.all.append(self.nc.alloc_semaphore(name))
        return self.all[-1]

    def clear(self):
        self.nc.clear_and_free_semaphores(self.all)
        self.nc.all_engine_barrier()


def row_on_all(v, width=P):
    return bass.AP(tensor=v.tensor, offset=v.offset, ap=[[0, P], [1, width]])


class Norm:

    def __init__(self, ctx, nc, sems, name):
        self.stats = ctx.enter_context(nc.sbuf_tensor(name + "_stats", [P, NT, 6], F32))
        self.mv = ctx.enter_context(nc.sbuf_tensor(name + "_mv", [P, NT, 2], F32))
        self.rstd = ctx.enter_context(nc.sbuf_tensor(name + "_rstd", [P, NT], F32))
        self.var_eps = ctx.enter_context(nc.sbuf_tensor(name + "_var_eps", [P, NT], F32))
        self.consts = ctx.enter_context(nc.sbuf_tensor(name + "_consts", [P, 2, NT], F32))
        self.consts_set = sems.new(name + "_consts_set")
        self.eps_added = sems.new(name + "_eps_added")
        self.passes = sems.new(name + "_passes")
        self.stats_ready = sems.new(name + "_stats_ready")
        self.var_ready = sems.new(name + "_var_ready")
        self.rstd_ready = sems.new(name + "_rstd_ready")

    def moments(self, dve, x, count):
        for t in range(NT):
            last = dve.bn_stats(self.stats[:, t, :], x[:, t, :])
        last.then_inc(self.stats_ready, 1)
        dve.wait_ge(self.stats_ready, count)
        dve.sem_inc(self.passes, 1)
        for t in range(NT):
            last = dve.bn_aggr(self.mv[:, t, :], self.stats[:, t, :])
        last.then_inc(self.var_ready, 1)

    def root(self, pool, count):
        pool.wait_ge(self.var_ready, count)
        pool.tensor_tensor(self.var_eps[:, :], self.mv[:, :, 1], self.consts[:, 0, :], ALU.add)\
            .then_inc(self.eps_added, 1)
        pool.wait_ge(self.eps_added, count)
        pool.tensor_tensor(self.rstd[:, :], self.var_eps[:, :], self.consts[:, 1, :], ALU.pow)\
            .then_inc(self.rstd_ready, 1)

    def constants(self, pool):
        pool.memset(self.consts[:, 0, :], EPS).then_inc(self.consts_set, 1)
        pool.memset(self.consts[:, 1, :], -0.5).then_inc(self.consts_set, 1)
        pool.wait_ge(self.consts_set, 2)

    def apply(self, dve, out, x, count):
        dve.wait_ge(self.rstd_ready, count)
        for t in range(NT):
            last = dve.tensor_scalar(out[:, t, :], x[:, t, :], self.mv[:, t, 0:1], self.rstd[:, t:t + 1],
                                     ALU.subtract, ALU.mult)
        return last


def phase_attention(nc, x_in, w_qkvT, w_fcT, b_fc, gamma, beta, ident_in, x1_out, z1_out):
    SCALE = P ** -0.5
    with ExitStack() as ctx:
        def sb(name, shape, dt=F32):
            return ctx.enter_context(nc.sbuf_tensor("a_" + name, shape, dt))

        sems = Semaphores(nc, ctx)

        def sem(name):
            return sems.new("a_" + name)

        wqkv = sb("wqkv", [P, 3, P])
        wfc = sb("wfc", [P, P])
        ident = sb("ident", [P, P])
        bfc = sb("bfc", [P, P])
        gam = sb("gam", [P, P])
        bet = sb("bet", [P, P])
        x = sb("x", [P, 2, NT, P])
        xb = sb("xb", [P, 2, NT, P])
        xbeta = sb("xbeta", [P, 2, NT, P])
        xT = sb("xT", [P, L])
        qT = sb("qT", [P, 2, L])
        kT = sb("kT", [P, 2, L])
        xsum = sb("xsum", [P, 2])
        vsum = sb("vsum", [P, P])
        mx = sb("mx", [P, NT])
        negm = sb("negm", [P, NT])
        rowsum = sb("rowsum", [P, NT])
        rinv = sb("rinv", [P, NT])
        attsum = sb("attsum", [P, 2, NT])
        probs = sb("probs", [P, 2, NT, L])
        att = sb("att", [P, 2, L])
        h = sb("h", [P, NT, P])
        h2 = sb("h2", [P, NT, P])
        x1 = sb("x1", [P, 2, NT, P])
        z1 = sb("z1", [P, 2, NT, P])
        norm = Norm(ctx, nc, sems, "a_norm")
        ps = [ctx.enter_context(nc.psum_tensor(f"a_ps{i}", [P, 512], F32)) for i in range(8)]

        consts = sem("consts")
        x_in_s = [sem("x_loaded0"), sem("x_loaded1")]
        x_free = sem("x_free")
        xb_ready = sem("xb_ready")
        xT_ps = sem("xT_ps")
        xT_sb = sem("xT_sb")
        qk_ps = sem("qk_ps")
        v_ps = sem("v_ps")
        q_sb = sem("q_sb")
        k_sb = sem("k_sb")
        vsum_sb = sem("vsum_sb")
        s_ps = sem("scores_ps")
        negm_ready = sem("negm_ready")
        p_sb = sem("probs_sb")
        rinv_ready = sem("rinv_ready")
        att_done = sem("att_done")
        fc_ps = sem("fc_ps")
        fc_read = sem("fc_read")
        chain_s = sem("dve_chain")
        max_ready = sem("max_ready")
        marks = sem("marks")
        x1_ready = sem("x1_ready")
        z1_ready = sem("z1_ready")
        stored = [sem("stored0"), sem("stored1")]
        block = ctx.enter_context(nc.Block())

        def steps(step, eng):
            with eng.Fori(0, NB // 2 - 1) as it:
                for s in range(2):
                    step(it, s, True)
            for s in range(2):
                step(NB // 2 - 1, s, s == 0)

        @block.sync
        def _(sp):
            sp.dma_start(wqkv[:, :, :], w_qkvT.rearrange("d (c e) -> d c e", c=3)).then_inc(consts, 16)
            sp.dma_start(wfc[:, :], w_fcT).then_inc(consts, 16)
            sp.dma_start(ident[:, :], ident_in).then_inc(consts, 16)
            sp.dma_start(bfc[:, :], row_on_all(b_fc)).then_inc(consts, 16)
            sp.dma_start(gam[:, :], row_on_all(gamma)).then_inc(consts, 16)
            sp.dma_start(bet[:, :], row_on_all(beta)).then_inc(consts, 16)
            for s in range(2):
                sp.dma_start(x[:, s, :, :], x_in[s].rearrange("(t p) d -> p t d", p=P)).then_inc(x_in_s[s], 16)
            for s in range(2):
                sp.sem_inc(stored[s], 32)
            with sp.Fori(0, NB // 2) as it:
                for s in range(2):
                    n = 2 * it + s
                    sp.wait_ge(x_free, n + 1)
                    sp.dma_start(x[:, s, :, :], x_in[(n + 2) % NB].rearrange("(t p) d -> p t d", p=P))\
                        .then_inc(x_in_s[s], 16)
                    sp.wait_ge(x1_ready, n + 1)
                    sp.dma_start(x1_out[n], x1[:, s, :, :]).then_inc(stored[s], 16)
                    sp.wait_ge(z1_ready, n + 1)
                    sp.dma_start(z1_out[n], z1[:, s, :, :]).then_inc(stored[s], 16)
            for s in range(2):
                sp.wait_ge(stored[s], 32 * (NB // 2 + 1))
                sp.wait_ge(x_in_s[s], 16 * (NB // 2 + 1))

        @block.gpsimd
        def _(pool):
            def add_bfc(n, s, loads):
                pool.wait_ge(x_in_s[s], 16 * loads)
                pool.tensor_tensor(xb[:, s, :, :], x[:, s, :, :], bfc[:, :].unsqueeze(1).broadcast_to([P, NT, P]),
                                   ALU.add).then_inc(xb_ready, 1)

            def add_beta(n, s):
                pool.wait_ge(xT_ps, n + 1)
                pool.tensor_tensor(xbeta[:, s, :, :], x[:, s, :, :],
                                   bet[:, :].unsqueeze(1).broadcast_to([P, NT, P]), ALU.add).then_inc(x_free, 1)

            def step(it, s, ahead):
                n = 2 * it + s
                norm.root(pool, 3 * n + 1)
                if ahead:
                    add_bfc(n + 1, 1 - s, it + 1 + s)
                norm.root(pool, 3 * n + 2)
                norm.root(pool, 3 * n + 3)
                if ahead:
                    add_beta(n + 1, 1 - s)

            norm.constants(pool)
            pool.wait_ge(consts, 96)
            add_bfc(0, 0, 1)
            add_beta(0, 0)
            steps(step, pool)

        @block.tensor
        def _(pe):
            def front(n, s, loads):
                pe.wait_ge(x_in_s[s], 16 * loads)
                for t in range(NT):
                    last = pe.transpose(ps[0][:, t * P:(t + 1) * P], x[:, s, t, :], ident[:, :])
                last.then_inc(xT_ps, 1)
                pe.wait_ge(xT_sb, n + 1)
                pe.matmul(ps[1][:, :], wqkv[:, 0, :], xT[:, :], start=True, stop=True).then_inc(qk_ps, 1)
                pe.matmul(ps[2][:, :], wqkv[:, 1, :], xT[:, :], start=True, stop=True).then_inc(qk_ps, 1)

            def step(it, s, ahead):
                n = 2 * it + s
                pe.wait_ge(q_sb, n + 1)
                pe.wait_ge(k_sb, n + 1)
                for i in range(NT):
                    pe.wait_ge(p_sb, NT * n + i + 1)
                    pe.matmul(ps[4 + i][:, :], qT[:, s, i * P:(i + 1) * P], kT[:, s, :], start=True, stop=True)\
                        .then_inc(s_ps, 1)
                if ahead:
                    front(n + 1, 1 - s, it + 1 + s)
                pe.wait_ge(fc_read, n + 1)
                pe.matmul(ps[3][:, 0:1], wqkv[:, 2, :], xsum[:, s:s + 1], start=True, stop=True).then_inc(v_ps, 1)
                pe.wait_ge(vsum_sb, n + 1)
                pe.matmul(ps[3][:, P:2 * P], vsum[:, :], wfc[:, :], start=True, stop=True).then_inc(fc_ps, 1)

            pe.wait_ge(consts, 96)
            front(0, 0, 1)
            steps(step, pe)

        @block.scalar
        def _(act):
            def front(n, s):
                act.wait_ge(xT_ps, n + 1)
                act.activation(xT[:, :], ps[0][:, :], ACT.Copy, accum_out=xsum[:, s:s + 1]).then_inc(xT_sb, 1)
                act.wait_ge(qk_ps, 2 * n + 1)
                act.activation(qT[:, s, :], ps[1][:, :], ACT.Copy).then_inc(q_sb, 1)
                act.wait_ge(qk_ps, 2 * n + 2)
                act.activation(kT[:, s, :], ps[2][:, :], ACT.Copy).then_inc(k_sb, 1)

            def step(it, s, ahead):
                n = 2 * it + s
                for i in range(NT):
                    act.wait_ge(negm_ready, NT * n + i + 1)
                    act.activation(probs[:, s, i, :], ps[4 + i][:, :], ACT.Exp, bias=negm[:, i:i + 1],
                                   scale=SCALE, accum_out=rowsum[:, i:i + 1]).then_inc(p_sb, 1)
                if ahead:
                    front(n + 1, 1 - s)
                act.wait_ge(v_ps, n + 1)
                act.activation(vsum[:, :], ps[3][:, 0:1].broadcast_to([P, P]), ACT.Copy).then_inc(vsum_sb, 1)
                act.wait_ge(rinv_ready, n + 1)
                for i in range(NT):
                    act.wait_ge(att_done, NT * n + i + 1)
                    act.activation(att[:, i % 2, :], probs[:, s, i, :], ACT.Copy, scale=rinv[:, i:i + 1],
                                   accum_out=attsum[:, s, i:i + 1]).then_inc(att_done, 1)

            act.sem_inc(p_sb, NT)
            act.sem_inc(att_done, 2)
            front(0, 0)
            steps(step, act)

        @block.vector
        def _(dve):
            def maxima(n, i):
                dve.wait_ge(s_ps, NT * n + i + 1)
                dve.tensor_reduce(mx[:, i:i + 1], ps[4 + i][:, :], AX_X, ALU.max).then_inc(max_ready, 1)
                dve.wait_ge(max_ready, NT * n + i + 1)
                dve.tensor_scalar(negm[:, i:i + 1], mx[:, i:i + 1], -SCALE, None, ALU.mult)\
                    .then_inc(negm_ready, 1)

            def sequence(it, s, ahead):
                n = 2 * it + s
                chain = Chain(dve, chain_s, n, 4)
                dve.wait_ge(p_sb, NT * (n + 2))
                dve.reciprocal(rinv[:, :], rowsum[:, :]).then_inc(rinv_ready, 1)
                if ahead:
                    maxima(n + 1, 0)
                    maxima(n + 1, 1)
                dve.wait_ge(fc_ps, n + 1)
                dve.wait_ge(xb_ready, n + 1)
                dve.sem_inc(marks, 1)
                dve.wait_ge(att_done, NT * (n + 1) + 2)
                for t in range(NT):
                    last = dve.scalar_tensor_tensor(out=h[:, t, :], in0=ps[3][:, P:2 * P],
                                                    scalar=attsum[:, s, t:t + 1], in1=xb[:, s, t, :],
                                                    op0=ALU.mult, op1=ALU.add)
                chain.step(last)
                dve.sem_inc(fc_read, 1)
                norm.moments(dve, h, 3 * n + 1)
                if ahead:
                    maxima(n + 1, 2)
                chain.step(norm.apply(dve, h2, h, 3 * n + 1))
                gm = gam[:, :].unsqueeze(1).broadcast_to([P, NT, P])
                chain.step(dve.tensor_tensor(h[:, :, :], h2[:, :, :], gm, ALU.mult))
                dve.wait_ge(x_free, n + 1)
                chain.step(dve.tensor_tensor(h2[:, :, :], h[:, :, :], xbeta[:, s, :, :], ALU.add))
                norm.moments(dve, h2, 3 * n + 2)
                if ahead:
                    maxima(n + 1, 3)
                dve.wait_ge(stored[s], 32 * it + 32)
                norm.apply(dve, x1[:, s, :, :], h2, 3 * n + 2).then_inc(x1_ready, 1)
                dve.wait_ge(x1_ready, n + 1)
                norm.moments(dve, x1[:, s, :, :], 3 * n + 3)
                norm.apply(dve, z1[:, s, :, :], x1[:, s, :, :], 3 * n + 3).then_inc(z1_ready, 1)
                chain.done()

            dve.sem_inc(fc_read, 1)
            dve.wait_ge(consts, 96)
            for i in range(NT):
                maxima(0, i)
            steps(sequence, dve)


def phase_project(nc, z_in, scale, shift, w_in, biases, tables, ident_in, stacks_out, v9_out, name):
    NC = len(w_in) - 1
    with ExitStack() as ctx:
        def sb(nm, shape, dt=F32):
            return ctx.enter_context(nc.sbuf_tensor(f"{name}_{nm}", shape, dt))

        sems = Semaphores(nc, ctx)

        def sem(nm):
            return sems.new(f"{name}_{nm}")

        w = sb("w", [P, NC + 1, P])
        sc = sb("scale", [P, 2])
        bias = sb("bias", [P, NC])
        ident = sb("ident", [P, P])
        z = sb("z", [P, 2, NT, P])
        zT = sb("zT", [P, L])
        part1 = sb("part1", [P, 2, NC, L], BF16)
        part2 = sb("part2", [P, 2, NC, L], BF16)
        part3 = sb("part3", [P, 2, NC, L], BF16)
        rest1 = sb("rest1", [P, NC, L])
        v9 = sb("v9", [P, 2, NT, H * VW])
        ps_zT = ctx.enter_context(nc.psum_tensor(f"{name}_ps_zT", [P, L], F32))
        ps_c = [ctx.enter_context(nc.psum_tensor(f"{name}_ps_c{c}", [P, L], F32)) for c in range(NC)]
        ps_v = ctx.enter_context(nc.psum_tensor(f"{name}_ps_v", [P, NT * P], F32))

        consts = sem("consts")
        z_loaded = [sem("z_loaded0"), sem("z_loaded1")]
        zT_ps = sem("zT_ps")
        zT_sb = sem("zT_sb")
        c_ps = sem("operands_ps")
        v_ps = sem("v_ps")
        v_sb = sem("v_sb")
        ones_set = sem("ones_set")
        part1_ready = sem("part1_ready")
        rest1_ready = sem("rest1_ready")
        part2_ready = sem("part2_ready")
        part3_ready = sem("part3_ready")
        stored = [sem("stored0"), sem("stored1")]
        pool_stored = sem("pool_stored")
        pool_slots = sem("pool_slots")
        v_stored = [sem("v_stored0"), sem("v_stored1")]
        n_const = 16 * (NC + 2 + (2 if scale is not None else 0) + sum(b is not None for b in biases))
        n_set = 1 + sum(b is None for b in biases)
        NSP = NC - 1
        STORES = 16 * len(TERMS_Q) * NSP
        POOL_STORES = 16 * len(TERMS_Q)
        block = ctx.enter_context(nc.Block())

        def term_stores(eng, n, s, c, signal):
            parts = (part1, part2, part3)
            for t, which in enumerate(tables[c]):
                dst = stacks_out[c][n, DH * t:DH * t + DH, :, :].rearrange("d h n -> h d n")
                eng.dma_start(dst, parts[which][:, s, c, :]).then_inc(signal, 16)

        @block.sync
        def _(sp):
            for c in range(NC + 1):
                sp.dma_start(w[:, c, :], w_in[c]).then_inc(consts, 16)
            sp.dma_start(ident[:, :], ident_in).then_inc(consts, 16)
            if scale is not None:
                sp.dma_start(sc[:, 0:1], scale.rearrange("(d o) -> d o", o=1)).then_inc(consts, 16)
                sp.dma_start(sc[:, 1:2], shift.rearrange("(d o) -> d o", o=1)).then_inc(consts, 16)
            for c in range(NC):
                if biases[c] is not None:
                    sp.dma_start(bias[:, c:c + 1], biases[c].rearrange("(d o) -> d o", o=1)).then_inc(consts, 16)
            for s in range(2):
                sp.dma_start(z[:, s, :, :], z_in[s]).then_inc(z_loaded[s], 16)
                sp.sem_inc(stored[s], STORES)
                sp.sem_inc(v_stored[s], 16)
            with sp.Fori(0, NB // 2) as it:
                for s in range(2):
                    n = 2 * it + s
                    sp.wait_ge(zT_ps, n + 1)
                    sp.dma_start(z[:, s, :, :], z_in[(n + 2) % NB]).then_inc(z_loaded[s], 16)
                    sp.wait_ge(v_sb, n + 1)
                    sp.dma_start(v9_out[n], v9[:, s, :, :]).then_inc(v_stored[s], 16)
                    for c in range(NSP):
                        sp.wait_ge(part3_ready, NC * (n + 1) + c + 1)
                        term_stores(sp, n, s, c, stored[s])
            for s in range(2):
                sp.wait_ge(stored[s], STORES * (NB // 2 + 1))
                sp.wait_ge(v_stored[s], 16 * (NB // 2 + 1))
                sp.wait_ge(z_loaded[s], 16 * (NB // 2 + 1))

        @block.gpsimd
        def _(pool):
            for c in range(NC):
                if biases[c] is None:
                    pool.memset(bias[:, c:c + 1], 0.0).then_inc(ones_set, 1)
            pool.memset(v9[:, :, :, :], 1.0).then_inc(ones_set, 1)
            pool.sem_inc(pool_slots, 2)
            with pool.Fori(0, NB // 2) as it:
                for s in range(2):
                    n = 2 * it + s
                    pool.wait_ge(part3_ready, NC * (n + 2))
                    term_stores(pool, n, s, NC - 1, pool_stored)
                    pool.wait_ge(pool_stored, POOL_STORES * (n + 1))
                    pool.sem_inc(pool_slots, 1)

        @block.tensor
        def _(pe):
            pe.wait_ge(consts, n_const)
            with pe.Fori(0, NB // 2) as it:
                for s in range(2):
                    n = 2 * it + s
                    pe.wait_ge(z_loaded[s], 16 * it + 16)
                    for t in range(NT):
                        last = pe.transpose(ps_zT[:, t * P:(t + 1) * P], z[:, s, t, :], ident[:, :])
                    last.then_inc(zT_ps, 1)
                    pe.wait_ge(zT_sb, n + 1)
                    for c in range(NC):
                        pe.wait_ge(rest1_ready, NC * n + c + 1)
                        pe.matmul(ps_c[c][:, :], w[:, c, :], zT[:, :], start=True, stop=True).then_inc(c_ps, 1)
                    for t in range(NT):
                        last = pe.matmul(ps_v[:, t * P:(t + 1) * P], zT[:, t * P:(t + 1) * P], w[:, NC, :],
                                         start=True, stop=True)
                    last.then_inc(v_ps, 1)

        @block.scalar
        def _(act):
            act.wait_ge(consts, n_const)
            act.wait_ge(ones_set, n_set)
            with act.Fori(0, NB // 2) as it:
                for s in range(2):
                    n = 2 * it + s
                    act.wait_ge(zT_ps, n + 1)
                    if scale is not None:
                        act.activation(zT[:, :], ps_zT[:, :], ACT.Identity, bias=sc[:, 1:2], scale=sc[:, 0:1])\
                            .then_inc(zT_sb, 1)
                    else:
                        act.activation(zT[:, :], ps_zT[:, :], ACT.Copy).then_inc(zT_sb, 1)
                    act.wait_ge(stored[s], STORES * (it + 1))
                    act.wait_ge(pool_slots, n + 1)
                    for c in range(NC):
                        act.wait_ge(c_ps, NC * n + c + 1)
                        act.activation(part1[:, s, c, :], ps_c[c][:, :], ACT.Identity, bias=bias[:, c:c + 1])\
                            .then_inc(part1_ready, 1)
                    act.wait_ge(v_ps, n + 1)
                    act.wait_ge(v_stored[s], 16 * (it + 1))
                    act.activation(v9[:, s, :, :].rearrange("p t (h v) -> p (t h) v", v=VW)[:, :, 0:DH],
                                   ps_v[:, :].rearrange("p (g d) -> p g d", d=DH), ACT.Copy).then_inc(v_sb, 1)
                    for c in range(NC):
                        act.wait_ge(rest1_ready, NC * (n + 1) + c + 1)
                        act.activation(part2[:, s, c, :], rest1[:, c, :], ACT.Copy).then_inc(part2_ready, 1)

        @block.vector
        def _(dve):
            dve.sem_inc(rest1_ready, NC)
            dve.sem_inc(part3_ready, NC)
            dve.wait_ge(consts, n_const)
            dve.wait_ge(ones_set, n_set)
            with dve.Fori(0, NB // 2) as it:
                for s in range(2):
                    n = 2 * it + s
                    dve.wait_ge(part3_ready, NC * (n + 1))
                    for c in range(NC):
                        dve.wait_ge(part1_ready, NC * n + c + 1)
                        dve.scalar_tensor_tensor(out=rest1[:, c, :], in0=ps_c[c][:, :], scalar=bias[:, c:c + 1],
                                                 in1=part1[:, s, c, :], op0=ALU.add, op1=ALU.subtract)\
                            .then_inc(rest1_ready, 1)
                    for c in range(NC):
                        dve.wait_ge(part2_ready, NC * n + c + 1)
                        dve.tensor_tensor(part3[:, s, c, :], rest1[:, c, :], part2[:, s, c, :], ALU.subtract)\
                            .then_inc(part3_ready, 1)


def phase_causal(nc, q_stacks, k_stacks, v9_in, mask_in, maskT_in, ident_in, ctx_out):
    SCALE = DH ** -0.5
    M0 = 64
    TILES = ((0,), (1, 3), (2,))
    OFF = {0: 0, 1: 512, 3: 896, 2: 1024}
    WIDTH = {0: 512, 1: 384, 2: 256, 3: 128}
    NTILE = len(TILES)
    SLOTS = 4
    ROUNDS = NI // SLOTS
    with ExitStack() as ctx:
        def sb(name, shape, dt=F32):
            return ctx.enter_context(nc.sbuf_tensor("c_" + name, shape, dt))

        sems = Semaphores(nc, ctx)

        def sem(name):
            return sems.new("c_" + name)

        def bank(name):
            return ctx.enter_context(nc.psum_tensor("c_" + name, [P, 512], F32))

        q = sb("q", [P, SLOTS, G, L], BF16)
        k = sb("k", [P, SLOTS, G, L], BF16)
        v9 = sb("v9", [P, SLOTS, NT, G * VW])
        mask32 = sb("mask32", [P, P])
        maskT32 = sb("maskT32", [P, P])
        mask = sb("mask", [P, P], BF16)
        maskT = sb("maskT", [P, P], BF16)
        identb = sb("identb", [P, P], BF16)
        ident = sb("ident", [P, P])
        zeros = sb("zeros", [P, 512], BF16)
        mx = sb("mx", [P, 2, G * NT])
        mrow = sb("mrow", [G * NT, 2, 2, P], BF16)
        probs = sb("probs", [P, 2, 1280])
        osb = sb("osb", [P, 2, G, P])
        ps_rows = [bank("ps_rows0"), bank("ps_rows1")]
        ps_m = bank("ps_m")
        ps_keys = [bank(f"ps_keys{i}") for i in range(4)]
        ps_out = bank("ps_out")

        consts = sem("consts")
        preset = sem("preset")
        minus_ones = sem("minus_ones")
        loaded = [sem(f"loaded{i}") for i in range(SLOTS)]
        rows_ps = sem("rows_ps")
        max_read = sem("max_read")
        m_ps = sem("m_ps")
        m_first = sem("m_first")
        m_split = sem("m_split")
        m_loaded = [sem(f"m_loaded{i}") for i in range(SLOTS)]
        keys_ps = sem("keys_ps")
        exp_done = sem("exp_done")
        head_done = sem("head_done")
        out_sb = sem("out_sb")
        stored = [sem("stored0"), sem("stored1")]
        block = ctx.enter_context(nc.Block())

        def load(eng, n, s):
            b, g = n // NG, n % NG
            eng.dma_start(q[0:SK, s, :, :], q_stacks.rearrange("b r (g h) t -> b g r h t", h=G)[b, g])\
                .then_inc(loaded[s], 16)
            eng.dma_start(k[0:SK, s, :, :], k_stacks.rearrange("b r (g h) t -> b g r h t", h=G)[b, g])\
                .then_inc(loaded[s], 16)
            eng.dma_start(v9[:, s, :, :], v9_in.rearrange("b p t (g v) -> b g p t v", g=NG)[b, g])\
                .then_inc(loaded[s], 16)

        def load_maxima(eng, s):
            for r in range(2):
                eng.dma_start(q[M0 + r:M0 + r + 1, s, :, :], mrow[:, s % 2, r, :]).then_inc(m_loaded[s], 16)

        def steps(step, eng):
            with eng.Fori(0, ROUNDS - 1) as it:
                for s in range(SLOTS):
                    step(it, s, SLOTS)
            for s in range(SLOTS):
                step(ROUNDS - 1, s, SLOTS - 1 - s)

        @block.sync
        def _(sp):
            def step(it, s, left):
                n = SLOTS * it + s
                if left >= 3:
                    sp.wait_ge(head_done, G * n + 2)
                    load(sp, n + 3, (s + 3) % SLOTS)
                if left >= 1:
                    sp.wait_ge(m_split, n + 2)
                    load_maxima(sp, (s + 1) % SLOTS)
                sp.wait_ge(out_sb, n + 2)
                for b in range(NT):
                    sp.dma_start(ctx_out[n, :, :, b * P:(b + 1) * P].rearrange("h r i -> r h i"),
                                 osb[32 * b:32 * b + VW, s % 2, :, :]).then_inc(stored[s % 2], 16)

            for dst, src in ((mask32, mask_in), (maskT32, maskT_in), (ident, ident_in)):
                sp.dma_start(dst[:, :], src).then_inc(consts, 16)
            sp.wait_ge(preset, 2)
            sp.wait_ge(minus_ones, 1)
            for s in range(SLOTS - 1):
                load(sp, s, s)
            for s in range(2):
                sp.sem_inc(stored[s], 64)
            sp.wait_ge(m_split, 1)
            load_maxima(sp, 0)
            steps(step, sp)
            for s in range(SLOTS):
                sp.wait_ge(loaded[s], 48 * ROUNDS)
                sp.wait_ge(m_loaded[s], 32 * ROUNDS)
            for s in range(2):
                sp.wait_ge(stored[s], 64 * (NI // 2 + 1))

        @block.gpsimd
        def _(pool):
            pool.wait_ge(preset, 1)
            pool.memset(k[M0:M0 + 2, :, :, :], -1.0).then_inc(minus_ones, 1)

        @block.tensor
        def _(pe):
            def row_tile(n, s, h, b):
                tile = NT * (G * n + h) + b
                ps = ps_rows[b % 2]
                if not isinstance(tile, int) or tile >= 2:
                    pe.wait_ge(max_read, tile - 1)
                pe.matmul(ps[:, 0:(b + 1) * P], q[0:M0, s, h, b * P:(b + 1) * P], k[0:M0, s, h, 0:(b + 1) * P],
                          start=True, stop=False)
                pe.matmul(ps[:, b * P:(b + 1) * P], identb[:, :], mask[:, :], start=False, stop=True)\
                    .then_inc(rows_ps, 1)

            def turn_maxima(n, s):
                pe.wait_ge(max_read, G * NT * (n + 1))
                pe.transpose(ps_m[0:G * NT, 0:P], mx[:, s % 2, :], ident[:, :]).then_inc(m_ps, 1)

            def key_tile(n, s, h, c):
                tile = NTILE * (G * n + h) + c
                ps = ps_keys[(NTILE * h + c) % 4]
                pe.wait_ge(exp_done, tile + 1)
                at = 0
                for j in TILES[c]:
                    pe.matmul(ps[:, at:at + WIDTH[j]], k[:, s, h, j * P:(j + 1) * P], q[:, s, h, j * P:L],
                              start=True, stop=False)
                    last = pe.matmul(ps[:, at:at + P], identb[:, :], maskT[:, :], start=False, stop=True)
                    at += WIDTH[j]
                last.then_inc(keys_ps, 1)

            def value_head(n, s, h):
                pe.wait_ge(exp_done, NTILE * (G * n + h + 1) + 4)
                if h == 0:
                    pe.wait_ge(out_sb, n + 1)
                for j in range(NT):
                    for b in range(j, NT):
                        last = pe.matmul(ps_out[32 * b:32 * b + VW, h * P:(h + 1) * P],
                                         v9[:, s, j, h * VW:(h + 1) * VW],
                                         probs[:, h % 2, OFF[j] + (b - j) * P:OFF[j] + (b - j + 1) * P],
                                         start=(j == 0), stop=(j == b), skip_group_check=True)
                last.then_inc(head_done, 1)

            def step(it, s, left):
                n = SLOTS * it + s
                s1, s2 = (s + 1) % SLOTS, (s + 2) % SLOTS
                if left >= 1:
                    turn_maxima(n + 1, s1)
                if left >= 2:
                    pe.wait_ge(loaded[s2], 48 * (it + (s + 2) // SLOTS + 1))
                for h in range(G):
                    nxt = (n, s, h + 1) if h + 1 < G else (n + 1, s1, 0)
                    if h == G - 1 and left >= 1:
                        pe.wait_ge(m_loaded[s1], 32 * (it + (s + 1) // SLOTS + 1))
                    for b in range(NT):
                        if left >= 2:
                            row_tile(n + 2, s2, h, b)
                        if b >= 1 and (h + 1 < G or left >= 1):
                            key_tile(*nxt, b - 1)
                    value_head(n, s, h)

            pe.wait_ge(consts, 48)
            pe.wait_ge(preset, 6)
            pe.wait_ge(minus_ones, 1)
            pe.matmul(ps_out[:, :], zeros[:, 0:P], zeros[:, :], start=True, stop=True)
            for s in range(2):
                pe.wait_ge(loaded[s], 48)
                for h in range(G):
                    for b in range(NT):
                        row_tile(s, s, h, b)
                if s == 0:
                    turn_maxima(0, 0)
            pe.wait_ge(m_loaded[0], 32)
            for c in range(NTILE):
                key_tile(0, 0, 0, c)
            steps(step, pe)

        @block.scalar
        def _(act):
            def exponentials(n, h):
                act.wait_ge(head_done, G * n + h + 1)
                for c, blocks in enumerate(TILES):
                    width = sum(WIDTH[j] for j in blocks)
                    act.wait_ge(keys_ps, NTILE * (G * n + h) + c + 1)
                    act.activation(probs[:, h % 2, OFF[blocks[0]]:OFF[blocks[0]] + width],
                                   ps_keys[(NTILE * h + c) % 4][:, 0:width], ACT.Exp, scale=SCALE)\
                        .then_inc(exp_done, 1)

            def step(it, s, left):
                n = SLOTS * it + s
                for h in range(1, G):
                    exponentials(n, h)
                if left >= 1:
                    exponentials(n + 1, 0)
                act.wait_ge(head_done, G * (n + 1) + 2)
                act.wait_ge(stored[s % 2], 64 * (SLOTS // 2 * it + s // 2 + 1))
                act.activation(osb[:, s % 2, :, :].rearrange("p h i -> p (h i)"), ps_out[:, :], ACT.Copy)\
                    .then_inc(out_sb, 1)

            act.sem_inc(exp_done, 4)
            act.sem_inc(out_sb, 1)
            exponentials(0, 0)
            steps(step, act)

        @block.vector
        def _(dve):
            def maxima(n, s, m):
                dve.wait_ge(rows_ps, G * NT * n + m + 1)
                dve.tensor_reduce(mx[:, s % 2, m:m + 1], ps_rows[m % 2][:, 0:(m % NT + 1) * P], AX_X, ALU.max)\
                    .then_inc(max_read, 1)

            def split_maxima(n, s):
                dve.wait_ge(m_ps, n + 1)
                dve.tensor_copy(mrow[:, s % 2, 0, :], ps_m[0:G * NT, 0:P]).then_inc(m_first, 1)
                dve.wait_ge(m_first, n + 1)
                dve.tensor_tensor(mrow[:, s % 2, 1, :], ps_m[0:G * NT, 0:P], mrow[:, s % 2, 0, :], ALU.subtract)\
                    .then_inc(m_split, 1)

            def step(it, s, left):
                n = SLOTS * it + s
                for m in range(G * NT if left >= 2 else 0):
                    maxima(n + 2, s, m)
                    if m == 1:
                        split_maxima(n + 1, s + 1)
                if left == 1:
                    split_maxima(n + 1, s + 1)

            dve.memset(k[:, :, :, :].rearrange("p s h t -> p (s h t)").bitcast(F32), 0.0).then_inc(preset, 1)
            dve.memset(q[:, :, :, :].rearrange("p s h t -> p (s h t)").bitcast(F32), 0.0).then_inc(preset, 1)
            dve.memset(zeros[:, :].bitcast(F32), 0.0).then_inc(preset, 1)
            dve.wait_ge(consts, 48)
            for narrow, full in ((mask, mask32), (maskT, maskT32), (identb, ident)):
                dve.tensor_copy(narrow[:, :], full[:, :]).then_inc(preset, 1)
            dve.sem_inc(head_done, 2)
            for n in range(2):
                for m in range(G * NT):
                    maxima(n, n, m)
                if n == 0:
                    split_maxima(0, 0)
            steps(step, dve)


def phase_merge(nc, ctx_in, x_in, w_in, b_in, base_out, z_out, name):
    with ExitStack() as ctx:
        def sb(nm, shape, dt=F32):
            return ctx.enter_context(nc.sbuf_tensor(f"{name}_{nm}", shape, dt))

        sems = Semaphores(nc, ctx)

        def sem(nm):
            return sems.new(f"{name}_{nm}")

        w = sb("w", [P, P])
        bo = sb("bo", [P, P])
        num = sb("num", [P, 2, L])
        den = sb("den", [P, 2, L])
        x = sb("x", [P, 2, NT, P])
        xb = sb("xb", [P, 2, NT, P])
        rec = sb("rec", [P, L])
        cT = sb("cT", [P, 2, L])
        xa = sb("xa", [P, 2, NT, P])
        base = sb("base", [P, 2, NT, P])
        z = sb("z", [P, 2, NT, P])
        norm = Norm(ctx, nc, sems, name + "_norm")
        ps = [ctx.enter_context(nc.psum_tensor(f"{name}_ps{i}", [P, L], F32)) for i in range(2)]

        consts = sem("consts")
        loaded = [sem("loaded0"), sem("loaded1")]
        x_loaded = [sem("x_loaded0"), sem("x_loaded1")]
        rec_ready = sem("rec_ready")
        cT_ready = sem("cT_ready")
        a_ps = sem("a_ps")
        xb_ready = sem("xb_ready")
        xa_ready = sem("xa_ready")
        base_ready = sem("base_ready")
        z_ready = sem("z_ready")
        stored = [sem("stored0"), sem("stored1")]
        n_const = 16 + 16 * (b_in is not None)
        n_out = 16 + 16 * (base_out is not None)
        block = ctx.enter_context(nc.Block())

        def load(eng, n, s):
            sums = ctx_in[NG * n:NG * n + NG] if isinstance(n, int) else ctx_in.rearrange(
                "(b g) h r t -> b g h r t", g=NG)[n]
            sums = sums.rearrange("g h r t -> (g h) r t")
            eng.dma_start(num[:, s, :], sums[:, 0:DH, :]).then_inc(loaded[s], 16)
            eng.dma_start(den[:, s, :], sums[:, DH:DH + 1, :].broadcast_to([H, DH, L])).then_inc(loaded[s], 16)

        def load_x(eng, n, s):
            eng.dma_start(x[:, s, :, :], x_in[n]).then_inc(x_loaded[s], 16)

        def steps(step, eng):
            with eng.Fori(0, NB // 2 - 1) as it:
                for s in range(2):
                    step(it, s, True)
            for s in range(2):
                step(NB // 2 - 1, s, s == 0)

        @block.sync
        def _(sp):
            sp.dma_start(w[:, :], w_in).then_inc(consts, 16)
            if b_in is not None:
                sp.dma_start(bo[:, :], row_on_all(b_in)).then_inc(consts, 16)
            for s in range(2):
                load(sp, s, s)
                load_x(sp, s, s)
                sp.sem_inc(stored[s], n_out)
            with sp.Fori(0, NB // 2) as it:
                for s in range(2):
                    n = 2 * it + s
                    sp.wait_ge(cT_ready, n + 1)
                    load(sp, (n + 2) % NB, s)
                    if base_out is None:
                        sp.wait_ge(xa_ready, n + 3)
                        load_x(sp, (n + 2) % NB, s)
                    else:
                        sp.wait_ge(base_ready, n + 1)
                        load_x(sp, (n + 2) % NB, s)
                        sp.dma_start(base_out[n], base[:, s, :, :]).then_inc(stored[s], 16)
                    sp.wait_ge(z_ready, n + 1)
                    sp.dma_start(z_out[n], z[:, s, :, :]).then_inc(stored[s], 16)
            for s in range(2):
                sp.wait_ge(loaded[s], 32 * (NB // 2 + 1))
                sp.wait_ge(x_loaded[s], 16 * (NB // 2 + 1))
                sp.wait_ge(stored[s], n_out * (NB // 2 + 1))

        @block.gpsimd
        def _(pool):
            def add_bias(n, s, loads):
                pool.wait_ge(x_loaded[s], 16 * loads)
                pool.wait_ge(xa_ready, n + 1)
                pool.tensor_tensor(xb[:, s, :, :], x[:, s, :, :],
                                   bo[:, :].unsqueeze(1).broadcast_to([P, NT, P]), ALU.add).then_inc(xb_ready, 1)

            def step(it, s, ahead):
                n = 2 * it + s
                if b_in is not None and ahead:
                    add_bias(n + 1, 1 - s, it + 1 + s)
                norm.root(pool, n + 1)
                if base_out is not None:
                    pool.wait_ge(stored[s], n_out * (it + 1))
                    pool.tensor_tensor(base[:, s, :, :], xa[:, s, :, :], x[:, s, :, :], ALU.add)\
                        .then_inc(base_ready, 1)

            norm.constants(pool)
            pool.wait_ge(consts, n_const)
            if b_in is not None:
                add_bias(0, 0, 1)
            steps(step, pool)

        @block.tensor
        def _(pe):
            pe.wait_ge(consts, n_const)
            with pe.Fori(0, NB // 2) as it:
                for s in range(2):
                    n = 2 * it + s
                    pe.wait_ge(cT_ready, n + 1)
                    pe.wait_ge(xa_ready, n + 1)
                    for t in range(NT):
                        last = pe.matmul(ps[s][:, t * P:(t + 1) * P], cT[:, s, t * P:(t + 1) * P], w[:, :],
                                         start=True, stop=True)
                    last.then_inc(a_ps, 1)

        @block.vector
        def _(dve):
            def divide(n, s, loads):
                dve.wait_ge(loaded[s], 32 * loads)
                dve.reciprocal(rec[:, :], den[:, s, :]).then_inc(rec_ready, 1)
                dve.wait_ge(rec_ready, n + 1)
                dve.tensor_tensor(cT[:, s, :], num[:, s, :], rec[:, :], ALU.mult).then_inc(cT_ready, 1)

            def step(it, s, ahead):
                n = 2 * it + s
                dve.wait_ge(a_ps, n + 1)
                if b_in is not None:
                    dve.wait_ge(xb_ready, n + 1)
                else:
                    dve.wait_ge(x_loaded[s], 16 * (it + 1))
                dve.wait_ge(stored[s], n_out * (it + 1))
                src = xb if b_in is not None else x
                dve.tensor_tensor(xa[:, s, :, :], ps[s][:, :].rearrange("p (t d) -> p t d", t=NT),
                                  src[:, s, :, :], ALU.add).then_inc(xa_ready, 1)
                dve.wait_ge(xa_ready, n + 3)
                norm.moments(dve, xa[:, s, :, :], n + 1)
                if ahead:
                    divide(n + 1, 1 - s, it + 1 + s)
                norm.apply(dve, z[:, s, :, :], xa[:, s, :, :], n + 1).then_inc(z_ready, 1)

            dve.sem_inc(xa_ready, 2)
            divide(0, 0, 1)
            steps(step, dve)


def phase_experts(nc, z_in, base_in, scale, shift, gate_in, w1_in, w2_in, w3_in, iota_in, ident_in, x_out):
    with ExitStack() as ctx:
        def sb(name, shape, dt=F32):
            return ctx.enter_context(nc.sbuf_tensor("e_" + name, shape, dt))

        sems = Semaphores(nc, ctx)

        def sem(name):
            return sems.new("e_" + name)

        KH = HID // P
        w1 = sb("w1", [P, NE, HID])
        w2 = sb("w2", [P, NE, HID])
        w3 = sb("w3", [P, NE, KH, P])
        gate = sb("gate", [P, NE])
        sc = sb("scale", [P, 2])
        ident = sb("ident", [P, P])
        iota = sb("iota", [P, NE])
        z = sb("z", [P, 2, NT, P])
        base = sb("base", [P, 2, NT, P])
        hT = sb("hT", [P, 2, L])
        scores = sb("scores", [P, NT, NE])
        top = sb("top", [P, NT, 8])
        idx = sb("idx", [P, NT, 8], U32)
        idxf = sb("idxf", [P, NT, 8])
        diff = sb("diff", [P, NT])
        pr = sb("pr", [P, 2, NT])
        hot = sb("hot", [P, 2, NT, NE])
        weight = sb("weight", [P, 2, NT, NE])
        silu = sb("silu", [P, KH, L])
        gu = sb("gu", [P, 2, KH, L])
        acc = sb("acc", [P, NT, P])
        xo = sb("xo", [P, 2, NT, P])
        norm = Norm(ctx, nc, sems, "e_norm")
        ps_zT = ctx.enter_context(nc.psum_tensor("e_ps_zT", [P, L], F32))
        ps_s = ctx.enter_context(nc.psum_tensor("e_ps_s", [P, 512], F32))
        ps_a = ctx.enter_context(nc.psum_tensor("e_ps_a", [P, KH, L], F32))
        ps_b = ctx.enter_context(nc.psum_tensor("e_ps_b", [P, KH, L], F32))
        ps_o = [ctx.enter_context(nc.psum_tensor(f"e_ps_o{i}", [P, L], F32)) for i in range(2)]

        consts = sem("consts")
        loaded = [sem("loaded0"), sem("loaded1")]
        zT_ps = sem("zT_ps")
        hT_sb = sem("hT_sb")
        s_ps = sem("scores_ps")
        diff_ready = sem("diff_ready")
        pr_ready = sem("pr_ready")
        best_chain = sem("best_chain")
        weight_chain = sem("weight_chain")
        weight_ready = sem("weight_ready")
        marks = sem("marks")
        a_ps = sem("a_ps")
        b_ps = sem("b_ps")
        silu_sb = sem("silu_sb")
        gu_sb = sem("gu_sb")
        o_ps = sem("o_ps")
        o_read = sem("o_read")
        base_free = sem("base_free")
        x_ready = sem("x_ready")
        stored = [sem("stored0"), sem("stored1")]
        n_const = 16 * 8
        block = ctx.enter_context(nc.Block())

        def steps(step, eng):
            with eng.Fori(0, NB // 2 - 1) as it:
                for s in range(2):
                    step(it, s, True)
            for s in range(2):
                step(NB // 2 - 1, s, s == 0)

        def load(eng, n, s):
            eng.dma_start(z[:, s, :, :], z_in[n]).then_inc(loaded[s], 16)
            eng.dma_start(base[:, s, :, :], base_in[n]).then_inc(loaded[s], 16)

        @block.sync
        def _(sp):
            sp.dma_start(gate[:, :], gate_in).then_inc(consts, 16)
            sp.dma_start(sc[:, 0:1], scale.rearrange("(d o) -> d o", o=1)).then_inc(consts, 16)
            sp.dma_start(sc[:, 1:2], shift.rearrange("(d o) -> d o", o=1)).then_inc(consts, 16)
            sp.dma_start(ident[:, :], ident_in).then_inc(consts, 16)
            sp.dma_start(iota[:, :], row_on_all(iota_in, NE)).then_inc(consts, 16)
            for s in range(2):
                sp.sem_inc(stored[s], 16)
                load(sp, s, s)
            sp.dma_start(w1[:, :, :], w1_in.rearrange("e d h -> d e h")).then_inc(consts, 16)
            sp.dma_start(w2[:, :, :], w2_in.rearrange("e d h -> d e h")).then_inc(consts, 16)
            sp.dma_start(w3[:, :, :, :].rearrange("p e k d -> p (e k) d"),
                         w3_in.rearrange("e (k p) d -> p (e k) d", p=P)).then_inc(consts, 16)
            with sp.Fori(0, NB // 2) as it:
                for s in range(2):
                    n = 2 * it + s
                    sp.wait_ge(base_free, n + 1)
                    load(sp, (n + 2) % NB, s)
                    sp.wait_ge(x_ready, n + 1)
                    sp.dma_start(x_out[n], xo[:, s, :, :]).then_inc(stored[s], 16)
            for s in range(2):
                sp.wait_ge(loaded[s], 32 * (NB // 2 + 1))
                sp.wait_ge(stored[s], 16 * (NB // 2 + 1))

        @block.gpsimd
        def _(pool):
            norm.constants(pool)
            with pool.Fori(0, NB) as n:
                norm.root(pool, n + 1)

        @block.tensor
        def _(pe):
            def route(n, s, load_count):
                pe.wait_ge(loaded[s], load_count)
                for t in range(NT):
                    last = pe.transpose(ps_zT[:, t * P:(t + 1) * P], z[:, s, t, :], ident[:, :])
                last.then_inc(zT_ps, 1)
                pe.wait_ge(hT_sb, n + 1)
                for t in range(NT):
                    last = pe.matmul(ps_s[:, t * NE:(t + 1) * NE], hT[:, s, t * P:(t + 1) * P], gate[:, :],
                                     start=True, stop=True)
                last.then_inc(s_ps, 1)

            def up(w, ps, e, s, ready):
                for k in range(KH):
                    last = pe.matmul(ps[:, k, :], w[:, e, k * P:(k + 1) * P], hT[:, s, :], start=True, stop=True)
                last.then_inc(ready, 1)

            def down(m, e, parity):
                pe.wait_ge(gu_sb, m + 2)
                pe.wait_ge(o_read, m + 1)
                for t in range(NT):
                    for k in range(KH):
                        last = pe.matmul(ps_o[parity][:, t * P:(t + 1) * P], gu[:, parity, k, t * P:(t + 1) * P],
                                         w3[:, e, k, :], start=(k == 0), stop=(k == KH - 1))
                last.then_inc(o_ps, 1)

            def ups(n, s, e):
                m = NE * n + e
                pe.wait_ge(silu_sb, m + 1)
                up(w1, ps_a, e, s, a_ps)
                pe.wait_ge(gu_sb, m + 1)
                up(w2, ps_b, e, s, b_ps)

            def step(it, s, ahead):
                n = 2 * it + s
                for e in range(NE):
                    if e + 1 < NE:
                        ups(n, s, e + 1)
                    elif ahead:
                        ups(n + 1, 1 - s, 0)
                    if e == 0 and ahead:
                        route(n + 1, 1 - s, 32 * (it + 1 + s))
                    down(NE * n + e, e, e % 2)

            pe.wait_ge(consts, 16 * 5)
            route(0, 0, 32)
            pe.wait_ge(consts, n_const)
            ups(0, 0, 0)
            steps(step, pe)

        @block.scalar
        def _(act):
            def turn(n, s):
                act.wait_ge(zT_ps, n + 1)
                act.activation(hT[:, s, :], ps_zT[:, :], ACT.Identity, bias=sc[:, 1:2], scale=sc[:, 0:1])\
                    .then_inc(hT_sb, 1)

            def weigh(n):
                act.wait_ge(diff_ready, n + 1)
                act.activation(pr[:, 0, :], diff[:, :], ACT.Sigmoid, scale=-1.0).then_inc(pr_ready, 1)
                act.activation(pr[:, 1, :], diff[:, :], ACT.Sigmoid).then_inc(pr_ready, 1)

            def activate(m):
                act.wait_ge(a_ps, m + 1)
                act.wait_ge(gu_sb, m + 1)
                act.activation(silu[:, :, :], ps_a[:, :, :], ACT.Silu).then_inc(silu_sb, 1)

            def step(it, s, ahead):
                n = 2 * it + s
                for e in range(NE):
                    if e + 1 < NE or ahead:
                        activate(NE * n + e + 1)
                    if e == 0 and ahead:
                        turn(n + 1, 1 - s)
                    if e == 3 and ahead:
                        weigh(n + 1)

            act.sem_inc(silu_sb, 1)
            act.wait_ge(consts, 16 * 5)
            turn(0, 0)
            weigh(0)
            activate(0)
            steps(step, act)

        @block.vector
        def _(dve):
            def best(n):
                chain = Chain(dve, best_chain, n, 2)
                dve.wait_ge(s_ps, n + 1)
                chain.step(dve.tensor_copy(scores[:, :, :].rearrange("p t e -> p (t e)"), ps_s[:, 0:NT * NE]))
                dve.sem_inc(marks, 1)
                for t in range(NT):
                    last = dve.max(top[:, t, :], scores[:, t, :])
                chain.step(last)
                dve.tensor_tensor(diff[:, :], top[:, :, 1], top[:, :, 0], ALU.subtract).then_inc(diff_ready, 1)
                chain.done()

            def weights(n, s):
                chain = Chain(dve, weight_chain, n, 3)
                for t in range(NT):
                    last = dve.max_index(idx[:, t, :], top[:, t, :], scores[:, t, :])
                chain.step(last)
                chain.step(dve.tensor_copy(idxf[:, :, :], idx[:, :, :]))
                dve.wait_ge(pr_ready, 2 * (n + 1))
                for t in range(NT):
                    for r in range(2):
                        last = dve.tensor_scalar(hot[:, r, t, :], iota[:, :], idxf[:, t, r:r + 1],
                                                 pr[:, r, t:t + 1], ALU.is_equal, ALU.mult)
                chain.step(last)
                dve.tensor_tensor(weight[:, s, :, :], hot[:, 0, :, :], hot[:, 1, :, :], ALU.add)\
                    .then_inc(weight_ready, 1)
                chain.done()

            def gate_up(m, parity):
                dve.wait_ge(silu_sb, m + 2)
                dve.wait_ge(b_ps, m + 1)
                dve.tensor_tensor(gu[:, parity, :, :], silu[:, :, :], ps_b[:, :, :], ALU.mult)\
                    .then_inc(gu_sb, 1)

            def add_expert(n, m, s, e):
                dve.wait_ge(o_ps, m + 1)
                if e == 0:
                    dve.wait_ge(weight_ready, n + 1)
                dve.wait_ge(o_read, m + 1)
                for t in range(NT):
                    prev = base[:, s, t, :] if e == 0 else acc[:, t, :]
                    last = dve.scalar_tensor_tensor(out=acc[:, t, :], in0=ps_o[e % 2][:, t * P:(t + 1) * P],
                                                    scalar=weight[:, s, t, e:e + 1], in1=prev,
                                                    op0=ALU.mult, op1=ALU.add)
                last.then_inc(o_read, 1)
                if e == 0:
                    dve.wait_ge(o_read, m + 2)
                    dve.sem_inc(base_free, 1)

            def step(it, s, ahead):
                n = 2 * it + s
                for e in range(NE):
                    m = NE * n + e
                    if e + 1 < NE or ahead:
                        gate_up(m + 1, (e + 1) % 2)
                    add_expert(n, m, s, e)
                    if e == 1 and ahead:
                        best(n + 1)
                    if e == 4 and ahead:
                        weights(n + 1, 1 - s)
                dve.wait_ge(o_read, NE * (n + 1) + 1)
                norm.moments(dve, acc, n + 1)
                dve.wait_ge(stored[s], 16 * (it + 1))
                norm.apply(dve, xo[:, s, :, :], acc, n + 1).then_inc(x_ready, 1)
                dve.wait_ge(x_ready, n + 1)

            dve.sem_inc(gu_sb, 1)
            dve.sem_inc(o_read, 1)
            dve.wait_ge(consts, 16 * 5)
            best(0)
            weights(0, 0)
            gate_up(0, 0)
            steps(step, dve)


def phase_last(nc, x_in, u1T_in, v1_in, b1_in, u2_in, v2_in, b2_in, ident_in, out):
    KF = FF // P
    assert KF * RANK == P
    with ExitStack() as ctx:
        def sb(name, shape, dt=F32):
            return ctx.enter_context(nc.sbuf_tensor("f_" + name, shape, dt))

        sems = Semaphores(nc, ctx)

        def sem(name):
            return sems.new("f_" + name)

        u1T = sb("u1T", [RANK, P])
        v1 = sb("v1", [RANK, FF])
        uv = sb("uv", [P, FF])
        b1 = sb("b1", [P, KF])
        u2 = sb("u2", [P, KF, RANK])
        v2 = sb("v2", [P, P])
        b2 = sb("b2", [P, P])
        ident = sb("ident", [P, P])
        x = sb("x", [P, 2, NT, P])
        xb = sb("xb", [P, 2, NT, P])
        xT = sb("xT", [P, 2, L])
        hT = sb("hT", [P, KF, L])
        qT = sb("qT", [P, L])
        t1 = sb("t1", [P, NT, P])
        y = sb("y", [P, 2, NT, P])
        norm = Norm(ctx, nc, sems, "f_norm")
        ps_xT = ctx.enter_context(nc.psum_tensor("f_ps_xT", [P, L], F32))
        ps_h = [ctx.enter_context(nc.psum_tensor(f"f_ps_h{i}", [P, L], F32)) for i in range(KF)]
        ps_q = ctx.enter_context(nc.psum_tensor("f_ps_q", [P, L], F32))
        ps_y = ctx.enter_context(nc.psum_tensor("f_ps_y", [P, L], F32))

        consts = sem("consts")
        loaded = [sem("loaded0"), sem("loaded1")]
        xT_ps = sem("xT_ps")
        xT_sb = sem("xT_sb")
        uv_ps = sem("uv_ps")
        uv_sb = sem("uv_sb")
        h_ps = sem("h_ps")
        h_sb = sem("h_sb")
        q_ps = sem("q_ps")
        q_sb = sem("q_sb")
        y_ps = sem("y_ps")
        y_read = sem("y_read")
        xb_ready = sem("xb_ready")
        out_ready = sem("out_ready")
        stored = [sem("stored0"), sem("stored1")]
        N_CONST = 16 * (6 + KF)
        block = ctx.enter_context(nc.Block())

        def steps(step, eng):
            with eng.Fori(0, NB // 2 - 1) as it:
                for s in range(2):
                    step(it, s, 2)
            for s in range(2):
                step(NB // 2 - 1, s, 1 - s)

        @block.sync
        def _(sp):
            for s in range(2):
                sp.dma_start(x[:, s, :, :], x_in[s]).then_inc(loaded[s], 16)
            sp.dma_start(ident[:, :], ident_in).then_inc(consts, 16)
            sp.dma_start(b1[:, :], b1_in).then_inc(consts, 16)
            sp.dma_start(u2[:, :, :], u2_in.rearrange("(k p) r -> p k r", p=P)).then_inc(consts, 16)
            sp.dma_start(u1T[:, :], u1T_in).then_inc(consts, 16)
            sp.dma_start(v1[:, :], v1_in).then_inc(consts, 16)
            sp.dma_start(b2[:, :], row_on_all(b2_in)).then_inc(consts, 16)
            for k in range(KF):
                sp.dma_start(v2[RANK * k:RANK * k + RANK, :], v2_in).then_inc(consts, 16)
            for s in range(2):
                sp.sem_inc(stored[s], 16)
            with sp.Fori(0, NB // 2) as it:
                for s in range(2):
                    n = 2 * it + s
                    sp.wait_ge(xb_ready, n + 1)
                    sp.dma_start(x[:, s, :, :], x_in[(n + 2) % NB]).then_inc(loaded[s], 16)
                    sp.wait_ge(out_ready, n + 1)
                    sp.dma_start(out[n].rearrange("(t p) d -> p t d", p=P), y[:, s, :, :]).then_inc(stored[s], 16)
            for s in range(2):
                sp.wait_ge(loaded[s], 16 * (NB // 2 + 1))
                sp.wait_ge(stored[s], 16 * (NB // 2 + 1))

        @block.gpsimd
        def _(pool):
            def add_b2(n, s):
                pool.wait_ge(xT_ps, n + 1)
                pool.tensor_tensor(xb[:, s, :, :], x[:, s, :, :],
                                   b2[:, :].unsqueeze(1).broadcast_to([P, NT, P]), ALU.add).then_inc(xb_ready, 1)

            def step(it, s, left):
                n = 2 * it + s
                if left >= 1:
                    pool.wait_ge(y_read, n + 1)
                    add_b2(n + 1, 1 - s)
                norm.root(pool, n + 1)

            norm.constants(pool)
            pool.wait_ge(consts, N_CONST)
            add_b2(0, 0)
            steps(step, pool)

        @block.tensor
        def _(pe):
            def turn(n, s, loads):
                pe.wait_ge(loaded[s], 16 * loads)
                for t in range(NT):
                    last = pe.transpose(ps_xT[:, t * P:(t + 1) * P], x[:, s, t, :], ident[:, :])
                last.then_inc(xT_ps, 1)

            def hidden(n, s):
                pe.wait_ge(xT_sb, n + 1)
                for k in range(KF):
                    pe.matmul(ps_h[k][:, :], uv[:, k * P:(k + 1) * P], xT[:, s, :], start=True, stop=True)\
                        .then_inc(h_ps, 1)

            def step(it, s, left):
                n = 2 * it + s
                pe.wait_ge(h_sb, KF * (n + 1))
                for k in range(KF):
                    last = pe.matmul(ps_q[RANK * k:RANK * k + RANK, :], u2[:, k, :], hT[:, k, :], start=True, stop=True)
                last.then_inc(q_ps, 1)
                if left >= 1:
                    hidden(n + 1, 1 - s)
                if left >= 2:
                    turn(n + 2, s, it + 2)
                pe.wait_ge(q_sb, n + 1)
                pe.wait_ge(y_read, n + 1)
                for t in range(NT):
                    last = pe.matmul(ps_y[:, t * P:(t + 1) * P], qT[:, t * P:(t + 1) * P], v2[:, :],
                                     start=True, stop=True)
                last.then_inc(y_ps, 1)

            pe.wait_ge(consts, N_CONST)
            turn(0, 0, 1)
            pe.wait_ge(xT_sb, 1)
            turn(1, 1, 1)
            pe.matmul(ps_h[0][:, :], u1T[:, :], v1[:, :], start=True, stop=True).then_inc(uv_ps, 1)
            pe.wait_ge(uv_sb, 1)
            hidden(0, 0)
            steps(step, pe)

        @block.scalar
        def _(act):
            def gelus(n):
                for k in range(KF):
                    act.wait_ge(h_ps, KF * n + k + 1)
                    act.activation(hT[:, k, :], ps_h[k][:, :], ACT.Gelu_apprx_tanh, bias=b1[:, k:k + 1])\
                        .then_inc(h_sb, 1)

            act.wait_ge(consts, N_CONST)
            gelus(0)
            with act.Fori(1, NB) as n:
                gelus(n)

        @block.vector
        def _(dve):
            def turned(n, s):
                dve.wait_ge(xT_ps, n + 1)
                dve.tensor_copy(xT[:, s, :], ps_xT[:, :]).then_inc(xT_sb, 1)

            def step(it, s, left):
                n = 2 * it + s
                dve.wait_ge(q_ps, n + 1)
                dve.tensor_copy(qT[:, :], ps_q[:, :]).then_inc(q_sb, 1)
                dve.wait_ge(y_ps, n + 1)
                dve.wait_ge(xb_ready, n + 1)
                dve.tensor_tensor(t1[:, :, :], ps_y[:, :].rearrange("p (t d) -> p t d", t=NT),
                                  xb[:, s, :, :], ALU.add).then_inc(y_read, 1)
                dve.wait_ge(y_read, n + 2)
                norm.moments(dve, t1, n + 1)
                if left >= 2:
                    turned(n + 2, s)
                dve.wait_ge(stored[s], 16 * (it + 1))
                norm.apply(dve, y[:, s, :, :], t1, n + 1).then_inc(out_ready, 1)

            dve.sem_inc(y_read, 1)
            turned(0, 0)
            turned(1, 1)
            dve.wait_ge(uv_ps, 1)
            dve.tensor_copy(uv[:, :], ps_h[0][:, :]).then_inc(uv_sb, 1)
            steps(step, dve)


def phase_positions(nc, w_rT, r_in, stack_out):
    with ExitStack() as ctx:
        def sb(name, shape, dt=F32):
            return ctx.enter_context(nc.sbuf_tensor("p_" + name, shape, dt))

        sems = Semaphores(nc, ctx)

        def sem(name):
            return sems.new("p_" + name)

        w = sb("w", [P, P])
        r = sb("r", [P, 2, L])
        part = [sb(f"part{i}", [P, HW + 2 * (L + HW)], BF16) for i in range(3)]
        rest = sb("rest", [P, 2, L])
        ps = ctx.enter_context(nc.psum_tensor("p_ps", [P, 2, L], F32))
        loaded = sem("loaded")
        done_ps = sem("done_ps")
        step = sem("step")
        zeroed = sem("zeroed")
        stored = sem("stored")
        block = ctx.enter_context(nc.Block())

        @block.sync
        def _(sp):
            sp.dma_start(w[:, :], w_rT).then_inc(loaded, 16)
            sp.dma_start(r[:, :, :].rearrange("p a t -> p (a t)"), r_in).then_inc(loaded, 16)
            sp.wait_ge(zeroed, 3)
            sp.wait_ge(step, 5)
            for t, which in enumerate(TERMS_K):
                for row, col in ((DH * t, HW), (SK + DH * t, 0)):
                    sp.dma_start(stack_out[row:row + DH, :, :].rearrange("d h n -> h d n"),
                                 part[which][:, col:col + 2 * L + HW]).then_inc(stored, 16)
            sp.wait_ge(stored, 32 * len(TERMS_K))

        @block.tensor
        def _(pe):
            pe.wait_ge(loaded, 32)
            for a in range(2):
                last = pe.matmul(ps[:, a, :], w[:, :], r[:, a, :], start=True, stop=True)
            last.then_inc(done_ps, 1)

        @block.vector
        def _(dve):
            def halves(part):
                return part[:, HW:].rearrange("p (a t) -> p a t", a=2)[:, :, 0:L]

            for p in part:
                dve.memset(p[:, :].bitcast(F32), 0.0).then_inc(zeroed, 1)
            dve.wait_ge(zeroed, 3)
            dve.wait_ge(done_ps, 1)
            dve.tensor_copy(halves(part[0]), ps[:, :, :]).then_inc(step, 1)
            dve.wait_ge(step, 1)
            dve.tensor_tensor(rest[:, :, :], ps[:, :, :], halves(part[0]), ALU.subtract).then_inc(step, 1)
            dve.wait_ge(step, 2)
            dve.tensor_copy(halves(part[1]), rest[:, :, :]).then_inc(step, 1)
            dve.wait_ge(step, 3)
            dve.tensor_tensor(rest[:, :, :], rest[:, :, :], halves(part[1]), ALU.subtract).then_inc(step, 1)
            dve.wait_ge(step, 4)
            dve.tensor_copy(halves(part[2]), rest[:, :, :]).then_inc(step, 1)


def phase_relative(nc, qu_stacks, qv_stacks, k_stacks, v9_in, r_stack, half_in, ident_in, ctx_out):
    SCALE = DH ** -0.5
    Q = 32
    W = L + HW
    TG = G * NT
    SKEW = 16 * HW
    ROUNDS = NI // 2
    LOWEST = -3.0e38
    with ExitStack() as ctx:
        def sb(name, shape, dt=F32):
            return ctx.enter_context(nc.sbuf_tensor("r_" + name, shape, dt))

        sems = Semaphores(nc, ctx)

        def sem(name):
            return sems.new("r_" + name)

        def bank(name):
            return ctx.enter_context(nc.psum_tensor("r_" + name, [P, 512], F32))

        qu = sb("qu", [P, 2, G, L], BF16)
        k = sb("k", [P, 2, G, L], BF16)
        qv = sb("qv", [2 * SK, G, L + 2], BF16)
        qv_here = sb("qv_here", [P, 2, G, L], BF16)
        qv_next = sb("qv_next", [P, 2, G, L], BF16)
        half = sb("half", [2 * SK, L], BF16)
        r = sb("r", [P, 2, G, 2 * L + HW], BF16)
        v9 = sb("v9", [P, 2, NT, G * VW])
        ident = sb("ident", [P, P])
        wide = sb("wide", [P, 2, TG, W])
        shifted = sb("shifted", [P, 2, TG, L])
        mx = sb("mx", [P, TG])
        probs = sb("probs", [P, 2, NT, L])
        osb = sb("osb", [P, G, P])
        ps_wide = [bank("ps_wide0"), bank("ps_wide1")]
        ps_tail = bank("ps_tail")
        ps_ac = [bank("ps_ac0"), bank("ps_ac1")]
        ps_keys = [bank("ps_keys0"), bank("ps_keys1")]
        ps_out = bank("ps_out")

        consts = sem("consts")
        pad_set = sem("pad_set")
        half_set = sem("half_set")
        loaded = [sem("loaded0"), sem("loaded1")]
        qv_loaded = sem("qv_loaded")
        qv_halved = sem("qv_halved")
        r_loaded = [sem("r_loaded0"), sem("r_loaded1")]
        wide_ps = sem("wide_ps")
        wide_sb = sem("wide_sb")
        tail_sb = sem("tail_sb")
        skewed = [sem("skewed0"), sem("skewed1")]
        ac_ps = sem("ac_ps")
        ac_used = sem("ac_used")
        marks = sem("marks")
        s_ready = sem("scores_ready")
        slot_marks = sem("slot_marks")
        keys_ps = sem("keys_ps")
        exp_done = sem("exp_done")
        head_done = sem("head_done")
        out_sb = sem("out_sb")
        stored = sem("stored")
        block = ctx.enter_context(nc.Block())

        def steps(step, eng):
            for s in range(2):
                step(0, s, s == 0, 2)
            with eng.Fori(0, ROUNDS - 2) as it:
                for s in range(2):
                    step(it + 1, s, False, 2)
            for s in range(2):
                step(ROUNDS - 1, s, False, 1 - s)

        @block.sync
        def _(sp):
            def load(n, s):
                b, g = n // NG, n % NG
                for dst, src in ((qu, qu_stacks), (k, k_stacks)):
                    sp.dma_start(dst[0:SK, s, :, :], src.rearrange("b r (g h) t -> b g r h t", h=G)[b, g])\
                        .then_inc(loaded[s], 16)
                sp.dma_start(v9[:, s, :, :], v9_in.rearrange("b p t (g v) -> b g p t v", g=NG)[b, g])\
                    .then_inc(loaded[s], 16)

            def load_queries(n):
                b, g = n // NG, n % NG
                for row in (0, SK):
                    sp.dma_start(qv[row:row + SK, :, 0:L], qv_stacks.rearrange("b r (g h) t -> b g r h t", h=G)[b, g])\
                        .then_inc(qv_loaded, 16)

            def load_positions(n, s):
                sp.dma_start(r[0:2 * SK, s, :, :], r_stack.rearrange("r (g h) t -> g r h t", h=G)[n % NG])\
                    .then_inc(r_loaded[s], 16)

            def skew(n, s):
                sp.wait_ge(tail_sb, n + 1)
                for i in range(HW):
                    sp.dma_start(shifted[i::HW, s, :, :], wide[i::HW, s, :, HW - 1 - i:HW - 1 - i + L])\
                        .then_inc(skewed[s], 16)

            def step(it, s, first, left):
                n = 2 * it + s
                if left >= 1:
                    if not first:
                        sp.wait_ge(keys_ps, TG * n)
                        sp.sem_inc(slot_marks, 1)
                    skew(n + 1, 1 - s)
                if left >= 2:
                    sp.wait_ge(qv_halved, 2 * (n + 3))
                    load_queries((n + 3) % NI)
                    sp.wait_ge(wide_ps, TG * (n + 2))
                    load_positions((n + 3) % NI, 1 - s)
                if left >= 1:
                    sp.wait_ge(head_done, G * n + 2)
                    load(n + 1, 1 - s)
                if not first:
                    store(n - 1)

            def store(n):
                sp.wait_ge(out_sb, n + 2)
                for b in range(NT):
                    sp.dma_start(ctx_out[n, :, :, b * P:(b + 1) * P].rearrange("h r i -> r h i"),
                                 osb[Q * b:Q * b + VW, :, :]).then_inc(stored, 16)

            sp.dma_start(ident[:, :], ident_in).then_inc(consts, 16)
            sp.dma_start(shifted[0:2 * SK, 0, 0, :], half_in).then_inc(consts, 16)
            sp.wait_ge(pad_set, 6)
            load_queries(0)
            load_positions(0, 0)
            load_positions(1, 1)
            load(0, 0)
            sp.wait_ge(qv_halved, 2)
            load_queries(1)
            sp.wait_ge(qv_halved, 4)
            load_queries(2)
            sp.wait_ge(wide_ps, TG)
            load_positions(2, 0)
            sp.sem_inc(stored, 64)
            sp.wait_ge(half_set, 1)
            skew(0, 0)
            steps(step, sp)
            store(NI - 1)
            for s in range(2):
                sp.wait_ge(loaded[s], 48 * ROUNDS)
                sp.wait_ge(r_loaded[s], 16 * (ROUNDS + 1 - s))
                sp.wait_ge(skewed[s], SKEW * ROUNDS)
            sp.wait_ge(qv_loaded, 32 * (NI + 1))
            sp.wait_ge(stored, 64 * (NI + 1))

        @block.gpsimd
        def _(pool):
            def halve(n, s):
                mask = half[:, :].unsqueeze(1).broadcast_to([2 * SK, G, L])
                pool.wait_ge(qv_loaded, 32 * (n + 1))
                pool.tensor_tensor(qv_here[0:2 * SK, s, :, :], qv[:, :, 0:L], mask, ALU.mult)\
                    .then_inc(qv_halved, 1)
                pool.tensor_tensor(qv_next[0:2 * SK, s, :, :], qv[:, :, 1:L + 1], mask, ALU.mult)\
                    .then_inc(qv_halved, 1)

            pool.wait_ge(pad_set, 6)
            pool.wait_ge(half_set, 1)
            for n in range(2):
                halve(n, n)
            with pool.Fori(0, ROUNDS - 1) as it:
                for s in range(2):
                    n = 2 * it + 2 + s
                    pool.wait_ge(wide_ps, TG * (n - 1))
                    halve(n, s)

        @block.tensor
        def _(pe):
            def wide_tile(n, s, u):
                h, b = u // NT, u % NT
                tile = TG * n + u
                ps = ps_wide[u % 2]
                if not isinstance(tile, int) or tile >= 2:
                    pe.wait_ge(wide_sb, tile - 1)
                if u == 0 and (not isinstance(n, int) or n):
                    pe.wait_ge(tail_sb, n)
                windows, tails = ([], []), []
                for a in range(P // Q):
                    q0 = b * P + a * Q
                    here, after = qv_here[:, s, h, q0:q0 + Q], qv_next[:, s, h, q0:q0 + Q]
                    at = L - HW - q0
                    windows[0].append((a, here, 0, q0 + Q, at))
                    windows[1].append((a, after, q0 + HW, L, at + HW))
                    tails.append((a, after, L, W, at + HW))
                for which in range(2):
                    for a, lhs, lo, hi, at in windows[which]:
                        pe.matmul(ps[Q * a:Q * a + Q, lo:hi], lhs, r[:, s, h, at + lo:at + hi],
                                  start=(which == 0), stop=(which == 1), skip_group_check=True)
                for a, lhs, lo, hi, at in tails:
                    last = pe.matmul(ps_tail[Q * a:Q * a + Q, HW * u:HW * (u + 1)], lhs,
                                     r[:, s, h, at + lo:at + hi], start=True, stop=True)
                last.then_inc(wide_ps, 1)

            def content_tile(n, s, u):
                h, b = u // NT, u % NT
                pe.wait_ge(ac_used, TG * n + u + 1)
                pe.matmul(ps_ac[u % 2][:, :], qu[:, s, h, b * P:(b + 1) * P], k[:, s, h, :], start=True, stop=True)\
                    .then_inc(ac_ps, 1)

            def turn_tile(n, s, u):
                pe.wait_ge(s_ready, TG * n + u + 1)
                pe.wait_ge(exp_done, TG * n + u + 1)
                for j in range(NT):
                    last = pe.transpose(ps_keys[u % 2][:, j * P:(j + 1) * P],
                                        shifted[:, s, u, j * P:(j + 1) * P], ident[:, :])
                last.then_inc(keys_ps, 1)

            def value_head(n, s, h):
                pe.wait_ge(exp_done, TG * n + NT * (h + 1) + 2)
                if h == 0:
                    pe.wait_ge(out_sb, n + 1)
                for j in range(NT):
                    for b in range(NT):
                        last = pe.matmul(ps_out[Q * b:Q * b + VW, h * P:(h + 1) * P],
                                         v9[:, s, j, h * VW:(h + 1) * VW], probs[:, h % 2, j, b * P:(b + 1) * P],
                                         start=(j == 0), stop=(j == NT - 1), skip_group_check=True)
                last.then_inc(head_done, 1)

            def step(it, s, first, left):
                n = 2 * it + s
                if left >= 2:
                    pe.wait_ge(qv_halved, 2 * (n + 3))
                    pe.wait_ge(r_loaded[s], 16 * (it + 2))
                for u in range(TG):
                    if u + 2 < TG:
                        content_tile(n, s, u + 2)
                    elif left >= 1:
                        if u + 2 == TG:
                            pe.wait_ge(loaded[1 - s], 48 * (it + 1 + s))
                        content_tile(n + 1, 1 - s, u + 2 - TG)
                    turn_tile(n, s, u)
                    if left >= 2:
                        wide_tile(n + 2, s, u)
                    if u == 1 and not first:
                        value_head(n - 1, 1 - s, G - 1)
                    if u % NT == 1 and u > NT:
                        value_head(n, s, u // NT - 1)

            pe.wait_ge(consts, 32)
            for j in range(NT):
                last = pe.transpose(ps_out[:, j * P:(j + 1) * P], ident[:, :], ident[:, :])
            for n in range(2):
                pe.wait_ge(r_loaded[n], 16)
                pe.wait_ge(qv_halved, 2 * (n + 1))
                for u in range(TG):
                    wide_tile(n, n, u)
            pe.wait_ge(loaded[0], 48)
            content_tile(0, 0, 0)
            content_tile(0, 0, 1)
            steps(step, pe)
            value_head(NI - 1, 1, G - 1)

        @block.scalar
        def _(act):
            def copy_wide(n, s, u):
                act.wait_ge(wide_ps, TG * n + u + 1)
                act.activation(wide[:, s, u, 0:L], ps_wide[u % 2][:, :], ACT.Copy).then_inc(wide_sb, 1)

            def copy_tail(s):
                act.activation(wide[:, s, :, L:W], ps_tail[:, 0:TG * HW].rearrange("p (u w) -> p u w", w=HW),
                               ACT.Copy).then_inc(tail_sb, 1)

            def take_sums(n):
                act.wait_ge(head_done, G * (n + 1) + 2)
                act.wait_ge(stored, 64 * (n + 1))
                act.activation(osb[:, :, :].rearrange("p h i -> p (h i)"), ps_out[:, :], ACT.Copy)\
                    .then_inc(out_sb, 1)

            def step(it, s, first, left):
                n = 2 * it + s
                act.wait_ge(skewed[s], SKEW * (it + 1))
                for u in range(TG):
                    h, b = u // NT, u % NT
                    if b == 0:
                        act.wait_ge(head_done, G * n + h + 1)
                    act.wait_ge(keys_ps, TG * n + u + 1)
                    act.activation(probs[:, h % 2, :, b * P:(b + 1) * P],
                                   ps_keys[u % 2][:, :].rearrange("p (j i) -> p j i", j=NT), ACT.Exp,
                                   scale=SCALE).then_inc(exp_done, 1)
                    if left >= 2:
                        copy_wide(n + 2, s, u)
                    if u == 2 and not first:
                        take_sums(n - 1)
                if left >= 2:
                    copy_tail(s)

            act.sem_inc(exp_done, 2)
            act.sem_inc(out_sb, 1)
            for n in range(2):
                for u in range(TG):
                    copy_wide(n, n, u)
                copy_tail(n)
            steps(step, act)
            take_sums(NI - 1)

        @block.vector
        def _(dve):
            def step(it, s, first, left):
                n = 2 * it + s
                dve.wait_ge(skewed[s], SKEW * (it + 1))
                for u in range(TG):
                    dve.wait_ge(ac_ps, TG * n + u + 1)
                    dve.sem_inc(marks, 1)
                    dve.tensor_tensor_reduce(out=shifted[:, s, u, :], in0=ps_ac[u % 2][:, :],
                                             in1=shifted[:, s, u, :], scale=1.0, scalar=LOWEST,
                                             op0=ALU.add, op1=ALU.max, accum_out=mx[:, u:u + 1])\
                        .then_inc(ac_used, 1)
                    take_maximum(n, s, u)

            def take_maximum(n, s, u):
                dve.wait_ge(ac_used, TG * n + u + 3)
                dve.tensor_scalar(shifted[:, s, u, :], shifted[:, s, u, :], mx[:, u:u + 1], None,
                                  ALU.subtract).then_inc(s_ready, 1)

            for stack in (qv_here, qv_next, r, qu, k):
                dve.memset(stack[:, :, :, :].rearrange("p s h t -> p (s h t)").bitcast(F32), 0.0)\
                    .then_inc(pad_set, 1)
            dve.memset(qv[:, :, :].rearrange("p h t -> p (h t)").bitcast(F32), 0.0).then_inc(pad_set, 1)
            dve.wait_ge(consts, 32)
            dve.tensor_copy(half[:, :], shifted[0:2 * SK, 0, 0, :]).then_inc(half_set, 1)
            dve.sem_inc(head_done, 2)
            dve.sem_inc(ac_used, 2)
            steps(step, dve)


def program(nc, x, w_qkvT, w_fcT, b_fc, gamma, beta, ln1_scale, ln1_shift, wq, wk, wv, wo, bo, ln2_scale,
            ln2_shift, gate_w, w1, w2, w3, rel_wqT, rel_wkT, rel_wvT, rel_wrT, u_bias, v_bias, u1T, v1, b1, u2,
            v2, b2, ident, mask, maskT, iota, positions, half, out):
    def dram(name, shape, dt=F32):
        return nc.dram_tensor(name, shape, dt, kind="Internal").ap()

    tokens = (NB, P, NT, P)
    x1, z1, base, z2, x2, x3 = (dram(name, tokens) for name in ("x1", "z1", "base", "z2", "x2", "x3"))
    stacks = [dram(f"stack{i}", (NB, SK, H, L), BF16) for i in range(5)]
    v9 = [dram(f"v9_{i}", (NB, P, NT, H * VW)) for i in range(2)]
    sums = [dram(f"sums{i}", (NI, G, VW, L)) for i in range(2)]
    r_stack = dram("r_stack", (2 * SK, H, 2 * L + HW), BF16)

    phase_attention(nc, x, w_qkvT, w_fcT, b_fc, gamma, beta, ident, x1, z1)
    phase_project(nc, z1, ln1_scale, ln1_shift, [wq, wk, wv], [None, None], [TERMS_Q, TERMS_K], ident,
                  stacks[0:2], v9[0], "b")
    phase_causal(nc, stacks[0], stacks[1], v9[0], mask, maskT, ident, sums[0])
    phase_merge(nc, sums[0], x1, wo, bo, base, z2, "m")
    phase_experts(nc, z2, base, ln2_scale, ln2_shift, gate_w, w1, w2, w3, iota, ident, x2)
    phase_positions(nc, rel_wrT, positions, r_stack)
    phase_project(nc, x2, None, None, [rel_wqT, rel_wqT, rel_wkT, rel_wvT], [u_bias, v_bias, None],
                  [TERMS_Q, TERMS_Q, TERMS_K], ident, stacks[2:5], v9[1], "d")
    phase_relative(nc, stacks[2], stacks[3], stacks[4], v9[1], r_stack, half, ident, sums[1])
    phase_merge(nc, sums[1], x2, ident, None, None, x3, "n")
    phase_last(nc, x3, u1T, v1, b1, u2, v2, b2, ident, out)


_PLAIN = ("L0_attn_x", "L0_attn_b_fc", "L0_attn_gamma", "L0_attn_beta", "L0_ffn_ln1_scale", "L0_ffn_ln1_shift",
          "L0_ffn_wq", "L0_ffn_wk", "L0_ffn_wv", "L0_ffn_wo", "L0_ffn_bo", "L0_ffn_ln2_scale",
          "L0_ffn_ln2_shift", "L0_ffn_gate_w", "L0_ffn_w1", "L0_ffn_w2", "L0_ffn_w3", "L1_ffn_V1",
          "L1_ffn_U2", "L1_ffn_V2", "L1_ffn_b2")
_TURNED = ("L0_attn_w_qkv", "L0_attn_w_fc", "L1_attn_Wq", "L1_attn_Wk", "L1_attn_Wv", "L1_attn_Wr",
           "L1_ffn_U1")
_FLAT = ("L1_attn_u_bias", "L1_attn_v_bias")
_ORDER = ("L0_attn_x", "L0_attn_w_qkv", "L0_attn_w_fc", "L0_attn_b_fc", "L0_attn_gamma", "L0_attn_beta",
          "L0_ffn_ln1_scale", "L0_ffn_ln1_shift", "L0_ffn_wq", "L0_ffn_wk", "L0_ffn_wv", "L0_ffn_wo",
          "L0_ffn_bo", "L0_ffn_ln2_scale", "L0_ffn_ln2_shift", "L0_ffn_gate_w", "L0_ffn_w1", "L0_ffn_w2",
          "L0_ffn_w3", "L1_attn_Wq", "L1_attn_Wk", "L1_attn_Wv", "L1_attn_Wr", "L1_attn_u_bias",
          "L1_attn_v_bias", "L1_ffn_U1", "L1_ffn_V1", "L1_ffn_b1", "L1_ffn_U2", "L1_ffn_V2", "L1_ffn_b2",
          "ident", "mask", "maskT", "iota", "positions", "half")


def constants():
    import numpy as np

    i = np.arange(P)
    mask = np.where(i[None, :] > i[:, None], np.float32(BIG), np.float32(0))
    freq = (np.float32(1) / np.float32(10000) ** (np.arange(0, P, 2, dtype=np.float32) / np.float32(P)))
    angle = np.arange(-(L - 1), L, dtype=np.float32)[:, None] * freq.astype(np.float32)[None, :]
    r = np.zeros((2 * L - 1, P), np.float32)
    r[:, 0::2] = np.sin(angle)
    r[:, 1::2] = np.cos(angle)
    rows = np.zeros((2 * L, P), np.float32)
    rows[0:L] = r[L - 1:]
    rows[L + 1:] = r[:L - 1]
    upper = np.arange(L) % (2 * HW) >= HW
    half = np.where(np.arange(2 * SK)[:, None] >= SK, upper, ~upper).astype(np.float32)
    return {"ident": np.eye(P, dtype=np.float32), "mask": mask, "maskT": np.ascontiguousarray(mask.T),
            "iota": np.arange(NE, dtype=np.float32), "positions": np.ascontiguousarray(rows.T),
            "half": half}


def kernel(**inputs):
    import numpy as _np
    import concourse.bacc as _bacc
    from concourse import mybir as _mybir
    from concourse.bass_utils import run_bass_kernel_spmd as _run

    laid = dict(constants())
    for name in _PLAIN:
        laid[name] = _np.ascontiguousarray(inputs[name])
    for name in _TURNED:
        laid[name] = _np.ascontiguousarray(_np.asarray(inputs[name]).T)
    for name in _FLAT:
        laid[name] = _np.ascontiguousarray(inputs[name]).reshape(P)
    laid["L1_ffn_b1"] = _np.ascontiguousarray(_np.asarray(inputs["L1_ffn_b1"]).reshape(FF // P, P).T)

    nc = _bacc.Bacc("TRN2", target_bir_lowering=False, num_devices=1)
    arrays, args = {}, []
    for name in _ORDER:
        a = laid[name]
        arrays[f"in_{name}_dram"] = a
        args.append(nc.dram_tensor(f"in_{name}_dram", a.shape, _mybir.dt.from_np(a.dtype),
                                   kind="ExternalInput").ap())
    args.append(nc.dram_tensor("out_0_dram", (NB, L, P), F32, kind="ExternalOutput").ap())
    program(nc, *args)
    r = _run(nc, [arrays], core_ids=[0])
    return r.results[0]["out_0_dram"]
```

```python
from contextlib import ExitStack

import concourse.bass as bass
from concourse import mybir

F32 = mybir.dt.float32
BF16 = mybir.dt.bfloat16
U32 = mybir.dt.uint32
F32R = mybir.dt.float32r
ACT = mybir.ActivationFunctionType
ALU = mybir.AluOpType
AX_X = mybir.AxisListType.X

P = 128
NB = 8
L = 512
NT = L // P
H = 16
DH = 8
G = 4
NG = H // G
NI = NB * NG
VW = DH + 1
TERMS_Q = (0, 0, 0, 1, 1, 2)
TERMS_K = (0, 1, 2, 0, 1, 0)
SK = DH * len(TERMS_Q)
NE = 8
HID = 256
FF = 512
RANK = 32
EPS = 1e-5
HW = 16
BIG = -1e30


class Chain:

    def __init__(self, eng, sem, n, per):
        self.eng, self.sem, self.n, self.per, self.k = eng, sem, n, per, 0

    def step(self, ins):
        self.k += 1
        ins.then_inc(self.sem, 1)
        self.eng.wait_ge(self.sem, self.n * self.per + self.k)

    def done(self):
        assert self.k == self.per, (self.k, self.per)


class Semaphores:

    def __init__(self, nc, earlier=None):
        self.nc, self.all = nc, []
        self.earlier = earlier

    def new(self, name):
        self.all.append(self.nc.alloc_semaphore(name))
        return self.all[-1]

    def block(self, ctx):
        if self.earlier is not None:
            self.nc.clear_and_free_semaphores(self.earlier.all)
        return ctx.enter_context(self.nc.Block())

    def finish(self):
        self.nc.clear_and_free_semaphores(self.all)
        self.nc.all_engine_barrier()


def row_on_all(v, width=P):
    return bass.AP(tensor=v.tensor, offset=v.offset, ap=[[0, P], [1, width]])


class Norm:

    def __init__(self, ctx, nc, sems, name):
        self.stats = ctx.enter_context(nc.sbuf_tensor(name + "_stats", [P, NT, 6], F32))
        self.mv = ctx.enter_context(nc.sbuf_tensor(name + "_mv", [P, NT, 2], F32))
        self.rstd = ctx.enter_context(nc.sbuf_tensor(name + "_rstd", [P, NT], F32))
        self.var_eps = ctx.enter_context(nc.sbuf_tensor(name + "_var_eps", [P, NT], F32))
        self.consts = ctx.enter_context(nc.sbuf_tensor(name + "_consts", [P, 2, NT], F32))
        self.consts_set = sems.new(name + "_consts_set")
        self.eps_added = sems.new(name + "_eps_added")
        self.passes = sems.new(name + "_passes")
        self.stats_ready = sems.new(name + "_stats_ready")
        self.var_ready = sems.new(name + "_var_ready")
        self.rstd_ready = sems.new(name + "_rstd_ready")

    def moments(self, dve, x, count):
        for t in range(NT):
            last = dve.bn_stats(self.stats[:, t, :], x[:, t, :])
        last.then_inc(self.stats_ready, 1)
        dve.wait_ge(self.stats_ready, count)
        dve.sem_inc(self.passes, 1)
        for t in range(NT):
            last = dve.bn_aggr(self.mv[:, t, :], self.stats[:, t, :])
        last.then_inc(self.var_ready, 1)

    def root(self, pool, count):
        pool.wait_ge(self.var_ready, count)
        pool.tensor_tensor(self.var_eps[:, :], self.mv[:, :, 1], self.consts[:, 0, :], ALU.add)\
            .then_inc(self.eps_added, 1)
        pool.wait_ge(self.eps_added, count)
        pool.tensor_tensor(self.rstd[:, :], self.var_eps[:, :], self.consts[:, 1, :], ALU.pow)\
            .then_inc(self.rstd_ready, 1)

    def constants(self, pool):
        pool.memset(self.consts[:, 0, :], EPS).then_inc(self.consts_set, 1)
        pool.memset(self.consts[:, 1, :], -0.5).then_inc(self.consts_set, 1)
        pool.wait_ge(self.consts_set, 2)

    def apply(self, dve, out, x, count):
        dve.wait_ge(self.rstd_ready, count)
        for t in range(NT):
            last = dve.tensor_scalar(out[:, t, :], x[:, t, :], self.mv[:, t, 0:1], self.rstd[:, t:t + 1],
                                     ALU.subtract, ALU.mult)
        return last


def phase_attention(nc, sems, x_in, w_qkvT, w_fcT, b_fc, gamma, beta, ident_in, x1_out, z1_out):
    SCALE = P ** -0.5
    with ExitStack() as ctx:
        def sb(name, shape, dt=F32):
            return ctx.enter_context(nc.sbuf_tensor("a_" + name, shape, dt))


        def sem(name):
            return sems.new("a_" + name)

        wqkv = sb("wqkv", [P, 3, P])
        wfc = sb("wfc", [P, P])
        ident = sb("ident", [P, P])
        bfc = sb("bfc", [P, P])
        gam = sb("gam", [P, P])
        bet = sb("bet", [P, P])
        x = sb("x", [P, 2, NT, P])
        xb = sb("xb", [P, 2, NT, P])
        xbeta = sb("xbeta", [P, 2, NT, P])
        xT = sb("xT", [P, L])
        qT = sb("qT", [P, 2, L])
        kT = sb("kT", [P, 2, L])
        xsum = sb("xsum", [P, 2])
        vsum = sb("vsum", [P, P])
        mx = sb("mx", [P, NT])
        negm = sb("negm", [P, NT])
        rowsum = sb("rowsum", [P, NT])
        rinv = sb("rinv", [P, NT])
        attsum = sb("attsum", [P, 2, NT])
        probs = sb("probs", [P, 2, NT, L])
        att = sb("att", [P, 2, L])
        h = sb("h", [P, NT, P])
        h2 = sb("h2", [P, NT, P])
        x1 = sb("x1", [P, 2, NT, P])
        z1 = sb("z1", [P, 2, NT, P])
        norm = Norm(ctx, nc, sems, "a_norm")
        ps = [ctx.enter_context(nc.psum_tensor(f"a_ps{i}", [P, 512], F32)) for i in range(8)]

        consts = sem("consts")
        x_in_s = [sem("x_loaded0"), sem("x_loaded1")]
        x_free = sem("x_free")
        xb_ready = sem("xb_ready")
        xT_ps = sem("xT_ps")
        xT_sb = sem("xT_sb")
        qk_ps = sem("qk_ps")
        v_ps = sem("v_ps")
        q_sb = sem("q_sb")
        k_sb = sem("k_sb")
        vsum_sb = sem("vsum_sb")
        s_ps = sem("scores_ps")
        negm_ready = sem("negm_ready")
        p_sb = sem("probs_sb")
        rinv_ready = sem("rinv_ready")
        att_done = sem("att_done")
        fc_ps = sem("fc_ps")
        fc_read = sem("fc_read")
        chain_s = sem("dve_chain")
        max_ready = sem("max_ready")
        marks = sem("marks")
        x1_ready = sem("x1_ready")
        z1_ready = sem("z1_ready")
        stored = [sem("stored0"), sem("stored1")]
        block = sems.block(ctx)

        def steps(step, eng):
            with eng.Fori(0, NB // 2 - 1) as it:
                for s in range(2):
                    step(it, s, True)
            for s in range(2):
                step(NB // 2 - 1, s, s == 0)

        @block.sync
        def _(sp):
            sp.dma_start(wqkv[:, :, :], w_qkvT.rearrange("d (c e) -> d c e", c=3)).then_inc(consts, 16)
            sp.dma_start(wfc[:, :], w_fcT).then_inc(consts, 16)
            sp.dma_start(ident[:, :], ident_in).then_inc(consts, 16)
            sp.dma_start(bfc[:, :], row_on_all(b_fc)).then_inc(consts, 16)
            sp.dma_start(gam[:, :], row_on_all(gamma)).then_inc(consts, 16)
            sp.dma_start(bet[:, :], row_on_all(beta)).then_inc(consts, 16)
            for s in range(2):
                sp.dma_start(x[:, s, :, :], x_in[s].rearrange("(t p) d -> p t d", p=P)).then_inc(x_in_s[s], 16)
            for s in range(2):
                sp.sem_inc(stored[s], 32)
            with sp.Fori(0, NB // 2) as it:
                for s in range(2):
                    n = 2 * it + s
                    sp.wait_ge(x_free, n + 1)
                    sp.dma_start(x[:, s, :, :], x_in[(n + 2) % NB].rearrange("(t p) d -> p t d", p=P))\
                        .then_inc(x_in_s[s], 16)
                    sp.wait_ge(x1_ready, n + 1)
                    sp.dma_start(x1_out[n], x1[:, s, :, :]).then_inc(stored[s], 16)
                    sp.wait_ge(z1_ready, n + 1)
                    sp.dma_start(z1_out[n], z1[:, s, :, :]).then_inc(stored[s], 16)
            for s in range(2):
                sp.wait_ge(stored[s], 32 * (NB // 2 + 1))
                sp.wait_ge(x_in_s[s], 16 * (NB // 2 + 1))

        @block.gpsimd
        def _(pool):
            def add_bfc(n, s, loads):
                pool.wait_ge(x_in_s[s], 16 * loads)
                pool.tensor_tensor(xb[:, s, :, :], x[:, s, :, :], bfc[:, :].unsqueeze(1).broadcast_to([P, NT, P]),
                                   ALU.add).then_inc(xb_ready, 1)

            def add_beta(n, s):
                pool.wait_ge(xT_ps, n + 1)
                pool.tensor_tensor(xbeta[:, s, :, :], x[:, s, :, :],
                                   bet[:, :].unsqueeze(1).broadcast_to([P, NT, P]), ALU.add).then_inc(x_free, 1)

            def step(it, s, ahead):
                n = 2 * it + s
                norm.root(pool, 3 * n + 1)
                if ahead:
                    add_bfc(n + 1, 1 - s, it + 1 + s)
                norm.root(pool, 3 * n + 2)
                norm.root(pool, 3 * n + 3)
                if ahead:
                    add_beta(n + 1, 1 - s)

            norm.constants(pool)
            pool.wait_ge(consts, 96)
            add_bfc(0, 0, 1)
            add_beta(0, 0)
            steps(step, pool)

        @block.tensor
        def _(pe):
            def front(n, s, loads):
                pe.wait_ge(x_in_s[s], 16 * loads)
                for t in range(NT):
                    last = pe.transpose(ps[0][:, t * P:(t + 1) * P], x[:, s, t, :], ident[:, :])
                last.then_inc(xT_ps, 1)
                pe.wait_ge(xT_sb, n + 1)
                pe.matmul(ps[1][:, :], wqkv[:, 0, :], xT[:, :], start=True, stop=True).then_inc(qk_ps, 1)
                pe.matmul(ps[2][:, :], wqkv[:, 1, :], xT[:, :], start=True, stop=True).then_inc(qk_ps, 1)

            def step(it, s, ahead):
                n = 2 * it + s
                pe.wait_ge(q_sb, n + 1)
                pe.wait_ge(k_sb, n + 1)
                for i in range(NT):
                    pe.wait_ge(p_sb, NT * n + i + 1)
                    pe.matmul(ps[4 + i][:, :], qT[:, s, i * P:(i + 1) * P], kT[:, s, :], start=True, stop=True)\
                        .then_inc(s_ps, 1)
                if ahead:
                    front(n + 1, 1 - s, it + 1 + s)
                pe.wait_ge(fc_read, n + 1)
                pe.matmul(ps[3][:, 0:1], wqkv[:, 2, :], xsum[:, s:s + 1], start=True, stop=True).then_inc(v_ps, 1)
                pe.wait_ge(vsum_sb, n + 1)
                pe.matmul(ps[3][:, P:2 * P], vsum[:, :], wfc[:, :], start=True, stop=True).then_inc(fc_ps, 1)

            pe.wait_ge(consts, 96)
            front(0, 0, 1)
            steps(step, pe)

        @block.scalar
        def _(act):
            def front(n, s):
                act.wait_ge(xT_ps, n + 1)
                act.activation(xT[:, :], ps[0][:, :], ACT.Copy, accum_out=xsum[:, s:s + 1]).then_inc(xT_sb, 1)
                act.wait_ge(qk_ps, 2 * n + 1)
                act.activation(qT[:, s, :], ps[1][:, :], ACT.Copy).then_inc(q_sb, 1)
                act.wait_ge(qk_ps, 2 * n + 2)
                act.activation(kT[:, s, :], ps[2][:, :], ACT.Copy).then_inc(k_sb, 1)

            def step(it, s, ahead):
                n = 2 * it + s
                for i in range(NT):
                    act.wait_ge(negm_ready, NT * n + i + 1)
                    act.activation(probs[:, s, i, :], ps[4 + i][:, :], ACT.Exp, bias=negm[:, i:i + 1],
                                   scale=SCALE, accum_out=rowsum[:, i:i + 1]).then_inc(p_sb, 1)
                if ahead:
                    front(n + 1, 1 - s)
                act.wait_ge(v_ps, n + 1)
                act.activation(vsum[:, :], ps[3][:, 0:1].broadcast_to([P, P]), ACT.Copy).then_inc(vsum_sb, 1)
                act.wait_ge(rinv_ready, n + 1)
                for i in range(NT):
                    act.wait_ge(att_done, NT * n + i + 1)
                    act.activation(att[:, i % 2, :], probs[:, s, i, :], ACT.Copy, scale=rinv[:, i:i + 1],
                                   accum_out=attsum[:, s, i:i + 1]).then_inc(att_done, 1)

            act.sem_inc(p_sb, NT)
            act.sem_inc(att_done, 2)
            front(0, 0)
            steps(step, act)

        @block.vector
        def _(dve):
            def maxima(n, i):
                dve.wait_ge(s_ps, NT * n + i + 1)
                dve.tensor_reduce(mx[:, i:i + 1], ps[4 + i][:, :], AX_X, ALU.max).then_inc(max_ready, 1)
                dve.wait_ge(max_ready, NT * n + i + 1)
                dve.tensor_scalar(negm[:, i:i + 1], mx[:, i:i + 1], -SCALE, None, ALU.mult)\
                    .then_inc(negm_ready, 1)

            def sequence(it, s, ahead):
                n = 2 * it + s
                chain = Chain(dve, chain_s, n, 4)
                dve.wait_ge(p_sb, NT * (n + 2))
                dve.reciprocal(rinv[:, :], rowsum[:, :]).then_inc(rinv_ready, 1)
                if ahead:
                    maxima(n + 1, 0)
                    maxima(n + 1, 1)
                dve.wait_ge(fc_ps, n + 1)
                dve.wait_ge(xb_ready, n + 1)
                dve.sem_inc(marks, 1)
                dve.wait_ge(att_done, NT * (n + 1) + 2)
                for t in range(NT):
                    last = dve.scalar_tensor_tensor(out=h[:, t, :], in0=ps[3][:, P:2 * P],
                                                    scalar=attsum[:, s, t:t + 1], in1=xb[:, s, t, :],
                                                    op0=ALU.mult, op1=ALU.add)
                chain.step(last)
                dve.sem_inc(fc_read, 1)
                norm.moments(dve, h, 3 * n + 1)
                if ahead:
                    maxima(n + 1, 2)
                    maxima(n + 1, 3)
                chain.step(norm.apply(dve, h2, h, 3 * n + 1))
                gm = gam[:, :].unsqueeze(1).broadcast_to([P, NT, P])
                chain.step(dve.tensor_tensor(h[:, :, :], h2[:, :, :], gm, ALU.mult))
                dve.wait_ge(x_free, n + 1)
                chain.step(dve.tensor_tensor(h2[:, :, :], h[:, :, :], xbeta[:, s, :, :], ALU.add))
                norm.moments(dve, h2, 3 * n + 2)
                dve.wait_ge(stored[s], 32 * it + 32)
                norm.apply(dve, x1[:, s, :, :], h2, 3 * n + 2).then_inc(x1_ready, 1)
                dve.wait_ge(x1_ready, n + 1)
                norm.moments(dve, x1[:, s, :, :], 3 * n + 3)
                norm.apply(dve, z1[:, s, :, :], x1[:, s, :, :], 3 * n + 3).then_inc(z1_ready, 1)
                chain.done()

            dve.sem_inc(fc_read, 1)
            dve.wait_ge(consts, 96)
            for i in range(NT):
                maxima(0, i)
            steps(sequence, dve)


def phase_project(nc, sems, z_in, scale, shift, w_in, biases, tables, ident_in, stacks_out, v9_out, name,
                  positions=None):
    NC = len(w_in) - 1
    with ExitStack() as ctx:
        def sb(nm, shape, dt=F32):
            return ctx.enter_context(nc.sbuf_tensor(f"{name}_{nm}", shape, dt))


        def sem(nm):
            return sems.new(f"{name}_{nm}")

        w = sb("w", [P, NC + 1, P])
        sc = sb("scale", [P, 2])
        bias = sb("bias", [P, NC])
        ident = sb("ident", [P, P])
        z = sb("z", [P, 2, NT, P])
        zT = sb("zT", [P, L])
        part1 = sb("part1", [P, 2, NC, L], BF16)
        part2 = sb("part2", [P, 2, NC, L], BF16)
        part3 = sb("part3", [P, 2, NC, L], BF16)
        rest1 = sb("rest1", [P, NC, L])
        v9 = sb("v9", [P, 2, NT, H * VW])
        ps_zT = ctx.enter_context(nc.psum_tensor(f"{name}_ps_zT", [P, L], F32))
        ps_c = [ctx.enter_context(nc.psum_tensor(f"{name}_ps_c{c}", [P, L], F32)) for c in range(NC)]
        ps_v = ctx.enter_context(nc.psum_tensor(f"{name}_ps_v", [P, NT * P], F32))

        if positions is not None:
            w_rT, r_in, r_stack = positions
            wr = sb("wr", [P, P])
            r = sb("r", [P, 2, L])
            r_part = [sb(f"r_part{i}", [P, HW + 2 * (L + HW)], BF16) for i in range(3)]
            r_rest = sb("r_rest", [P, 2, L])
            ps_r = ctx.enter_context(nc.psum_tensor(f"{name}_ps_r", [P, 2, L], F32))
            r_loaded = sem("r_loaded")
            r_ps = sem("r_ps")
            r_zeroed = sem("r_zeroed")
            r_split = sem("r_split")
            r_stored = sem("r_stored")
        consts = sem("consts")
        z_loaded = [sem("z_loaded0"), sem("z_loaded1")]
        zT_ps = sem("zT_ps")
        zT_sb = sem("zT_sb")
        c_ps = sem("operands_ps")
        v_ps = sem("v_ps")
        v_sb = sem("v_sb")
        ones_set = sem("ones_set")
        part1_ready = sem("part1_ready")
        rest1_ready = sem("rest1_ready")
        part2_ready = sem("part2_ready")
        part3_ready = sem("part3_ready")
        stored = [sem("stored0"), sem("stored1")]
        pool_stored = sem("pool_stored")
        pool_slots = sem("pool_slots")
        v_stored = [sem("v_stored0"), sem("v_stored1")]
        n_const = 16 * (NC + 2 + (2 if scale is not None else 0) + sum(b is not None for b in biases))
        n_set = 1 + sum(b is None for b in biases)
        NSP = NC - 1
        STORES = 16 * len(TERMS_Q) * NSP
        POOL_STORES = 16 * len(TERMS_Q)
        block = sems.block(ctx)

        def term_stores(eng, n, s, c, signal):
            parts = (part1, part2, part3)
            for t, which in enumerate(tables[c]):
                dst = stacks_out[c][n, DH * t:DH * t + DH, :, :].rearrange("d h n -> h d n")
                eng.dma_start(dst, parts[which][:, s, c, :]).then_inc(signal, 16)

        @block.sync
        def _(sp):
            for c in range(NC + 1):
                sp.dma_start(w[:, c, :], w_in[c]).then_inc(consts, 16)
            sp.dma_start(ident[:, :], ident_in).then_inc(consts, 16)
            if scale is not None:
                sp.dma_start(sc[:, 0:1], scale.rearrange("(d o) -> d o", o=1)).then_inc(consts, 16)
                sp.dma_start(sc[:, 1:2], shift.rearrange("(d o) -> d o", o=1)).then_inc(consts, 16)
            for c in range(NC):
                if biases[c] is not None:
                    sp.dma_start(bias[:, c:c + 1], biases[c].rearrange("(d o) -> d o", o=1)).then_inc(consts, 16)
            for s in range(2):
                sp.dma_start(z[:, s, :, :], z_in[s]).then_inc(z_loaded[s], 16)
                sp.sem_inc(stored[s], STORES)
                sp.sem_inc(v_stored[s], 16)
            if positions is not None:
                sp.dma_start(wr[:, :], w_rT).then_inc(r_loaded, 16)
                sp.dma_start(r[:, :, :].rearrange("p a t -> p (a t)"), r_in).then_inc(r_loaded, 16)
            with sp.Fori(0, NB // 2) as it:
                for s in range(2):
                    n = 2 * it + s
                    sp.wait_ge(zT_ps, n + 1)
                    sp.dma_start(z[:, s, :, :], z_in[(n + 2) % NB]).then_inc(z_loaded[s], 16)
                    sp.wait_ge(v_sb, n + 1)
                    sp.dma_start(v9_out[n], v9[:, s, :, :]).then_inc(v_stored[s], 16)
                    for c in range(NSP):
                        sp.wait_ge(part3_ready, NC * (n + 1) + c + 1)
                        term_stores(sp, n, s, c, stored[s])
            for s in range(2):
                sp.wait_ge(stored[s], STORES * (NB // 2 + 1))
                sp.wait_ge(v_stored[s], 16 * (NB // 2 + 1))
                sp.wait_ge(z_loaded[s], 16 * (NB // 2 + 1))

        @block.gpsimd
        def _(pool):
            for c in range(NC):
                if biases[c] is None:
                    pool.memset(bias[:, c:c + 1], 0.0).then_inc(ones_set, 1)
            pool.memset(v9[:, :, :, :], 1.0).then_inc(ones_set, 1)
            pool.sem_inc(pool_slots, 2)
            if positions is not None:
                pool.wait_ge(r_zeroed, 3)
                pool.wait_ge(r_split, 5)
                for t, which in enumerate(TERMS_K):
                    for row, col in ((DH * t, HW), (SK + DH * t, 0)):
                        pool.dma_start(r_stack[row:row + DH, :, :].rearrange("d h n -> h d n"),
                                       r_part[which][:, col:col + 2 * L + HW]).then_inc(r_stored, 16)
            with pool.Fori(0, NB // 2) as it:
                for s in range(2):
                    n = 2 * it + s
                    pool.wait_ge(part3_ready, NC * (n + 2))
                    term_stores(pool, n, s, NC - 1, pool_stored)
                    pool.wait_ge(pool_stored, POOL_STORES * (n + 1))
                    pool.sem_inc(pool_slots, 1)
            if positions is not None:
                pool.wait_ge(r_stored, 32 * len(TERMS_K))

        @block.tensor
        def _(pe):
            pe.wait_ge(consts, n_const)
            if positions is not None:
                pe.wait_ge(r_loaded, 32)
                for a in range(2):
                    last = pe.matmul(ps_r[:, a, :], wr[:, :], r[:, a, :], start=True, stop=True)
                last.then_inc(r_ps, 1)
            with pe.Fori(0, NB // 2) as it:
                for s in range(2):
                    n = 2 * it + s
                    pe.wait_ge(z_loaded[s], 16 * it + 16)
                    for t in range(NT):
                        last = pe.transpose(ps_zT[:, t * P:(t + 1) * P], z[:, s, t, :], ident[:, :])
                    last.then_inc(zT_ps, 1)
                    pe.wait_ge(zT_sb, n + 1)
                    for c in range(NC):
                        pe.wait_ge(rest1_ready, NC * n + c + 1)
                        pe.matmul(ps_c[c][:, :], w[:, c, :], zT[:, :], start=True, stop=True).then_inc(c_ps, 1)
                    for t in range(NT):
                        last = pe.matmul(ps_v[:, t * P:(t + 1) * P], zT[:, t * P:(t + 1) * P], w[:, NC, :],
                                         start=True, stop=True)
                    last.then_inc(v_ps, 1)

        @block.scalar
        def _(act):
            act.wait_ge(consts, n_const)
            act.wait_ge(ones_set, n_set)
            with act.Fori(0, NB // 2) as it:
                for s in range(2):
                    n = 2 * it + s
                    act.wait_ge(zT_ps, n + 1)
                    if scale is not None:
                        act.activation(zT[:, :], ps_zT[:, :], ACT.Identity, bias=sc[:, 1:2], scale=sc[:, 0:1])\
                            .then_inc(zT_sb, 1)
                    else:
                        act.activation(zT[:, :], ps_zT[:, :], ACT.Copy).then_inc(zT_sb, 1)
                    act.wait_ge(stored[s], STORES * (it + 1))
                    act.wait_ge(pool_slots, n + 1)
                    for c in range(NC):
                        act.wait_ge(c_ps, NC * n + c + 1)
                        act.activation(part1[:, s, c, :], ps_c[c][:, :], ACT.Identity, bias=bias[:, c:c + 1])\
                            .then_inc(part1_ready, 1)
                    act.wait_ge(v_ps, n + 1)
                    act.wait_ge(v_stored[s], 16 * (it + 1))
                    act.activation(v9[:, s, :, :].rearrange("p t (h v) -> p (t h) v", v=VW)[:, :, 0:DH],
                                   ps_v[:, :].rearrange("p (g d) -> p g d", d=DH), ACT.Copy).then_inc(v_sb, 1)
                    for c in range(NC):
                        act.wait_ge(rest1_ready, NC * (n + 1) + c + 1)
                        act.activation(part2[:, s, c, :], rest1[:, c, :], ACT.Copy).then_inc(part2_ready, 1)

        @block.vector
        def _(dve):
            dve.sem_inc(rest1_ready, NC)
            dve.sem_inc(part3_ready, NC)
            if positions is not None:
                def halves(part):
                    return part[:, HW:].rearrange("p (a t) -> p a t", a=2)[:, :, 0:L]

                for p in r_part:
                    dve.memset(p[:, :].bitcast(F32), 0.0).then_inc(r_zeroed, 1)
                dve.wait_ge(r_zeroed, 3)
                dve.wait_ge(r_ps, 1)
                dve.tensor_copy(halves(r_part[0]), ps_r[:, :, :]).then_inc(r_split, 1)
                dve.wait_ge(r_split, 1)
                dve.tensor_tensor(r_rest[:, :, :], ps_r[:, :, :], halves(r_part[0]), ALU.subtract)\
                    .then_inc(r_split, 1)
                dve.wait_ge(r_split, 2)
                dve.tensor_copy(halves(r_part[1]), r_rest[:, :, :]).then_inc(r_split, 1)
                dve.wait_ge(r_split, 3)
                dve.tensor_tensor(r_rest[:, :, :], r_rest[:, :, :], halves(r_part[1]), ALU.subtract)\
                    .then_inc(r_split, 1)
                dve.wait_ge(r_split, 4)
                dve.tensor_copy(halves(r_part[2]), r_rest[:, :, :]).then_inc(r_split, 1)
            dve.wait_ge(consts, n_const)
            dve.wait_ge(ones_set, n_set)
            with dve.Fori(0, NB // 2) as it:
                for s in range(2):
                    n = 2 * it + s
                    dve.wait_ge(part3_ready, NC * (n + 1))
                    for c in range(NC):
                        dve.wait_ge(part1_ready, NC * n + c + 1)
                        dve.scalar_tensor_tensor(out=rest1[:, c, :], in0=ps_c[c][:, :], scalar=bias[:, c:c + 1],
                                                 in1=part1[:, s, c, :], op0=ALU.add, op1=ALU.subtract)\
                            .then_inc(rest1_ready, 1)
                    for c in range(NC):
                        dve.wait_ge(part2_ready, NC * n + c + 1)
                        dve.tensor_tensor(part3[:, s, c, :], rest1[:, c, :], part2[:, s, c, :], ALU.subtract)\
                            .then_inc(part3_ready, 1)


def phase_causal(nc, sems, q_stacks, k_stacks, v9_in, mask_in, maskT_in, ident_in, ctx_out):
    SCALE = DH ** -0.5
    M0 = 64
    TILES = ((0,), (1, 3), (2,))
    OFF = {0: 0, 1: 512, 3: 896, 2: 1024}
    WIDTH = {0: 512, 1: 384, 2: 256, 3: 128}
    NTILE = len(TILES)
    SLOTS = 4
    ROUNDS = NI // SLOTS
    with ExitStack() as ctx:
        def sb(name, shape, dt=F32):
            return ctx.enter_context(nc.sbuf_tensor("c_" + name, shape, dt))


        def sem(name):
            return sems.new("c_" + name)

        def bank(name):
            return ctx.enter_context(nc.psum_tensor("c_" + name, [P, 512], F32))

        q = sb("q", [P, SLOTS, G, L], BF16)
        k = sb("k", [P, SLOTS, G, L], BF16)
        v9 = sb("v9", [P, SLOTS, NT, G * VW])
        mask32 = sb("mask32", [P, P])
        maskT32 = sb("maskT32", [P, P])
        mask = sb("mask", [P, P], BF16)
        maskT = sb("maskT", [P, P], BF16)
        identb = sb("identb", [P, P], BF16)
        ident = sb("ident", [P, P])
        zeros = sb("zeros", [P, 512], BF16)
        mx = sb("mx", [P, 2, G * NT])
        mrow = sb("mrow", [G * NT, 2, 2, P], BF16)
        probs = sb("probs", [P, 2, 1280])
        osb = sb("osb", [P, 2, G, P])
        ps_rows = [bank(f"ps_rows{i}") for i in range(3)]
        ps_m = bank("ps_m")
        ps_keys = [bank(f"ps_keys{i}") for i in range(NTILE)]
        ps_out = bank("ps_out")

        consts = sem("consts")
        preset = sem("preset")
        minus_ones = sem("minus_ones")
        loaded = [sem(f"loaded{i}") for i in range(SLOTS)]
        rows_ps = sem("rows_ps")
        max_read = sem("max_read")
        m_ps = sem("m_ps")
        m_first = sem("m_first")
        m_split = sem("m_split")
        m_loaded = [sem(f"m_loaded{i}") for i in range(SLOTS)]
        keys_ps = sem("keys_ps")
        exp_done = sem("exp_done")
        head_done = sem("head_done")
        out_sb = sem("out_sb")
        stored = [sem("stored0"), sem("stored1")]
        block = sems.block(ctx)

        def load(eng, n, s):
            b, g = n // NG, n % NG
            eng.dma_start(q[0:SK, s, :, :], q_stacks.rearrange("b r (g h) t -> b g r h t", h=G)[b, g])\
                .then_inc(loaded[s], 16)
            eng.dma_start(k[0:SK, s, :, :], k_stacks.rearrange("b r (g h) t -> b g r h t", h=G)[b, g])\
                .then_inc(loaded[s], 16)
            eng.dma_start(v9[:, s, :, :], v9_in.rearrange("b p t (g v) -> b g p t v", g=NG)[b, g])\
                .then_inc(loaded[s], 16)

        def load_maxima(eng, s):
            for r in range(2):
                eng.dma_start(q[M0 + r:M0 + r + 1, s, :, :], mrow[:, s % 2, r, :]).then_inc(m_loaded[s], 16)

        def steps(step, eng):
            with eng.Fori(0, ROUNDS - 1) as it:
                for s in range(SLOTS):
                    step(it, s, SLOTS)
            for s in range(SLOTS):
                step(ROUNDS - 1, s, SLOTS - 1 - s)

        @block.sync
        def _(sp):
            def step(it, s, left):
                n = SLOTS * it + s
                if left >= 1:
                    sp.wait_ge(m_split, n + 2)
                    load_maxima(sp, (s + 1) % SLOTS)
                if left >= 3:
                    sp.wait_ge(head_done, G * n + 2)
                    load(sp, n + 3, (s + 3) % SLOTS)
                sp.wait_ge(out_sb, n + 2)
                for b in range(NT):
                    sp.dma_start(ctx_out[n, :, :, b * P:(b + 1) * P].rearrange("h r i -> r h i"),
                                 osb[32 * b:32 * b + VW, s % 2, :, :]).then_inc(stored[s % 2], 16)

            for dst, src in ((mask32, mask_in), (maskT32, maskT_in), (ident, ident_in)):
                sp.dma_start(dst[:, :], src).then_inc(consts, 16)
            sp.wait_ge(preset, 2)
            sp.wait_ge(minus_ones, 1)
            for s in range(SLOTS - 1):
                load(sp, s, s)
            for s in range(2):
                sp.sem_inc(stored[s], 64)
            sp.wait_ge(m_split, 1)
            load_maxima(sp, 0)
            steps(step, sp)
            for s in range(SLOTS):
                sp.wait_ge(loaded[s], 48 * ROUNDS)
                sp.wait_ge(m_loaded[s], 32 * ROUNDS)
            for s in range(2):
                sp.wait_ge(stored[s], 64 * (NI // 2 + 1))

        @block.gpsimd
        def _(pool):
            pool.wait_ge(preset, 1)
            pool.memset(k[M0:M0 + 2, :, :, :], -1.0).then_inc(minus_ones, 1)

        @block.tensor
        def _(pe):
            def row_tile(n, s, h, b):
                m = NT * h + b
                ps = ps_rows[m % 3]
                last = G * NT * n + (m - 3 if m >= 3 else m - 4 if m else -1)
                if not isinstance(last, int) or last >= 0:
                    pe.wait_ge(max_read, last + 1)
                pe.matmul(ps[:, 0:(b + 1) * P], q[0:M0, s, h, b * P:(b + 1) * P], k[0:M0, s, h, 0:(b + 1) * P],
                          start=True, stop=False)
                pe.matmul(ps[:, b * P:(b + 1) * P], identb[:, :], mask[:, :], start=False, stop=True)\
                    .then_inc(rows_ps, 1)

            def turn_maxima(n, s):
                pe.wait_ge(max_read, G * NT * (n + 1))
                pe.transpose(ps_m[0:G * NT, 0:P], mx[:, s % 2, :], ident[:, :]).then_inc(m_ps, 1)

            def key_tile(n, s, h, c):
                tile = NTILE * (G * n + h) + c
                ps = ps_keys[c]
                pe.wait_ge(exp_done, tile + 1)
                at = 0
                for j in TILES[c]:
                    pe.matmul(ps[:, at:at + WIDTH[j]], k[:, s, h, j * P:(j + 1) * P], q[:, s, h, j * P:L],
                              start=True, stop=False)
                    last = pe.matmul(ps[:, at:at + P], identb[:, :], maskT[:, :], start=False, stop=True)
                    at += WIDTH[j]
                last.then_inc(keys_ps, 1)

            def value_head(n, s, h):
                pe.wait_ge(exp_done, NTILE * (G * n + h + 2))
                if h == 0:
                    pe.wait_ge(out_sb, n + 1)
                for j in range(NT):
                    for b in range(j, NT):
                        last = pe.matmul(ps_out[32 * b:32 * b + VW, h * P:(h + 1) * P],
                                         v9[:, s, j, h * VW:(h + 1) * VW],
                                         probs[:, h % 2, OFF[j] + (b - j) * P:OFF[j] + (b - j + 1) * P],
                                         start=(j == 0), stop=(j == b), skip_group_check=True)
                last.then_inc(head_done, 1)

            def step(it, s, left):
                n = SLOTS * it + s
                s1, s2 = (s + 1) % SLOTS, (s + 2) % SLOTS
                if left >= 2:
                    pe.wait_ge(loaded[s2], 48 * (it + (s + 2) // SLOTS + 1))
                for h in range(G):
                    nxt = (n, s, h + 1) if h + 1 < G else (n + 1, s1, 0)
                    if h == G - 1 and left >= 1:
                        pe.wait_ge(m_loaded[s1], 32 * (it + (s + 1) // SLOTS + 1))
                    for b in range(NT):
                        if left >= 2:
                            row_tile(n + 2, s2, h, b)
                        if b >= 1 and (h + 1 < G or left >= 1):
                            key_tile(*nxt, b - 1)
                    if h == 0 and left >= 1:
                        turn_maxima(n + 1, s1)
                    value_head(n, s, h)

            pe.wait_ge(consts, 48)
            pe.wait_ge(preset, 6)
            pe.wait_ge(minus_ones, 1)
            pe.matmul(ps_out[:, :], zeros[:, 0:P], zeros[:, :], start=True, stop=True)
            for s in range(2):
                pe.wait_ge(loaded[s], 48)
                for h in range(G):
                    for b in range(NT):
                        row_tile(s, s, h, b)
                if s == 0:
                    turn_maxima(0, 0)
            pe.wait_ge(m_loaded[0], 32)
            for c in range(NTILE):
                key_tile(0, 0, 0, c)
            steps(step, pe)

        @block.scalar
        def _(act):
            def exponentials(n, h):
                act.wait_ge(head_done, G * n + h + 1)
                for c, blocks in enumerate(TILES):
                    width = sum(WIDTH[j] for j in blocks)
                    act.wait_ge(keys_ps, NTILE * (G * n + h) + c + 1)
                    act.activation(probs[:, h % 2, OFF[blocks[0]]:OFF[blocks[0]] + width],
                                   ps_keys[c][:, 0:width], ACT.Exp, scale=SCALE)\
                        .then_inc(exp_done, 1)

            def step(it, s, left):
                n = SLOTS * it + s
                for h in range(1, G):
                    exponentials(n, h)
                if left >= 1:
                    exponentials(n + 1, 0)
                act.wait_ge(head_done, G * (n + 1) + 2)
                act.wait_ge(stored[s % 2], 64 * (SLOTS // 2 * it + s // 2 + 1))
                act.activation(osb[:, s % 2, :, :].rearrange("p h i -> p (h i)"), ps_out[:, :], ACT.Copy)\
                    .then_inc(out_sb, 1)

            act.sem_inc(exp_done, NTILE)
            act.sem_inc(out_sb, 1)
            exponentials(0, 0)
            steps(step, act)

        @block.vector
        def _(dve):
            def maxima(n, s, m):
                dve.wait_ge(rows_ps, G * NT * n + m + 1)
                dve.tensor_reduce(mx[:, s % 2, m:m + 1], ps_rows[m % 3][:, 0:(m % NT + 1) * P], AX_X, ALU.max)\
                    .then_inc(max_read, 1)

            def split_maxima(n, s):
                dve.wait_ge(m_ps, n + 1)
                dve.tensor_copy(mrow[:, s % 2, 0, :], ps_m[0:G * NT, 0:P]).then_inc(m_first, 1)
                dve.wait_ge(m_first, n + 1)
                dve.tensor_tensor(mrow[:, s % 2, 1, :], ps_m[0:G * NT, 0:P], mrow[:, s % 2, 0, :], ALU.subtract)\
                    .then_inc(m_split, 1)

            def step(it, s, left):
                n = SLOTS * it + s
                for m in range(G * NT if left >= 2 else 0):
                    maxima(n + 2, s, m)
                    if m == NT - 1:
                        split_maxima(n + 1, s + 1)
                if left == 1:
                    split_maxima(n + 1, s + 1)

            dve.memset(k[:, :, :, :].rearrange("p s h t -> p (s h t)").bitcast(F32), 0.0).then_inc(preset, 1)
            dve.memset(q[:, :, :, :].rearrange("p s h t -> p (s h t)").bitcast(F32), 0.0).then_inc(preset, 1)
            dve.memset(zeros[:, :].bitcast(F32), 0.0).then_inc(preset, 1)
            dve.wait_ge(consts, 48)
            for narrow, full in ((mask, mask32), (maskT, maskT32), (identb, ident)):
                dve.tensor_copy(narrow[:, :], full[:, :]).then_inc(preset, 1)
            dve.sem_inc(head_done, 2)
            for n in range(2):
                for m in range(G * NT):
                    maxima(n, n, m)
                if n == 0:
                    split_maxima(0, 0)
            steps(step, dve)


def phase_merge(nc, sems, ctx_in, x_in, w_in, b_in, base_out, z_out, inverted, name):
    with ExitStack() as ctx:
        def sb(nm, shape, dt=F32):
            return ctx.enter_context(nc.sbuf_tensor(f"{name}_{nm}", shape, dt))


        def sem(nm):
            return sems.new(f"{name}_{nm}")

        w = sb("w", [P, P])
        bo = sb("bo", [P, P])
        num = sb("num", [P, 2, L])
        den = sb("den", [P, L])
        den_inv = sb("den_inv", [P, L])
        inv = sb("inv", [P, 2, L])
        x = sb("x", [P, 2, NT, P])
        xb = sb("xb", [P, 2, NT, P])
        cT = sb("cT", [P, 2, L])
        xa = sb("xa", [P, 2, NT, P])
        base = sb("base", [P, 2, NT, P])
        z = sb("z", [P, 2, NT, P])
        norm = Norm(ctx, nc, sems, name + "_norm")
        ps = [ctx.enter_context(nc.psum_tensor(f"{name}_ps{i}", [P, L], F32)) for i in range(2)]

        consts = sem("consts")
        loaded = [sem("loaded0"), sem("loaded1")]
        x_loaded = [sem("x_loaded0"), sem("x_loaded1")]
        den_loaded = sem("den_loaded")
        den_inverted = sem("den_inverted")
        inv_stored = sem("inv_stored")
        cT_ready = sem("cT_ready")
        a_ps = sem("a_ps")
        xb_ready = sem("xb_ready")
        xa_ready = sem("xa_ready")
        base_ready = sem("base_ready")
        z_ready = sem("z_ready")
        stored = [sem("stored0"), sem("stored1")]
        n_const = 16 + 16 * (b_in is not None)
        n_out = 16 + 16 * (base_out is not None)
        block = sems.block(ctx)

        def load(eng, n, s):
            sums = ctx_in.rearrange("(b g) h r t -> b g h r t", g=NG)[n].rearrange("g h r t -> (g h) r t")
            eng.dma_start(num[:, s, :], sums[:, 0:DH, :]).then_inc(loaded[s], 16)
            eng.dma_start(inv[:, s, :], inverted[n].broadcast_to([H, DH, L])).then_inc(loaded[s], 16)

        def load_x(eng, n, s):
            eng.dma_start(x[:, s, :, :], x_in[n]).then_inc(x_loaded[s], 16)

        def steps(step, eng):
            with eng.Fori(0, NB // 2 - 1) as it:
                for s in range(2):
                    step(it, s, True)
            for s in range(2):
                step(NB // 2 - 1, s, s == 0)

        @block.sync
        def _(sp):
            sp.dma_start(den[:, :], ctx_in.rearrange("n h r t -> (n h) r t")[:, DH, :]).then_inc(den_loaded, 16)
            sp.dma_start(w[:, :], w_in).then_inc(consts, 16)
            if b_in is not None:
                sp.dma_start(bo[:, :], row_on_all(b_in)).then_inc(consts, 16)
            for s in range(2):
                load_x(sp, s, s)
                sp.sem_inc(stored[s], n_out)
            sp.wait_ge(den_inverted, 1)
            sp.dma_start(inverted.rearrange("b h o t -> (b h) (o t)"), den_inv[:, :]).then_inc(inv_stored, 16)
            sp.wait_ge(inv_stored, 16)
            for s in range(2):
                load(sp, s, s)
            with sp.Fori(0, NB // 2) as it:
                for s in range(2):
                    n = 2 * it + s
                    sp.wait_ge(cT_ready, n + 1)
                    load(sp, (n + 2) % NB, s)
                    if base_out is None:
                        sp.wait_ge(xa_ready, n + 3)
                    else:
                        sp.wait_ge(base_ready, n + 1)
                    load_x(sp, (n + 2) % NB, s)
            for s in range(2):
                sp.wait_ge(loaded[s], 32 * (NB // 2 + 1))
                sp.wait_ge(x_loaded[s], 16 * (NB // 2 + 1))
                sp.wait_ge(stored[s], n_out * (NB // 2 + 1))

        @block.scalar
        def _(act):
            with act.Fori(0, NB // 2) as it:
                for s in range(2):
                    n = 2 * it + s
                    if base_out is not None:
                        act.wait_ge(base_ready, n + 1)
                        act.dma_start(base_out[n], base[:, s, :, :]).then_inc(stored[s], 16)
                    act.wait_ge(z_ready, n + 1)
                    act.dma_start(z_out[n], z[:, s, :, :]).then_inc(stored[s], 16)

        @block.gpsimd
        def _(pool):
            def add_bias(n, s, loads):
                pool.wait_ge(x_loaded[s], 16 * loads)
                pool.wait_ge(xa_ready, n + 1)
                pool.tensor_tensor(xb[:, s, :, :], x[:, s, :, :],
                                   bo[:, :].unsqueeze(1).broadcast_to([P, NT, P]), ALU.add).then_inc(xb_ready, 1)

            def step(it, s, ahead):
                n = 2 * it + s
                norm.root(pool, n + 1)
                if base_out is not None:
                    pool.wait_ge(stored[s], n_out * (it + 1))
                    pool.tensor_tensor(base[:, s, :, :], xa[:, s, :, :], x[:, s, :, :], ALU.add)\
                        .then_inc(base_ready, 1)
                if b_in is not None and ahead:
                    add_bias(n + 1, 1 - s, it + 1 + s)

            norm.constants(pool)
            pool.wait_ge(consts, n_const)
            if b_in is not None:
                add_bias(0, 0, 1)
            steps(step, pool)

        @block.tensor
        def _(pe):
            pe.wait_ge(consts, n_const)
            with pe.Fori(0, NB // 2) as it:
                for s in range(2):
                    n = 2 * it + s
                    pe.wait_ge(cT_ready, n + 1)
                    pe.wait_ge(xa_ready, n + 1)
                    for t in range(NT):
                        last = pe.matmul(ps[s][:, t * P:(t + 1) * P], cT[:, s, t * P:(t + 1) * P], w[:, :],
                                         start=True, stop=True)
                    last.then_inc(a_ps, 1)

        @block.vector
        def _(dve):
            def divide(n, s, loads):
                dve.wait_ge(loaded[s], 32 * loads)
                dve.tensor_tensor(cT[:, s, :], num[:, s, :], inv[:, s, :], ALU.mult).then_inc(cT_ready, 1)

            def step(it, s, ahead):
                n = 2 * it + s
                if ahead:
                    divide(n + 1, 1 - s, it + 1 + s)
                dve.wait_ge(a_ps, n + 1)
                if b_in is not None:
                    dve.wait_ge(xb_ready, n + 1)
                else:
                    dve.wait_ge(x_loaded[s], 16 * (it + 1))
                dve.wait_ge(stored[s], n_out * (it + 1))
                src = xb if b_in is not None else x
                dve.tensor_tensor(xa[:, s, :, :], ps[s][:, :].rearrange("p (t d) -> p t d", t=NT),
                                  src[:, s, :, :], ALU.add).then_inc(xa_ready, 1)
                dve.wait_ge(xa_ready, n + 3)
                norm.moments(dve, xa[:, s, :, :], n + 1)
                norm.apply(dve, z[:, s, :, :], xa[:, s, :, :], n + 1).then_inc(z_ready, 1)

            dve.sem_inc(xa_ready, 2)
            dve.wait_ge(den_loaded, 16)
            dve.reciprocal(den_inv[:, :], den[:, :]).then_inc(den_inverted, 1)
            divide(0, 0, 1)
            steps(step, dve)


def phase_experts(nc, sems, z_in, base_in, scale, shift, gate_in, w1_in, w2_in, w3_in, iota_in, ident_in,
                  weights_out, x_out):
    with ExitStack() as ctx:
        def sb(name, shape, dt=F32):
            return ctx.enter_context(nc.sbuf_tensor("e_" + name, shape, dt))


        def sem(name):
            return sems.new("e_" + name)

        KH = HID // P
        w1 = sb("w1", [P, NE, HID])
        w2 = sb("w2", [P, NE, HID])
        w3 = sb("w3", [P, NE, HID])
        w1_halves = [sb(f"w1_half{i}", [P, NE, HID], F32R) for i in range(2)]
        w2_halves = [sb(f"w2_half{i}", [P, NE, HID], F32R) for i in range(2)]
        w3_halves = [sb(f"w3_half{i}", [P, NE, HID], F32R) for i in range(2)]
        gate = sb("gate", [P, NE])
        sc = sb("scale", [P, 2])
        ident = sb("ident", [P, P])
        iota = sb("iota", [P, NE])
        z = sb("z", [P, 2, NT, P])
        base = sb("base", [P, 2, NT, P])
        hT = sb("hT", [P, 2, L])
        hT_halves = [sb(f"hT_half{i}", [P, 2, L], F32R) for i in range(2)]
        scores = sb("scores", [P, NT, NE])
        weight_rows = sb("weight_rows", [NE, L])
        weight_all = sb("weight_all", [P, 2, NE, L])
        top = sb("top", [P, NT, 8])
        idx = sb("idx", [P, NT, 8], U32)
        idxf = sb("idxf", [P, NT, 8])
        diff = sb("diff", [P, NT])
        pr = sb("pr", [P, 2, NT])
        hot = sb("hot", [P, 2, NT, NE])
        weight = sb("weight", [P, NT, NE])
        silu = sb("silu", [P, KH, L])
        gu = sb("gu", [P, 2, KH, L])
        gu_halves = [sb(f"gu_half{i}", [P, 4, KH, L], F32R) for i in range(2)]
        weighed = sb("weighed", [P, 2, KH, L])
        yT = sb("yT", [P, L])
        acc = sb("acc", [P, NT, P])
        xo = sb("xo", [P, 2, NT, P])
        norm = Norm(ctx, nc, sems, "e_norm")
        ps_t = ctx.enter_context(nc.psum_tensor("e_ps_t", [P, L], F32))
        ps_s = ctx.enter_context(nc.psum_tensor("e_ps_s", [P, 512], F32))
        ps_a = ctx.enter_context(nc.psum_tensor("e_ps_a", [P, KH, L], F32))
        ps_b = ctx.enter_context(nc.psum_tensor("e_ps_b", [P, KH, L], F32))
        ps_o = [ctx.enter_context(nc.psum_tensor(f"e_ps_o{i}", [P, L], F32)) for i in range(2)]

        consts = sem("consts")
        z_loaded = [sem("z_loaded0"), sem("z_loaded1")]
        base_loaded = [sem("base_loaded0"), sem("base_loaded1")]
        rows_ps = sem("weight_rows_ps")
        rows_sb = sem("weight_rows_sb")
        rows_stored = sem("weight_rows_stored")
        weights_loaded = [sem("weights_loaded0"), sem("weights_loaded1")]
        weighed_sb = sem("weighed_sb")
        yT_sb = sem("yT_sb")
        y_ps = sem("y_ps")
        acc_ready = sem("acc_ready")
        zT_ps = sem("zT_ps")
        hT_sb = sem("hT_sb")
        s_ps = sem("scores_ps")
        diff_ready = sem("diff_ready")
        pr_ready = sem("pr_ready")
        best_chain = sem("best_chain")
        weight_chain = sem("weight_chain")
        weight_ready = sem("weight_ready")
        marks = sem("marks")
        a_ps = sem("a_ps")
        b_ps = sem("b_ps")
        silu_sb = sem("silu_sb")
        gu_sb = sem("gu_sb")
        gu_high = sem("gu_high")
        gu_low = sem("gu_low")
        hT_high = sem("hT_high")
        hT_low = sem("hT_low")
        w_high = sem("w_high")
        w_low = sem("w_low")
        w3_low = sem("w3_low")
        w_loaded = [sem(f"w{i}_loaded") for i in (1, 2, 3)]
        o_ps = sem("o_ps")
        x_ready = sem("x_ready")
        stored = [sem("stored0"), sem("stored1")]
        n_const = 16 * 5
        block = sems.block(ctx)

        def steps(step, eng):
            for s in range(2):
                step(0, s, s == 0, True)
            with eng.Fori(0, NB // 2 - 2) as it:
                for s in range(2):
                    step(it + 1, s, False, True)
            for s in range(2):
                step(NB // 2 - 1, s, False, s == 0)

        @block.sync
        def _(sp):
            def load_z(n, s):
                sp.dma_start(z[:, s, :, :], z_in[n]).then_inc(z_loaded[s], 16)

            def load_base(n, s):
                sp.dma_start(base[:, s, :, :], base_in[n]).then_inc(base_loaded[s], 16)

            def spread_weights(n, s):
                sp.wait_ge(rows_sb, n + 1)
                sp.dma_start(weights_out[n].rearrange("o (e t) -> (o e) t", e=NE), weight_rows[:, :])\
                    .then_inc(rows_stored, 16)
                sp.wait_ge(rows_stored, 16 * (n + 1))
                sp.dma_start(weight_all[:, s, :, :].rearrange("p e t -> p (e t)"),
                             weights_out[n].broadcast_to([P, NE * L])).then_inc(weights_loaded[s], 16)

            def store(n, s):
                sp.wait_ge(x_ready, n + 1)
                sp.dma_start(x_out[n], xo[:, s, :, :]).then_inc(stored[s], 16)

            def step(it, s, first, ahead):
                n = 2 * it + s
                sp.wait_ge(zT_ps, n + 1)
                load_z((n + 2) % NB, s)
                if ahead:
                    spread_weights(n + 1, 1 - s)
                if not first:
                    sp.wait_ge(acc_ready, n)
                    load_base((n + 1) % NB, 1 - s)
                if not first:
                    store(n - 1, 1 - s)

            sp.dma_start(gate[:, :], gate_in).then_inc(consts, 16)
            sp.dma_start(sc[:, 0:1], scale.rearrange("(d o) -> d o", o=1)).then_inc(consts, 16)
            sp.dma_start(sc[:, 1:2], shift.rearrange("(d o) -> d o", o=1)).then_inc(consts, 16)
            sp.dma_start(ident[:, :], ident_in).then_inc(consts, 16)
            sp.dma_start(iota[:, :], row_on_all(iota_in, NE)).then_inc(consts, 16)
            for s in range(2):
                sp.sem_inc(stored[s], 16)
                load_z(s, s)
            sp.dma_start(w1[:, :, :], w1_in.rearrange("e d h -> d e h")).then_inc(w_loaded[0], 16)
            sp.dma_start(w2[:, :, :], w2_in.rearrange("e d h -> d e h")).then_inc(w_loaded[1], 16)
            sp.dma_start(w3[:, :, :].rearrange("p e (k d) -> p (e k) d", k=KH),
                         w3_in.rearrange("e (k p) d -> p (e k) d", p=P)).then_inc(w_loaded[2], 16)
            spread_weights(0, 0)
            for s in range(2):
                load_base(s, s)
            steps(step, sp)
            store(NB - 1, 1)
            for s in range(2):
                sp.wait_ge(z_loaded[s], 16 * (NB // 2 + 1))
                sp.wait_ge(base_loaded[s], 16 * (NB // 2 + 1 - s))
                sp.wait_ge(weights_loaded[s], 16 * (NB // 2))
                sp.wait_ge(stored[s], 16 * (NB // 2 + 1))

        @block.gpsimd
        def _(pool):
            def low_product(m, e):
                pool.wait_ge(gu_high, m + 1)
                pool.tensor_tensor(gu_halves[1][:, e % 4, :, :], weighed[:, e % 2, :, :],
                                   gu_halves[0][:, e % 4, :, :], ALU.subtract).then_inc(gu_low, 1)

            def low_tokens(n, s):
                pool.wait_ge(hT_high, n + 1)
                pool.tensor_tensor(hT_halves[1][:, s, :], hT[:, s, :], hT_halves[0][:, s, :],
                                   ALU.subtract).then_inc(hT_low, 1)

            def step(it, s, first, ahead):
                n = 2 * it + s
                for e in range(NE):
                    if e + 2 < NE or ahead:
                        low_product(NE * n + e + 2, (e + 2) % NE)
                    if e == 0 and ahead:
                        low_tokens(n + 1, 1 - s)
                    if e == 3 and not first:
                        norm.root(pool, n)

            norm.constants(pool)
            low_tokens(0, 0)
            pool.wait_ge(w_high, 3)
            pool.tensor_tensor(w3_halves[1][:, :, :], w3[:, :, :], w3_halves[0][:, :, :],
                               ALU.subtract).then_inc(w3_low, 1)
            low_product(0, 0)
            low_product(1, 1)
            steps(step, pool)
            norm.root(pool, NB)

        @block.tensor
        def _(pe):
            HALVES = ((0, 0), (0, 1), (1, 0))

            def route(n, s, load_count):
                pe.wait_ge(z_loaded[s], load_count)
                for t in range(NT):
                    last = pe.transpose(ps_t[:, t * P:(t + 1) * P], z[:, s, t, :], ident[:, :])
                last.then_inc(zT_ps, 1)
                pe.wait_ge(hT_sb, n + 1)
                for t in range(NT):
                    last = pe.matmul(ps_s[:, t * NE:(t + 1) * NE], hT[:, s, t * P:(t + 1) * P], gate[:, :],
                                     start=True, stop=True)
                last.then_inc(s_ps, 1)

            def turn_weights(n):
                pe.wait_ge(weight_ready, n + 1)
                for t in range(NT):
                    last = pe.transpose(ps_s[0:NE, t * P:(t + 1) * P], weight[:, t, :], ident[:, :])
                last.then_inc(rows_ps, 1)

            def turn_sums(n):
                pe.wait_ge(yT_sb, n + 1)
                for t in range(NT):
                    last = pe.transpose(ps_t[:, t * P:(t + 1) * P], yT[:, t * P:(t + 1) * P], ident[:, :])
                last.then_inc(y_ps, 1)

            def up(w, ps, e, s, ready):
                for k in range(KH):
                    for i, (a, b) in enumerate(HALVES):
                        last = pe.matmul(ps[:, k, :], w[a][:, e, k * P:(k + 1) * P], hT_halves[b][:, s, :],
                                         start=(i == 0), stop=(i == 2))
                last.then_inc(ready, 1)

            def ups(n, s, e):
                m = NE * n + e
                pe.wait_ge(silu_sb, m + 1)
                up(w1_halves, ps_a, e, s, a_ps)
                pe.wait_ge(gu_sb, m + 1)
                up(w2_halves, ps_b, e, s, b_ps)

            def down(m, s, e):
                pe.wait_ge(gu_low, m + 1)
                for k in range(KH):
                    for i, (a, b) in enumerate(HALVES):
                        last = pe.matmul(ps_o[s][:, :], w3_halves[a][:, e, k * P:(k + 1) * P],
                                         gu_halves[b][:, e % 4, k, :], start=(e == 0 and k == 0 and i == 0),
                                         stop=(e == NE - 1 and k == KH - 1 and i == 2))
                last.then_inc(o_ps, 1)

            def step(it, s, first, ahead):
                n = 2 * it + s
                for e in range(NE):
                    if e + 2 < NE:
                        ups(n, s, e + 2)
                    elif ahead:
                        if e + 2 == NE:
                            pe.wait_ge(hT_low, n + 2)
                        ups(n + 1, 1 - s, e + 2 - NE)
                    if e == 0 and ahead:
                        route(n + 1, 1 - s, 16 * (it + 1 + s))
                    if e == 3 and not first:
                        turn_sums(n - 1)
                    if e == 2 and ahead:
                        turn_weights(n + 1)
                    down(NE * n + e, s, e)

            pe.wait_ge(consts, n_const)
            route(0, 0, 16)
            turn_weights(0)
            pe.wait_ge(hT_low, 1)
            pe.wait_ge(w_low, 1)
            up(w1_halves, ps_a, 0, 0, a_ps)
            pe.wait_ge(w_low, 2)
            up(w2_halves, ps_b, 0, 0, b_ps)
            ups(0, 0, 1)
            pe.wait_ge(w3_low, 1)
            steps(step, pe)
            turn_sums(NB - 1)

        @block.scalar
        def _(act):
            def turn(n, s):
                act.wait_ge(zT_ps, n + 1)
                act.activation(hT[:, s, :], ps_t[:, :], ACT.Identity, bias=sc[:, 1:2], scale=sc[:, 0:1])\
                    .then_inc(hT_sb, 1)

            def weigh(n):
                act.wait_ge(diff_ready, n + 1)
                act.activation(pr[:, 0, :], diff[:, :], ACT.Sigmoid, scale=-1.0).then_inc(pr_ready, 1)
                act.activation(pr[:, 1, :], diff[:, :], ACT.Sigmoid).then_inc(pr_ready, 1)

            def activate(m):
                act.wait_ge(a_ps, m + 1)
                act.wait_ge(gu_sb, m + 1)
                act.activation(silu[:, :, :], ps_a[:, :, :], ACT.Silu).then_inc(silu_sb, 1)

            def high_product(m, e):
                if not isinstance(m, int) or m >= 4:
                    act.wait_ge(o_ps, m - 3)
                act.wait_ge(weighed_sb, m + 1)
                act.activation(gu_halves[0][:, e % 4, :, :], weighed[:, e % 2, :, :], ACT.Copy).then_inc(gu_high, 1)

            def take_sums(n, s):
                act.wait_ge(o_ps, NE * (n + 1))
                act.activation(yT[:, :], ps_o[s][:, :], ACT.Copy).then_inc(yT_sb, 1)

            def step(it, s, first, ahead):
                n = 2 * it + s
                for e in range(NE):
                    if e + 2 < NE or ahead:
                        activate(NE * n + e + 2)
                    if e + 1 < NE or ahead:
                        high_product(NE * n + e + 1, (e + 1) % NE)
                    if e == 0 and ahead:
                        turn(n + 1, 1 - s)
                    if e == 0 and not first:
                        take_sums(n - 1, 1 - s)
                    if e == 1 and ahead:
                        weigh(n + 1)

            act.sem_inc(silu_sb, 1)
            act.wait_ge(consts, n_const)
            turn(0, 0)
            weigh(0)
            activate(0)
            activate(1)
            high_product(0, 0)
            steps(step, act)
            take_sums(NB - 1, 1)

        @block.vector
        def _(dve):
            def best(n):
                chain = Chain(dve, best_chain, n, 2)
                dve.wait_ge(s_ps, n + 1)
                chain.step(dve.tensor_copy(scores[:, :, :].rearrange("p t e -> p (t e)"), ps_s[:, 0:NT * NE]))
                dve.sem_inc(marks, 1)
                for t in range(NT):
                    last = dve.max(top[:, t, :], scores[:, t, :])
                chain.step(last)
                dve.tensor_tensor(diff[:, :], top[:, :, 1], top[:, :, 0], ALU.subtract).then_inc(diff_ready, 1)
                chain.done()

            def weights(n):
                chain = Chain(dve, weight_chain, n, 3)
                for t in range(NT):
                    last = dve.max_index(idx[:, t, :], top[:, t, :], scores[:, t, :])
                chain.step(last)
                chain.step(dve.tensor_copy(idxf[:, :, :], idx[:, :, :]))
                dve.wait_ge(pr_ready, 2 * (n + 1))
                for t in range(NT):
                    for r in range(2):
                        last = dve.tensor_scalar(hot[:, r, t, :], iota[:, :], idxf[:, t, r:r + 1],
                                                 pr[:, r, t:t + 1], ALU.is_equal, ALU.mult)
                chain.step(last)
                dve.tensor_tensor(weight[:, :, :], hot[:, 0, :, :], hot[:, 1, :, :], ALU.add)\
                    .then_inc(weight_ready, 1)
                chain.done()

            def take_rows(n):
                dve.wait_ge(rows_ps, n + 1)
                dve.tensor_copy(weight_rows[:, :], ps_s[0:NE, 0:L]).then_inc(rows_sb, 1)

            def high(out, x, ready):
                dve.tensor_copy(out, x).then_inc(ready, 1)

            def high_tokens(n, s):
                dve.wait_ge(hT_sb, n + 1)
                high(hT_halves[0][:, s, :], hT[:, s, :], hT_high)

            def product(m, e, s, loads):
                dve.wait_ge(silu_sb, m + 2)
                dve.wait_ge(b_ps, m + 1)
                dve.tensor_tensor(gu[:, e % 2, :, :], silu[:, :, :], ps_b[:, :, :], ALU.mult)\
                    .then_inc(gu_sb, 1)
                if e == 0:
                    dve.wait_ge(weights_loaded[s], 16 * loads)
                if not isinstance(m, int) or m >= 2:
                    dve.wait_ge(gu_low, m - 1)
                dve.wait_ge(gu_sb, m + 2)
                dve.tensor_tensor(weighed[:, e % 2, :, :], gu[:, e % 2, :, :],
                                  weight_all[:, s, e, :].unsqueeze(1).broadcast_to([P, KH, L]), ALU.mult)\
                    .then_inc(weighed_sb, 1)

            def add_base(n, s, loads):
                dve.wait_ge(y_ps, n + 1)
                dve.wait_ge(base_loaded[s], 16 * loads)
                dve.tensor_tensor(acc[:, :, :], ps_t[:, :].rearrange("p (t d) -> p t d", t=NT), base[:, s, :, :],
                                  ALU.add).then_inc(acc_ready, 1)
                dve.wait_ge(acc_ready, n + 1)
                norm.moments(dve, acc, n + 1)

            def finish(n, s, stores):
                dve.wait_ge(stored[s], 16 * stores)
                norm.apply(dve, xo[:, s, :, :], acc, n + 1).then_inc(x_ready, 1)

            def step(it, s, first, ahead):
                n = 2 * it + s
                for e in range(NE):
                    m = NE * n + e
                    if e + 2 < NE:
                        product(m + 2, e + 2, s, it + 1)
                    elif ahead:
                        product(m + 2, e + 2 - NE, 1 - s, it + 1 + s)
                    if e == 0 and ahead:
                        best(n + 1)
                        high_tokens(n + 1, 1 - s)
                    if e == 1 and ahead:
                        weights(n + 1)
                    if e == 2 and ahead:
                        take_rows(n + 1)
                    if e == 3 and not first:
                        add_base(n - 1, 1 - s, it + s)
                    if e == 4 and not first:
                        finish(n - 1, 1 - s, it + s)

            dve.sem_inc(gu_sb, 1)
            dve.wait_ge(consts, n_const)
            best(0)
            high_tokens(0, 0)
            weights(0)
            take_rows(0)
            for i, (w, halves) in enumerate(((w1, w1_halves), (w2, w2_halves), (w3, w3_halves))):
                dve.wait_ge(w_loaded[i], 16)
                high(halves[0][:, :, :], w[:, :, :], w_high)
                if i < 2:
                    dve.wait_ge(w_high, i + 1)
                    dve.tensor_tensor(halves[1][:, :, :], w[:, :, :], halves[0][:, :, :],
                                      ALU.subtract).then_inc(w_low, 1)
            for e in range(2):
                product(e, e, 0, 1)
            steps(step, dve)
            add_base(NB - 1, 1, NB // 2)
            finish(NB - 1, 1, NB // 2)


def phase_last(nc, sems, x_in, u1T_in, v1_in, b1_in, u2_in, v2_in, b2_in, ident_in, out):
    KF = FF // P
    assert KF * RANK == P
    with ExitStack() as ctx:
        def sb(name, shape, dt=F32):
            return ctx.enter_context(nc.sbuf_tensor("f_" + name, shape, dt))


        def sem(name):
            return sems.new("f_" + name)

        u1T = sb("u1T", [RANK, P])
        v1 = sb("v1", [RANK, FF])
        uv = sb("uv", [P, FF])
        b1 = sb("b1", [P, KF])
        u2 = sb("u2", [P, KF, RANK])
        v2 = sb("v2", [P, P])
        b2 = sb("b2", [P, P])
        ident = sb("ident", [P, P])
        x = sb("x", [P, 2, NT, P])
        xb = sb("xb", [P, NB, NT, P])
        xT = sb("xT", [P, 2, L])
        hT = sb("hT", [P, KF, L])
        qT = sb("qT", [P, L])
        t1 = sb("t1", [P, 2, NT, P])
        y = sb("y", [P, 2, NT, P])
        norm = Norm(ctx, nc, sems, "f_norm")
        ps_xT = ctx.enter_context(nc.psum_tensor("f_ps_xT", [P, L], F32))
        ps_h = [ctx.enter_context(nc.psum_tensor(f"f_ps_h{i}", [P, L], F32)) for i in range(KF)]
        ps_q = ctx.enter_context(nc.psum_tensor("f_ps_q", [P, L], F32))
        ps_y = ctx.enter_context(nc.psum_tensor("f_ps_y", [P, L], F32))

        consts = sem("consts")
        loaded = [sem("loaded0"), sem("loaded1")]
        xT_ps = sem("xT_ps")
        xT_sb = sem("xT_sb")
        uv_ps = sem("uv_ps")
        uv_sb = sem("uv_sb")
        h_ps = sem("h_ps")
        h_sb = sem("h_sb")
        q_ps = sem("q_ps")
        q_sb = sem("q_sb")
        y_ps = sem("y_ps")
        y_read = sem("y_read")
        xb_ready = sem("xb_ready")
        out_ready = sem("out_ready")
        stored = [sem("stored0"), sem("stored1")]
        N_CONST = 16 * (6 + KF)
        block = sems.block(ctx)

        def steps(step, eng):
            with eng.Fori(0, NB // 2 - 1) as it:
                for s in range(2):
                    step(it, s, 2)
            for s in range(2):
                step(NB // 2 - 1, s, 1 - s)

        @block.sync
        def _(sp):
            for s in range(2):
                sp.dma_start(x[:, s, :, :], x_in[s]).then_inc(loaded[s], 16)
            sp.dma_start(ident[:, :], ident_in).then_inc(consts, 16)
            sp.dma_start(b1[:, :], b1_in).then_inc(consts, 16)
            sp.dma_start(u2[:, :, :], u2_in.rearrange("(k p) r -> p k r", p=P)).then_inc(consts, 16)
            sp.dma_start(u1T[:, :], u1T_in).then_inc(consts, 16)
            sp.dma_start(v1[:, :], v1_in).then_inc(consts, 16)
            sp.dma_start(b2[:, :], row_on_all(b2_in)).then_inc(consts, 16)
            for k in range(KF):
                sp.dma_start(v2[RANK * k:RANK * k + RANK, :], v2_in).then_inc(consts, 16)
            for s in range(2):
                sp.sem_inc(stored[s], 16)

            def load(n, s):
                sp.wait_ge(xb_ready, n - 1)
                sp.dma_start(x[:, s, :, :], x_in[n]).then_inc(loaded[s], 16)

            def store(n, s):
                sp.wait_ge(out_ready, n + 1)
                sp.dma_start(out[n].rearrange("(t p) d -> p t d", p=P), y[:, s, :, :]).then_inc(stored[s], 16)

            for s in range(2):
                load(2 + s, s)
            with sp.Fori(0, NB // 2 - 2) as it:
                for s in range(2):
                    load(2 * it + 4 + s, s)
                    store(2 * it + s, s)
            for n in range(NB - 4, NB):
                store(n, n % 2)
            for s in range(2):
                sp.wait_ge(stored[s], 16 * (NB // 2 + 1))

        @block.gpsimd
        def _(pool):
            def add_b2(n, s):
                pool.wait_ge(xT_ps, n + 1)
                pool.tensor_tensor(xb[:, n, :, :], x[:, s, :, :],
                                   b2[:, :].unsqueeze(1).broadcast_to([P, NT, P]), ALU.add).then_inc(xb_ready, 1)

            def step(it, s, left):
                n = 2 * it + s
                if left >= 2:
                    add_b2(n + 2, s)
                norm.root(pool, n + 1)

            norm.constants(pool)
            pool.wait_ge(consts, N_CONST)
            add_b2(0, 0)
            add_b2(1, 1)
            steps(step, pool)

        @block.tensor
        def _(pe):
            def turn(n, s, loads):
                pe.wait_ge(loaded[s], 16 * loads)
                for t in range(NT):
                    last = pe.transpose(ps_xT[:, t * P:(t + 1) * P], x[:, s, t, :], ident[:, :])
                last.then_inc(xT_ps, 1)

            def hidden(n, s):
                pe.wait_ge(xT_sb, n + 1)
                for k in range(KF):
                    pe.matmul(ps_h[k][:, :], uv[:, k * P:(k + 1) * P], xT[:, s, :], start=True, stop=True)\
                        .then_inc(h_ps, 1)

            def reduced(n):
                pe.wait_ge(h_sb, KF * (n + 1))
                for k in range(KF):
                    last = pe.matmul(ps_q[RANK * k:RANK * k + RANK, :], u2[:, k, :], hT[:, k, :],
                                     start=True, stop=True)
                last.then_inc(q_ps, 1)

            def step(it, s, left):
                n = 2 * it + s
                if left >= 1:
                    hidden(n + 1, 1 - s)
                if left >= 2:
                    turn(n + 2, s, it + 2)
                pe.wait_ge(q_sb, n + 1)
                pe.wait_ge(y_read, n + 1)
                for t in range(NT):
                    last = pe.matmul(ps_y[:, t * P:(t + 1) * P], qT[:, t * P:(t + 1) * P], v2[:, :],
                                     start=True, stop=True)
                last.then_inc(y_ps, 1)
                if left >= 1:
                    reduced(n + 1)

            pe.wait_ge(consts, N_CONST)
            turn(0, 0, 1)
            pe.wait_ge(xT_sb, 1)
            turn(1, 1, 1)
            pe.matmul(ps_h[0][:, :], u1T[:, :], v1[:, :], start=True, stop=True).then_inc(uv_ps, 1)
            pe.wait_ge(uv_sb, 1)
            hidden(0, 0)
            reduced(0)
            steps(step, pe)

        @block.scalar
        def _(act):
            def gelus(n):
                for k in range(KF):
                    act.wait_ge(h_ps, KF * n + k + 1)
                    act.activation(hT[:, k, :], ps_h[k][:, :], ACT.Gelu_apprx_tanh, bias=b1[:, k:k + 1])\
                        .then_inc(h_sb, 1)

            act.wait_ge(consts, N_CONST)
            gelus(0)
            with act.Fori(1, NB) as n:
                gelus(n)

        @block.vector
        def _(dve):
            def turned(n, s):
                dve.wait_ge(xT_ps, n + 1)
                dve.tensor_copy(xT[:, s, :], ps_xT[:, :]).then_inc(xT_sb, 1)

            def copy_reduced(n):
                dve.wait_ge(q_ps, n + 1)
                dve.tensor_copy(qT[:, :], ps_q[:, :]).then_inc(q_sb, 1)

            def step(it, s, left):
                n = 2 * it + s
                if left >= 2:
                    turned(n + 2, s)
                dve.wait_ge(y_ps, n + 1)
                dve.wait_ge(xb_ready, n + 1)
                dve.tensor_tensor(t1[:, s, :, :], ps_y[:, :].rearrange("p (t d) -> p t d", t=NT),
                                  xb[:, n, :, :], ALU.add).then_inc(y_read, 1)
                if left >= 1:
                    copy_reduced(n + 1)
                dve.wait_ge(y_read, n + 2)
                norm.moments(dve, t1[:, s, :, :], n + 1)
                dve.wait_ge(stored[s], 16 * (it + 1))
                norm.apply(dve, y[:, s, :, :], t1[:, s, :, :], n + 1).then_inc(out_ready, 1)

            dve.sem_inc(y_read, 1)
            turned(0, 0)
            turned(1, 1)
            dve.wait_ge(uv_ps, 1)
            dve.tensor_copy(uv[:, :], ps_h[0][:, :]).then_inc(uv_sb, 1)
            copy_reduced(0)
            steps(step, dve)


def phase_relative(nc, sems, qu_stacks, qv_stacks, k_stacks, v9_in, r_stack, half_in, ident_in, ctx_out):
    SCALE = DH ** -0.5
    Q = 32
    W = L + HW
    TG = G * NT
    SKEW = 16 * HW
    ROUNDS = NI // 2
    LOWEST = -3.0e38
    with ExitStack() as ctx:
        def sb(name, shape, dt=F32):
            return ctx.enter_context(nc.sbuf_tensor("r_" + name, shape, dt))


        def sem(name):
            return sems.new("r_" + name)

        def bank(name):
            return ctx.enter_context(nc.psum_tensor("r_" + name, [P, 512], F32))

        qu = sb("qu", [P, 2, G, L], BF16)
        k = sb("k", [P, 2, G, L], BF16)
        qv = sb("qv", [2 * SK, G, L + 2], BF16)
        qv_here = sb("qv_here", [P, 2, G, L], BF16)
        qv_next = sb("qv_next", [P, 2, G, L], BF16)
        half = sb("half", [2 * SK, L], BF16)
        r = sb("r", [P, 2, G, 2 * L + HW], BF16)
        v9 = sb("v9", [P, 2, NT, G * VW])
        ident = sb("ident", [P, P])
        wide = sb("wide", [P, 2, TG, W])
        shifted = sb("shifted", [P, 2, TG, L])
        mx = sb("mx", [P, TG])
        probs = sb("probs", [P, 2, NT, L])
        osb = sb("osb", [P, G, P])
        ps_wide = [bank("ps_wide0"), bank("ps_wide1")]
        ps_tail = bank("ps_tail")
        ps_ac = [bank("ps_ac0"), bank("ps_ac1")]
        ps_keys = [bank("ps_keys0"), bank("ps_keys1")]
        ps_out = bank("ps_out")

        consts = sem("consts")
        half_loaded = sem("half_loaded")
        pad_set = sem("pad_set")
        half_set = sem("half_set")
        loaded = [sem("loaded0"), sem("loaded1")]
        qv_loaded = sem("qv_loaded")
        qv_halved = sem("qv_halved")
        r_loaded = [sem("r_loaded0"), sem("r_loaded1")]
        wide_ps = sem("wide_ps")
        wide_sb = sem("wide_sb")
        tail_sb = sem("tail_sb")
        skewed = [sem("skewed0"), sem("skewed1")]
        ac_ps = sem("ac_ps")
        ac_used = sem("ac_used")
        marks = sem("marks")
        s_ready = sem("scores_ready")
        slot_marks = sem("slot_marks")
        keys_ps = sem("keys_ps")
        exp_done = sem("exp_done")
        head_done = sem("head_done")
        out_sb = sem("out_sb")
        stored = sem("stored")
        block = sems.block(ctx)

        def steps(step, eng):
            for s in range(2):
                step(0, s, s == 0, 2)
            with eng.Fori(0, ROUNDS - 2) as it:
                for s in range(2):
                    step(it + 1, s, False, 2)
            for s in range(2):
                step(ROUNDS - 1, s, False, 1 - s)

        @block.sync
        def _(sp):
            def load(n, s):
                b, g = n // NG, n % NG
                for dst, src in ((qu, qu_stacks), (k, k_stacks)):
                    sp.dma_start(dst[0:SK, s, :, :], src.rearrange("b r (g h) t -> b g r h t", h=G)[b, g])\
                        .then_inc(loaded[s], 16)
                sp.dma_start(v9[:, s, :, :], v9_in.rearrange("b p t (g v) -> b g p t v", g=NG)[b, g])\
                    .then_inc(loaded[s], 16)

            def load_queries(n):
                b, g = n // NG, n % NG
                for row in (0, SK):
                    sp.dma_start(qv[row:row + SK, :, 0:L], qv_stacks.rearrange("b r (g h) t -> b g r h t", h=G)[b, g])\
                        .then_inc(qv_loaded, 16)

            def load_positions(n, s):
                sp.dma_start(r[0:2 * SK, s, :, :], r_stack.rearrange("r (g h) t -> g r h t", h=G)[n % NG])\
                    .then_inc(r_loaded[s], 16)

            def skew(n, s):
                sp.wait_ge(tail_sb, n + 1)
                for i in range(HW):
                    sp.dma_start(shifted[i::HW, s, :, :], wide[i::HW, s, :, HW - 1 - i:HW - 1 - i + L])\
                        .then_inc(skewed[s], 16)

            def step(it, s, first, left):
                n = 2 * it + s
                if left >= 2:
                    sp.wait_ge(qv_halved, 2 * (n + 3))
                    load_queries((n + 3) % NI)
                if left >= 1:
                    if not first:
                        sp.wait_ge(keys_ps, TG * n)
                        sp.sem_inc(slot_marks, 1)
                    skew(n + 1, 1 - s)
                if left >= 2:
                    sp.wait_ge(wide_ps, TG * (n + 2))
                    load_positions((n + 3) % NI, 1 - s)
                if left >= 1:
                    sp.wait_ge(head_done, G * n + 2)
                    load(n + 1, 1 - s)
                if not first:
                    store(n - 1)

            def store(n):
                sp.wait_ge(out_sb, n + 2)
                for b in range(NT):
                    sp.dma_start(ctx_out[n, :, :, b * P:(b + 1) * P].rearrange("h r i -> r h i"),
                                 osb[Q * b:Q * b + VW, :, :]).then_inc(stored, 16)

            sp.dma_start(shifted[0:2 * SK, 0, 0, :], half_in).then_inc(half_loaded, 16)
            load_queries(0)
            load_positions(0, 0)
            load_positions(1, 1)
            sp.dma_start(ident[:, :], ident_in).then_inc(consts, 16)
            sp.wait_ge(qv_halved, 2)
            load_queries(1)
            sp.wait_ge(pad_set, 6)
            load(0, 0)
            sp.wait_ge(qv_halved, 4)
            load_queries(2)
            sp.wait_ge(wide_ps, TG)
            load_positions(2, 0)
            sp.sem_inc(stored, 64)
            sp.wait_ge(half_set, 1)
            skew(0, 0)
            steps(step, sp)
            store(NI - 1)
            for s in range(2):
                sp.wait_ge(loaded[s], 48 * ROUNDS)
                sp.wait_ge(r_loaded[s], 16 * (ROUNDS + 1 - s))
                sp.wait_ge(skewed[s], SKEW * ROUNDS)
            sp.wait_ge(qv_loaded, 32 * (NI + 1))
            sp.wait_ge(stored, 64 * (NI + 1))

        @block.gpsimd
        def _(pool):
            def halve(n, s):
                mask = half[:, :].unsqueeze(1).broadcast_to([2 * SK, G, L])
                pool.wait_ge(qv_loaded, 32 * (n + 1))
                pool.tensor_tensor(qv_here[0:2 * SK, s, :, :], qv[:, :, 0:L], mask, ALU.mult)\
                    .then_inc(qv_halved, 1)
                pool.tensor_tensor(qv_next[0:2 * SK, s, :, :], qv[:, :, 1:L + 1], mask, ALU.mult)\
                    .then_inc(qv_halved, 1)

            pool.wait_ge(pad_set, 1)
            pool.wait_ge(half_set, 1)
            for n in range(2):
                halve(n, n)
            with pool.Fori(0, ROUNDS - 1) as it:
                for s in range(2):
                    n = 2 * it + 2 + s
                    pool.wait_ge(wide_ps, TG * (n - 1))
                    halve(n, s)

        @block.tensor
        def _(pe):
            def wide_tile(n, s, u):
                h, b = u // NT, u % NT
                tile = TG * n + u
                ps = ps_wide[u % 2]
                if not isinstance(tile, int) or tile >= 2:
                    pe.wait_ge(wide_sb, tile - 1)
                if u == 0 and (not isinstance(n, int) or n):
                    pe.wait_ge(tail_sb, n)
                windows, tails = ([], []), []
                for a in range(P // Q):
                    q0 = b * P + a * Q
                    here, after = qv_here[:, s, h, q0:q0 + Q], qv_next[:, s, h, q0:q0 + Q]
                    at = L - HW - q0
                    windows[0].append((a, here, 0, q0 + Q, at))
                    windows[1].append((a, after, q0 + HW, L, at + HW))
                    tails.append((a, after, L, W, at + HW))
                for which in range(2):
                    for a, lhs, lo, hi, at in windows[which]:
                        pe.matmul(ps[Q * a:Q * a + Q, lo:hi], lhs, r[:, s, h, at + lo:at + hi],
                                  start=(which == 0), stop=(which == 1), skip_group_check=True)
                for a, lhs, lo, hi, at in tails:
                    last = pe.matmul(ps_tail[Q * a:Q * a + Q, HW * u:HW * (u + 1)], lhs,
                                     r[:, s, h, at + lo:at + hi], start=True, stop=True)
                last.then_inc(wide_ps, 1)

            def content_tile(n, s, u):
                h, b = u // NT, u % NT
                pe.wait_ge(ac_used, TG * n + u + 1)
                pe.matmul(ps_ac[u % 2][:, :], qu[:, s, h, b * P:(b + 1) * P], k[:, s, h, :], start=True, stop=True)\
                    .then_inc(ac_ps, 1)

            def turn_tile(n, s, u):
                pe.wait_ge(s_ready, TG * n + u + 1)
                pe.wait_ge(exp_done, TG * n + u + 1)
                for j in range(NT):
                    last = pe.transpose(ps_keys[u % 2][:, j * P:(j + 1) * P],
                                        shifted[:, s, u, j * P:(j + 1) * P], ident[:, :])
                last.then_inc(keys_ps, 1)

            def value_head(n, s, h):
                pe.wait_ge(exp_done, TG * n + NT * (h + 1) + 2)
                if h == 0:
                    pe.wait_ge(out_sb, n + 1)
                for j in range(NT):
                    for b in range(NT):
                        last = pe.matmul(ps_out[Q * b:Q * b + VW, h * P:(h + 1) * P],
                                         v9[:, s, j, h * VW:(h + 1) * VW], probs[:, h % 2, j, b * P:(b + 1) * P],
                                         start=(j == 0), stop=(j == NT - 1), skip_group_check=True)
                last.then_inc(head_done, 1)

            def step(it, s, first, left):
                n = 2 * it + s
                if left >= 2:
                    pe.wait_ge(qv_halved, 2 * (n + 3))
                    pe.wait_ge(r_loaded[s], 16 * (it + 2))
                for u in range(TG):
                    if u + 2 < TG:
                        content_tile(n, s, u + 2)
                    elif left >= 1:
                        if u + 2 == TG:
                            pe.wait_ge(loaded[1 - s], 48 * (it + 1 + s))
                        content_tile(n + 1, 1 - s, u + 2 - TG)
                    turn_tile(n, s, u)
                    if left >= 2:
                        wide_tile(n + 2, s, u)
                    if u == 1 and not first:
                        value_head(n - 1, 1 - s, G - 1)
                    if u % NT == 1 and u > NT:
                        value_head(n, s, u // NT - 1)

            pe.wait_ge(consts, 16)
            for j in range(NT):
                last = pe.transpose(ps_out[:, j * P:(j + 1) * P], ident[:, :], ident[:, :])
            pe.wait_ge(pad_set, 6)
            for n in range(2):
                pe.wait_ge(r_loaded[n], 16)
                pe.wait_ge(qv_halved, 2 * (n + 1))
                for u in range(TG):
                    wide_tile(n, n, u)
            pe.wait_ge(loaded[0], 48)
            content_tile(0, 0, 0)
            content_tile(0, 0, 1)
            steps(step, pe)
            value_head(NI - 1, 1, G - 1)

        @block.scalar
        def _(act):
            def copy_wide(n, s, u):
                act.wait_ge(wide_ps, TG * n + u + 1)
                act.activation(wide[:, s, u, 0:L], ps_wide[u % 2][:, :], ACT.Copy).then_inc(wide_sb, 1)

            def copy_tail(s):
                act.activation(wide[:, s, :, L:W], ps_tail[:, 0:TG * HW].rearrange("p (u w) -> p u w", w=HW),
                               ACT.Copy).then_inc(tail_sb, 1)

            def take_sums(n):
                act.wait_ge(head_done, G * (n + 1) + 2)
                act.wait_ge(stored, 64 * (n + 1))
                act.activation(osb[:, :, :].rearrange("p h i -> p (h i)"), ps_out[:, :], ACT.Copy)\
                    .then_inc(out_sb, 1)

            def step(it, s, first, left):
                n = 2 * it + s
                act.wait_ge(skewed[s], SKEW * (it + 1))
                for u in range(TG):
                    h, b = u // NT, u % NT
                    if b == 0:
                        act.wait_ge(head_done, G * n + h + 1)
                    act.wait_ge(keys_ps, TG * n + u + 1)
                    act.activation(probs[:, h % 2, :, b * P:(b + 1) * P],
                                   ps_keys[u % 2][:, :].rearrange("p (j i) -> p j i", j=NT), ACT.Exp,
                                   scale=SCALE).then_inc(exp_done, 1)
                    if left >= 2:
                        copy_wide(n + 2, s, u)
                    if u == 2 and not first:
                        take_sums(n - 1)
                if left >= 2:
                    copy_tail(s)

            act.sem_inc(exp_done, 2)
            act.sem_inc(out_sb, 1)
            for n in range(2):
                for u in range(TG):
                    copy_wide(n, n, u)
                copy_tail(n)
            steps(step, act)
            take_sums(NI - 1)

        @block.vector
        def _(dve):
            def step(it, s, first, left):
                n = 2 * it + s
                dve.wait_ge(skewed[s], SKEW * (it + 1))
                for u in range(TG):
                    dve.wait_ge(ac_ps, TG * n + u + 1)
                    dve.sem_inc(marks, 1)
                    dve.tensor_tensor_reduce(out=shifted[:, s, u, :], in0=ps_ac[u % 2][:, :],
                                             in1=shifted[:, s, u, :], scale=1.0, scalar=LOWEST,
                                             op0=ALU.add, op1=ALU.max, accum_out=mx[:, u:u + 1])\
                        .then_inc(ac_used, 1)
                    take_maximum(n, s, u)

            def take_maximum(n, s, u):
                dve.wait_ge(ac_used, TG * n + u + 3)
                dve.tensor_scalar(shifted[:, s, u, :], shifted[:, s, u, :], mx[:, u:u + 1], None,
                                  ALU.subtract).then_inc(s_ready, 1)

            dve.memset(qv[:, :, L:L + 2], 0.0).then_inc(pad_set, 1)
            dve.wait_ge(half_loaded, 16)
            dve.tensor_copy(half[:, :], shifted[0:2 * SK, 0, 0, :]).then_inc(half_set, 1)
            for stack, rows in ((qv_here, slice(2 * SK, P)), (qv_next, slice(2 * SK, P)), (r, slice(2 * SK, P)),
                                (qu, slice(0, P)), (k, slice(0, P))):
                dve.memset(stack[rows, :, :, :].rearrange("p s h t -> p (s h t)").bitcast(F32), 0.0)\
                    .then_inc(pad_set, 1)
            dve.sem_inc(head_done, 2)
            dve.sem_inc(ac_used, 2)
            steps(step, dve)


def program(nc, x, w_qkvT, w_fcT, b_fc, gamma, beta, ln1_scale, ln1_shift, wq, wk, wv, wo, bo, ln2_scale,
            ln2_shift, gate_w, w1, w2, w3, rel_wqT, rel_wkT, rel_wvT, rel_wrT, u_bias, v_bias, u1T, v1, b1, u2,
            v2, b2, ident, mask, maskT, iota, positions, half, out):
    def dram(name, shape, dt=F32):
        return nc.dram_tensor(name, shape, dt, kind="Internal").ap()

    tokens = (NB, P, NT, P)
    x1, z1, base, z2, x2, x3 = (dram(name, tokens) for name in ("x1", "z1", "base", "z2", "x2", "x3"))
    stacks = [dram(f"stack{i}", (NB, SK, H, L), BF16) for i in range(5)]
    v9 = [dram(f"v9_{i}", (NB, P, NT, H * VW)) for i in range(2)]
    sums = [dram(f"sums{i}", (NI, G, VW, L)) for i in range(2)]
    inverted = [dram(f"inverted{i}", (NB, H, 1, L)) for i in range(2)]
    weights = dram("weights", (NB, 1, NE * L))
    r_stack = dram("r_stack", (2 * SK, H, 2 * L + HW), BF16)

    sems = Semaphores(nc)
    phase_attention(nc, sems, x, w_qkvT, w_fcT, b_fc, gamma, beta, ident, x1, z1)
    sems = Semaphores(nc, sems)
    phase_project(nc, sems, z1, ln1_scale, ln1_shift, [wq, wk, wv], [None, None], [TERMS_Q, TERMS_K], ident,
                  stacks[0:2], v9[0], "b", (rel_wrT, positions, r_stack))
    sems = Semaphores(nc, sems)
    phase_causal(nc, sems, stacks[0], stacks[1], v9[0], mask, maskT, ident, sums[0])
    sems = Semaphores(nc, sems)
    phase_merge(nc, sems, sums[0], x1, wo, bo, base, z2, inverted[0], "m")
    sems = Semaphores(nc, sems)
    phase_experts(nc, sems, z2, base, ln2_scale, ln2_shift, gate_w, w1, w2, w3, iota, ident, weights, x2)
    sems = Semaphores(nc, sems)
    phase_project(nc, sems, x2, None, None, [rel_wqT, rel_wqT, rel_wkT, rel_wvT], [u_bias, v_bias, None],
                  [TERMS_Q, TERMS_Q, TERMS_K], ident, stacks[2:5], v9[1], "d")
    sems = Semaphores(nc, sems)
    phase_relative(nc, sems, stacks[2], stacks[3], stacks[4], v9[1], r_stack, half, ident, sums[1])
    sems = Semaphores(nc, sems)
    phase_merge(nc, sems, sums[1], x2, ident, None, None, x3, inverted[1], "n")
    sems = Semaphores(nc, sems)
    phase_last(nc, sems, x3, u1T, v1, b1, u2, v2, b2, ident, out)
    sems.finish()


_PLAIN = ("L0_attn_x", "L0_attn_b_fc", "L0_attn_gamma", "L0_attn_beta", "L0_ffn_ln1_scale", "L0_ffn_ln1_shift",
          "L0_ffn_wq", "L0_ffn_wk", "L0_ffn_wv", "L0_ffn_wo", "L0_ffn_bo", "L0_ffn_ln2_scale",
          "L0_ffn_ln2_shift", "L0_ffn_gate_w", "L0_ffn_w1", "L0_ffn_w2", "L0_ffn_w3", "L1_ffn_V1",
          "L1_ffn_U2", "L1_ffn_V2", "L1_ffn_b2")
_TURNED = ("L0_attn_w_qkv", "L0_attn_w_fc", "L1_attn_Wq", "L1_attn_Wk", "L1_attn_Wv", "L1_attn_Wr",
           "L1_ffn_U1")
_FLAT = ("L1_attn_u_bias", "L1_attn_v_bias")
_ORDER = ("L0_attn_x", "L0_attn_w_qkv", "L0_attn_w_fc", "L0_attn_b_fc", "L0_attn_gamma", "L0_attn_beta",
          "L0_ffn_ln1_scale", "L0_ffn_ln1_shift", "L0_ffn_wq", "L0_ffn_wk", "L0_ffn_wv", "L0_ffn_wo",
          "L0_ffn_bo", "L0_ffn_ln2_scale", "L0_ffn_ln2_shift", "L0_ffn_gate_w", "L0_ffn_w1", "L0_ffn_w2",
          "L0_ffn_w3", "L1_attn_Wq", "L1_attn_Wk", "L1_attn_Wv", "L1_attn_Wr", "L1_attn_u_bias",
          "L1_attn_v_bias", "L1_ffn_U1", "L1_ffn_V1", "L1_ffn_b1", "L1_ffn_U2", "L1_ffn_V2", "L1_ffn_b2",
          "ident", "mask", "maskT", "iota", "positions", "half")


def constants():
    import numpy as np

    i = np.arange(P)
    mask = np.where(i[None, :] > i[:, None], np.float32(BIG), np.float32(0))
    freq = (np.float32(1) / np.float32(10000) ** (np.arange(0, P, 2, dtype=np.float32) / np.float32(P)))
    angle = np.arange(-(L - 1), L, dtype=np.float32)[:, None] * freq.astype(np.float32)[None, :]
    r = np.zeros((2 * L - 1, P), np.float32)
    r[:, 0::2] = np.sin(angle)
    r[:, 1::2] = np.cos(angle)
    rows = np.zeros((2 * L, P), np.float32)
    rows[0:L] = r[L - 1:]
    rows[L + 1:] = r[:L - 1]
    upper = np.arange(L) % (2 * HW) >= HW
    half = np.where(np.arange(2 * SK)[:, None] >= SK, upper, ~upper).astype(np.float32)
    return {"ident": np.eye(P, dtype=np.float32), "mask": mask, "maskT": np.ascontiguousarray(mask.T),
            "iota": np.arange(NE, dtype=np.float32), "positions": np.ascontiguousarray(rows.T),
            "half": half}


def kernel(**inputs):
    import numpy as _np
    import concourse.bacc as _bacc
    from concourse import mybir as _mybir
    from concourse.bass_utils import run_bass_kernel_spmd as _run

    laid = dict(constants())
    for name in _PLAIN:
        laid[name] = _np.ascontiguousarray(inputs[name])
    for name in _TURNED:
        laid[name] = _np.ascontiguousarray(_np.asarray(inputs[name]).T)
    for name in _FLAT:
        laid[name] = _np.ascontiguousarray(inputs[name]).reshape(P)
    laid["L1_ffn_b1"] = _np.ascontiguousarray(_np.asarray(inputs["L1_ffn_b1"]).reshape(FF // P, P).T)

    nc = _bacc.Bacc("TRN2", target_bir_lowering=False, num_devices=1)
    arrays, args = {}, []
    for name in _ORDER:
        a = laid[name]
        arrays[f"in_{name}_dram"] = a
        args.append(nc.dram_tensor(f"in_{name}_dram", a.shape, _mybir.dt.from_np(a.dtype),
                                   kind="ExternalInput").ap())
    args.append(nc.dram_tensor("out_0_dram", (NB, L, P), F32, kind="ExternalOutput").ap())
    program(nc, *args)
    r = _run(nc, [arrays], core_ids=[0])
    return r.results[0]["out_0_dram"]
```
